# Optimizing a Trainium2 kernel written in Bass

```python
import numpy as np
import jax
import jax.numpy as jnp

def _softmax(x, axis=-1):
    return jax.nn.softmax(x, axis=axis)

def _gelu(x):
    return jax.nn.gelu(x, approximate=True)

def _silu(x):
    return jax.nn.silu(x)

def _sigmoid(x):
    return jax.nn.sigmoid(x)

def _layernorm(x, axis=-1, eps=1e-05):
    m = jnp.mean(x, axis=axis, keepdims=True)
    v = jnp.var(x, axis=axis, keepdims=True)
    return (x - m) / jnp.sqrt(v + eps)

def _scatter_add(tgt, idx, src, axis=0):
    return tgt.at[idx].add(src)

def _segment_sum(src, seg, n):
    return jax.ops.segment_sum(src, seg, n)
kernel_name = 'mk_vit_tower_d1_tok_img256_r4_a5154c'

def setup_inputs(seed: int=0):
    np.random.seed(seed)
    _w = jnp.asarray

    def _rec_inputs():
        import jax
        import jax.numpy as jnp
        _rk = jax.random.key(seed)
        x = 9.04603e-05 + 1.00016 * jax.random.normal(jax.random.fold_in(_rk, 1), (16, 1, 224, 224), jnp.float32)
        return x
    x = _rec_inputs()

    def _L0_tok_setup():
        import jax, jax.numpy as jnp
        import numpy as np
        WS = 7
        H = W = 56
        C = 64
        NH = 8
        HD = C // NH
        SCALE = HD ** (-0.5)
        SHIFT = WS // 2
        N = WS * WS

        def _rel_pos_index():
            coords = np.stack(np.meshgrid(np.arange(WS), np.arange(WS), indexing='ij'))
            cf = coords.reshape(2, -1)
            rel = (cf[:, :, None] - cf[:, None, :]).transpose(1, 2, 0).copy()
            rel[..., 0] += WS - 1
            rel[..., 1] += WS - 1
            rel[..., 0] *= 2 * WS - 1
            return jnp.array(rel.sum(-1))

        def _attn_mask():
            img = np.zeros((H, W), np.int32)
            cnt = 0
            for h in (slice(0, -WS), slice(-WS, -SHIFT), slice(-SHIFT, None)):
                for w in (slice(0, -WS), slice(-WS, -SHIFT), slice(-SHIFT, None)):
                    cnt += 1
                    img[h, w] = cnt
            mw = img.reshape(H // WS, WS, W // WS, WS).transpose(0, 2, 1, 3).reshape(-1, N)
            diff = mw[:, None, :] - mw[:, :, None]
            return jnp.array(np.where(diff != 0, -100.0, 0.0).astype(np.float32))

        def _layernorm(x, g, b):
            m = x.mean(-1, keepdims=True)
            v = ((x - m) ** 2).mean(-1, keepdims=True)
            return (x - m) * jax.lax.rsqrt(v + 1e-05) * g + b

        def _window_partition(x):
            B = x.shape[0]
            x = x.reshape(B, H // WS, WS, W // WS, WS, C).transpose(0, 1, 3, 2, 4, 5)
            return x.reshape(-1, N, C)

        def _window_reverse(xw, B):
            x = xw.reshape(B, H // WS, W // WS, WS, WS, C).transpose(0, 1, 3, 2, 4, 5)
            return x.reshape(B, H, W, C)

        def _swin_block(x, p, shift, rpi, amask):
            B = x.shape[0]
            shortcut = x
            h = _layernorm(x, p['n1g'], p['n1b']).reshape(B, H, W, C)
            if shift > 0:
                h = jnp.roll(h, (-shift, -shift), axis=(1, 2))
            xw = _window_partition(h)
            B_ = xw.shape[0]
            qkv = (xw @ p['qkv_w'].T + p['qkv_b']).reshape(B_, N, 3, NH, HD).transpose(2, 0, 3, 1, 4)
            q, k, v = (qkv[0], qkv[1], qkv[2])
            attn = jnp.einsum('bhnd,bhmd->bhnm', q * SCALE, k)
            attn = attn + p['rpb'][rpi].transpose(2, 0, 1)[None]
            if shift > 0:
                nW = amask.shape[0]
                attn = attn.reshape(B_ // nW, nW, NH, N, N) + amask[None, :, None]
                attn = attn.reshape(B_, NH, N, N)
            attn = jax.nn.softmax(attn, axis=-1)
            o = jnp.einsum('bhnm,bhmd->bhnd', attn, v).transpose(0, 2, 1, 3).reshape(B_, N, C)
            o = o @ p['proj_w'].T + p['proj_b']
            h = _window_reverse(o, B)
            if shift > 0:
                h = jnp.roll(h, (shift, shift), axis=(1, 2))
            x = shortcut + h.reshape(B, H * W, C)
            y = _layernorm(x, p['n2g'], p['n2b'])
            y = jax.nn.gelu(y @ p['w1'].T + p['b1'], approximate=False)
            return x + y @ p['w2'].T + p['b2']
        key = jax.random.key(seed)
        ks = jax.random.split(key, 8)
        s = 0.02
        return {'x': jax.random.normal(ks[0], (16, 1, 224, 224), jnp.float32), 'pe_w': jax.random.normal(ks[1], (C, 1, 4, 4), jnp.float32) * s, 'pe_b': jnp.zeros((C,), jnp.float32), 'pe_ng': jnp.ones((C,), jnp.float32), 'pe_nb': jnp.zeros((C,), jnp.float32), 'n1g': jnp.ones((2, C), jnp.float32), 'n1b': jnp.zeros((2, C), jnp.float32), 'qkv_w': jax.random.normal(ks[2], (2, 3 * C, C), jnp.float32) * s, 'qkv_b': jnp.zeros((2, 3 * C), jnp.float32), 'rpb': jax.random.normal(ks[3], (2, (2 * WS - 1) ** 2, NH), jnp.float32) * s, 'proj_w': jax.random.normal(ks[4], (2, C, C), jnp.float32) * s, 'proj_b': jnp.zeros((2, C), jnp.float32), 'n2g': jnp.ones((2, C), jnp.float32), 'n2b': jnp.zeros((2, C), jnp.float32), 'w1': jax.random.normal(ks[5], (2, 4 * C, C), jnp.float32) * s, 'b1': jnp.zeros((2, 4 * C), jnp.float32), 'w2': jax.random.normal(ks[6], (2, C, 4 * C), jnp.float32) * s, 'b2': jnp.zeros((2, C), jnp.float32)}
    _L0_tok_all = _L0_tok_setup()
    _L0_tok_in = {k: v for k, v in _L0_tok_all.items() if k in ('pe_w', 'pe_b', 'pe_ng', 'pe_nb', 'n1g', 'n1b', 'qkv_w', 'qkv_b', 'rpb', 'proj_w', 'proj_b', 'n2g', 'n2b', 'w1', 'b1', 'w2', 'b2')}
    del _L0_tok_all

    def _L0_attn_setup():
        import jax, jax.numpy as jnp
        import numpy as np
        MAX_ADAPTIVE_LR = 0.1

        def _l2n(z):
            n = jnp.linalg.norm(z, axis=-1, keepdims=True)
            return z / jnp.maximum(n, 1e-12)

        def _mlp(params, z):
            W0, W1, P0, P1 = params
            h = z @ W0 + z @ P0
            h = jax.nn.silu(h)
            return h @ W1 + h @ P1
        key = jax.random.key(seed)
        kx, kf, kp0, kp1 = jax.random.split(key, 4)
        B, T, H, E = (4, 64, 64, 4)
        D = H * E
        x = jax.random.normal(kx, (B, T, H), dtype=jnp.float32)
        W_fused = jax.random.normal(kf, (3 * H + 3, H), dtype=jnp.float32) / np.sqrt(H).astype(np.float32)
        W0 = jnp.zeros((H, D), dtype=jnp.float32)
        W1 = jnp.zeros((D, H), dtype=jnp.float32)
        P0 = jax.random.normal(kp0, (H, D), dtype=jnp.float32)
        P1 = jax.random.normal(kp1, (D, H), dtype=jnp.float32)
        return {'x': x, 'W_fused': W_fused, 'W0': W0, 'W1': W1, 'P0': P0, 'P1': P1}
    _L0_attn_all = _L0_attn_setup()
    _L0_attn_in = {k: v for k, v in _L0_attn_all.items() if k in ('W_fused', 'W0', 'W1', 'P0', 'P1')}
    del _L0_attn_all

    def _L0_ffn_setup():
        import math
        import jax, jax.numpy as jnp
        import numpy as np
        CAPACITY_FACTOR = 1.25
        key = jax.random.key(seed)
        ks = jax.random.split(key, 5)
        B, L, D, F, E = (8, 2048, 64, 256, 8)
        h = jax.random.normal(ks[0], (B, L, D), dtype=jnp.float32)
        gate_w = jax.random.normal(ks[1], (D, E), dtype=jnp.float32) * 0.02
        gate_b = jnp.zeros((E,), dtype=jnp.float32)
        w1 = jax.random.normal(ks[2], (E, D, F), dtype=jnp.float32) * (1.0 / math.sqrt(D))
        b1 = jnp.zeros((E, F), dtype=jnp.float32)
        w2 = jax.random.normal(ks[3], (E, F, D), dtype=jnp.float32) * (1.0 / math.sqrt(F))
        b2 = jnp.zeros((E, D), dtype=jnp.float32)
        return {'h': h, 'gate_w': gate_w, 'gate_b': gate_b, 'w1': w1, 'b1': b1, 'w2': w2, 'b2': b2}
    _L0_ffn_all = _L0_ffn_setup()
    _L0_ffn_in = {k: v for k, v in _L0_ffn_all.items() if k in ('gate_w', 'gate_b', 'w1', 'b1', 'w2', 'b2')}
    del _L0_ffn_all
    return {'x': x, 'L0_tok_pe_w': _L0_tok_in['pe_w'], 'L0_tok_pe_b': _L0_tok_in['pe_b'], 'L0_tok_pe_ng': _L0_tok_in['pe_ng'], 'L0_tok_pe_nb': _L0_tok_in['pe_nb'], 'L0_tok_n1g': _L0_tok_in['n1g'], 'L0_tok_n1b': _L0_tok_in['n1b'], 'L0_tok_qkv_w': _L0_tok_in['qkv_w'], 'L0_tok_qkv_b': _L0_tok_in['qkv_b'], 'L0_tok_rpb': _L0_tok_in['rpb'], 'L0_tok_proj_w': _L0_tok_in['proj_w'], 'L0_tok_proj_b': _L0_tok_in['proj_b'], 'L0_tok_n2g': _L0_tok_in['n2g'], 'L0_tok_n2b': _L0_tok_in['n2b'], 'L0_tok_w1': _L0_tok_in['w1'], 'L0_tok_b1': _L0_tok_in['b1'], 'L0_tok_w2': _L0_tok_in['w2'], 'L0_tok_b2': _L0_tok_in['b2'], 'L0_attn_W_fused': _L0_attn_in['W_fused'], 'L0_attn_W0': _L0_attn_in['W0'], 'L0_attn_W1': _L0_attn_in['W1'], 'L0_attn_P0': _L0_attn_in['P0'], 'L0_attn_P1': _L0_attn_in['P1'], 'L0_ffn_gate_w': _L0_ffn_in['gate_w'], 'L0_ffn_gate_b': _L0_ffn_in['gate_b'], 'L0_ffn_w1': _L0_ffn_in['w1'], 'L0_ffn_b1': _L0_ffn_in['b1'], 'L0_ffn_w2': _L0_ffn_in['w2'], 'L0_ffn_b2': _L0_ffn_in['b2']}

def reference(x, L0_tok_pe_w, L0_tok_pe_b, L0_tok_pe_ng, L0_tok_pe_nb, L0_tok_n1g, L0_tok_n1b, L0_tok_qkv_w, L0_tok_qkv_b, L0_tok_rpb, L0_tok_proj_w, L0_tok_proj_b, L0_tok_n2g, L0_tok_n2b, L0_tok_w1, L0_tok_b1, L0_tok_w2, L0_tok_b2, L0_attn_W_fused, L0_attn_W0, L0_attn_W1, L0_attn_P0, L0_attn_P1, L0_ffn_gate_w, L0_ffn_gate_b, L0_ffn_w1, L0_ffn_b1, L0_ffn_w2, L0_ffn_b2):
    import jax
    import jax.numpy as jnp

    def _L0_tok_ref(x, pe_w, pe_b, pe_ng, pe_nb, n1g, n1b, qkv_w, qkv_b, rpb, proj_w, proj_b, n2g, n2b, w1, b1, w2, b2):
        import jax, jax.numpy as jnp
        import numpy as np
        WS = 7
        H = W = 56
        C = 64
        NH = 8
        HD = C // NH
        SCALE = HD ** (-0.5)
        SHIFT = WS // 2
        N = WS * WS

        def _rel_pos_index():
            coords = np.stack(np.meshgrid(np.arange(WS), np.arange(WS), indexing='ij'))
            cf = coords.reshape(2, -1)
            rel = (cf[:, :, None] - cf[:, None, :]).transpose(1, 2, 0).copy()
            rel[..., 0] += WS - 1
            rel[..., 1] += WS - 1
            rel[..., 0] *= 2 * WS - 1
            return jnp.array(rel.sum(-1))

        def _attn_mask():
            img = np.zeros((H, W), np.int32)
            cnt = 0
            for h in (slice(0, -WS), slice(-WS, -SHIFT), slice(-SHIFT, None)):
                for w in (slice(0, -WS), slice(-WS, -SHIFT), slice(-SHIFT, None)):
                    cnt += 1
                    img[h, w] = cnt
            mw = img.reshape(H // WS, WS, W // WS, WS).transpose(0, 2, 1, 3).reshape(-1, N)
            diff = mw[:, None, :] - mw[:, :, None]
            return jnp.array(np.where(diff != 0, -100.0, 0.0).astype(np.float32))

        def _layernorm(x, g, b):
            m = x.mean(-1, keepdims=True)
            v = ((x - m) ** 2).mean(-1, keepdims=True)
            return (x - m) * jax.lax.rsqrt(v + 1e-05) * g + b

        def _window_partition(x):
            B = x.shape[0]
            x = x.reshape(B, H // WS, WS, W // WS, WS, C).transpose(0, 1, 3, 2, 4, 5)
            return x.reshape(-1, N, C)

        def _window_reverse(xw, B):
            x = xw.reshape(B, H // WS, W // WS, WS, WS, C).transpose(0, 1, 3, 2, 4, 5)
            return x.reshape(B, H, W, C)

        def _swin_block(x, p, shift, rpi, amask):
            B = x.shape[0]
            shortcut = x
            h = _layernorm(x, p['n1g'], p['n1b']).reshape(B, H, W, C)
            if shift > 0:
                h = jnp.roll(h, (-shift, -shift), axis=(1, 2))
            xw = _window_partition(h)
            B_ = xw.shape[0]
            qkv = (xw @ p['qkv_w'].T + p['qkv_b']).reshape(B_, N, 3, NH, HD).transpose(2, 0, 3, 1, 4)
            q, k, v = (qkv[0], qkv[1], qkv[2])
            attn = jnp.einsum('bhnd,bhmd->bhnm', q * SCALE, k)
            attn = attn + p['rpb'][rpi].transpose(2, 0, 1)[None]
            if shift > 0:
                nW = amask.shape[0]
                attn = attn.reshape(B_ // nW, nW, NH, N, N) + amask[None, :, None]
                attn = attn.reshape(B_, NH, N, N)
            attn = jax.nn.softmax(attn, axis=-1)
            o = jnp.einsum('bhnm,bhmd->bhnd', attn, v).transpose(0, 2, 1, 3).reshape(B_, N, C)
            o = o @ p['proj_w'].T + p['proj_b']
            h = _window_reverse(o, B)
            if shift > 0:
                h = jnp.roll(h, (shift, shift), axis=(1, 2))
            x = shortcut + h.reshape(B, H * W, C)
            y = _layernorm(x, p['n2g'], p['n2b'])
            y = jax.nn.gelu(y @ p['w1'].T + p['b1'], approximate=False)
            return x + y @ p['w2'].T + p['b2']
        B = x.shape[0]
        h = jax.lax.conv_general_dilated(x, pe_w, (4, 4), 'VALID', dimension_numbers=('NCHW', 'OIHW', 'NCHW'))
        h = h + pe_b[None, :, None, None]
        t = h.reshape(B, C, H * W).transpose(0, 2, 1)
        t = _layernorm(t, pe_ng, pe_nb)
        rpi = _rel_pos_index()
        amask = _attn_mask()
        for i, shift in enumerate((0, SHIFT)):
            p = {'n1g': n1g[i], 'n1b': n1b[i], 'qkv_w': qkv_w[i], 'qkv_b': qkv_b[i], 'rpb': rpb[i], 'proj_w': proj_w[i], 'proj_b': proj_b[i], 'n2g': n2g[i], 'n2b': n2b[i], 'w1': w1[i], 'b1': b1[i], 'w2': w2[i], 'b2': b2[i]}
            t = _swin_block(t, p, shift, rpi, amask)
        return t

    def _L0_attn_ref(x, W_fused, W0, W1, P0, P1):
        import jax, jax.numpy as jnp
        import numpy as np
        MAX_ADAPTIVE_LR = 0.1

        def _l2n(z):
            n = jnp.linalg.norm(z, axis=-1, keepdims=True)
            return z / jnp.maximum(n, 1e-12)

        def _mlp(params, z):
            W0, W1, P0, P1 = params
            h = z @ W0 + z @ P0
            h = jax.nn.silu(h)
            return h @ W1 + h @ P1
        B, T, H = x.shape
        fp = x @ W_fused.T
        q, k, v, alpha, theta, eta = jnp.split(fp, [H, 2 * H, 3 * H, 3 * H + 1, 3 * H + 2], axis=-1)
        q = _l2n(jax.nn.silu(q))
        k = _l2n(jax.nn.silu(k))
        v = jax.nn.silu(v)
        alpha = jax.nn.sigmoid(alpha)
        theta = jax.nn.sigmoid(theta) * MAX_ADAPTIVE_LR
        eta = jax.nn.sigmoid(eta)
        params0 = (W0, W1, P0, P1)
        bat = lambda p: jnp.broadcast_to(p[None], (B,) + p.shape)
        cur_p = jax.tree_util.tree_map(bat, params0)
        cur_m = jax.tree_util.tree_map(jnp.zeros_like, cur_p)

        def loss_fn(params, kk, vv):
            pred = _mlp(params, kk)
            return jnp.mean((pred - vv) ** 2)

        def step(carry, xs):
            cp, cm = carry
            k_t, v_t, q_t, a_t, th_t, e_t = xs
            g = jax.vmap(jax.grad(loss_fn))(cp, k_t, v_t)
            s = lambda c: c[:, :, None]
            nm = jax.tree_util.tree_map(lambda m, gg: m * s(e_t) - s(th_t) * gg, cm, g)
            np_ = jax.tree_util.tree_map(lambda p, m: p * (1.0 - s(a_t)) + m, cp, nm)
            out_t = jax.vmap(_mlp, in_axes=(0, 0))(np_, q_t)
            new_carry = jax.lax.stop_gradient((np_, nm))
            return (new_carry, out_t)
        tT = lambda a: jnp.swapaxes(a, 0, 1)
        xs = tuple(map(tT, (k, v, q, alpha, theta, eta)))
        _, ys = jax.lax.scan(step, (cur_p, cur_m), xs)
        return jnp.swapaxes(ys, 0, 1)

    def _L0_ffn_ref(h, gate_w, gate_b, w1, b1, w2, b2):
        import math
        import jax, jax.numpy as jnp
        import numpy as np
        CAPACITY_FACTOR = 1.25
        B, L, D = h.shape
        E = gate_w.shape[1]
        T = B * L
        C = max(1, math.ceil(CAPACITY_FACTOR * T / E))
        x = h.reshape(T, D)
        logits = x @ gate_w + gate_b
        probs = jax.nn.softmax(logits, axis=-1)
        idx = jnp.argmax(probs, axis=-1)
        prb = jnp.take_along_axis(probs, idx[:, None], axis=1)[:, 0]
        one_hot = jax.nn.one_hot(idx, E, dtype=jnp.float32)
        pos = (jnp.cumsum(one_hot, axis=0) * one_hot).sum(-1).astype(jnp.int32) - 1
        kept = pos < C
        pos_safe = jnp.where(kept, pos, C)
        buf = jnp.zeros((E, C, D), dtype=h.dtype).at[idx, pos_safe].set(x, mode='drop')
        hmid = jax.nn.relu(jnp.einsum('ecd,edf->ecf', buf, w1) + b1[:, None, :])
        ybuf = jnp.einsum('ecf,efd->ecd', hmid, w2) + b2[:, None, :]
        pos_g = jnp.minimum(pos, C - 1)
        y_tok = ybuf[idx, pos_g] * (prb * kept)[:, None]
        y = y_tok.reshape(B, L, D)
        y = jnp.nan_to_num(y, nan=0.0, posinf=10000.0, neginf=-10000.0)
        return y
    h = _L0_tok_ref(x, L0_tok_pe_w, L0_tok_pe_b, L0_tok_pe_ng, L0_tok_pe_nb, L0_tok_n1g, L0_tok_n1b, L0_tok_qkv_w, L0_tok_qkv_b, L0_tok_rpb, L0_tok_proj_w, L0_tok_proj_b, L0_tok_n2g, L0_tok_n2b, L0_tok_w1, L0_tok_b1, L0_tok_w2, L0_tok_b2)
    h = h + _L0_attn_ref(_layernorm(h, axis=-1), L0_attn_W_fused, L0_attn_W0, L0_attn_W1, L0_attn_P0, L0_attn_P1)
    h = h + _L0_ffn_ref(_layernorm(h, axis=-1), L0_ffn_gate_w, L0_ffn_gate_b, L0_ffn_w1, L0_ffn_b1, L0_ffn_w2, L0_ffn_b2)
    return h

_drawn_inputs = setup_inputs


def setup_inputs(seed=0):
    import zlib

    import numpy as np

    out = dict(_drawn_inputs(seed))
    spreads = {'L0_tok_pe_b': (0.0, 0.1),
     'L0_tok_pe_ng': (1.0, 0.2),
     'L0_tok_pe_nb': (0.0, 0.1),
     'L0_tok_n1g': (1.0, 0.6),
     'L0_tok_n1b': (0.0, 0.8),
     'L0_tok_qkv_b': (0.0, 0.433),
     'L0_tok_proj_b': (0.0, 0.1),
     'L0_tok_n2g': (1.0, 0.6),
     'L0_tok_n2b': (0.0, 2.0),
     'L0_tok_b1': (0.0, 0.391),
     'L0_tok_b2': (0.0, 0.1),
     'L0_attn_W0': (0.0, 0.8),
     'L0_attn_W1': (0.0, 0.8),
     'L0_ffn_gate_b': (0.0, 0.1),
     'L0_ffn_b1': (0.0, 0.8),
     'L0_ffn_b2': (0.0, 0.8)}
    factors = {'L0_tok_rpb': 200.0}
    for name, (base, spread) in spreads.items():
        noise = np.random.default_rng([zlib.crc32(name.encode()), seed]).standard_normal(out[name].shape)
        drawn = base * np.exp(spread * noise) if base else spread * noise
        out[name] = jnp.asarray(drawn.astype(out[name].dtype))
    for name, factor in factors.items():
        out[name] = (out[name] * factor).astype(out[name].dtype)
    return out
```

```python
from contextlib import ExitStack

import concourse.bass as bass
from concourse import mybir

F32 = mybir.dt.float32
I32 = mybir.dt.int32
ALU = mybir.AluOpType
ACT = mybir.ActivationFunctionType
AX = mybir.AxisListType

B = 16
C = 64
WS = 7
NW = 8
N = WS * WS
SIDE = NW * WS
NH = 8
HD = C // NH
SHIFT = WS // 2
KEEP = WS - SHIFT
PAIRS = NW // 2
HALF = 64
P = 128
GROUPS = B * NW
UNCUT = B * (NW - 1)
KEYS = NH * N
HV = HD + 1
F = 4 * C
EPS = 1e-5
PIX = 16

T = SIDE * SIDE
CH = 16
CHUNKS = T // CH
QKV3 = 3 * C + 3
FS = P // B
FI = F // FS
LR = 0.1
L2_LIMIT = 1e12
TOKENS = B * T
TILES = 4
SIZE = TILES * P
SETS = TOKENS // SIZE
E = 8
CAPACITY = -(-5 * TOKENS // (4 * E))
K1 = C + E + 1
OFF = -1e18
HUGE = 3.4028234663852886e38
CLIP = 1e4

class Steps:

    def __init__(self, sem, per):
        self.sem, self.per, self.base, self.n = sem, per, 0, 0

    def start(self, group):
        self.base, self.n = group * self.per, 0

    def did(self, instruction):
        instruction.then_inc(self.sem, 1)
        self.n += 1

    def wait(self, engine):
        engine.wait_ge(self.sem, self.base + self.n)

    def end(self):
        assert self.n == self.per, (self.n, self.per)


class Group:

    def __init__(self, half, odd):
        self.half, self.odd, self.g = half, odd, half * 2 + odd

    def next(self):
        return Group(self.half, 1) if not self.odd else Group(self.half + 1, 0)

    def prev(self):
        return Group(self.half, 0) if self.odd else Group(self.half - 1, 1)


def after(engine, sem, value):
    if not isinstance(value, int) or value > 0:
        engine.wait_ge(sem, value)


def settle(engine):
    engine.nop(nofuse=True)


def ones_row(ap):
    return ap[C:C + 1]


def tokens(ap, half):
    return ap.rearrange("(p w) t c -> w t p c", w=2)[half]


def swin_block(nc, k, V, src, dst):
    with ExitStack() as ctx:
        def sb(name, shape, dt=F32):
            return ctx.enter_context(nc.sbuf_tensor(f"{name}_{k}", shape, dt))

        def sem(name):
            return ctx.enter_context(nc.semaphore(f"{name}_{k}"))

        banks = [ctx.enter_context(nc.psum_tensor(f"bank{i}_{k}", [P, 512], F32)) for i in range(8)]
        ps_a, ps_pt1, ps_c, ps_d, ps_s0, ps_s1, ps_pt0, ps_o = banks
        ps_s, ps_pt = [ps_s0, ps_s1], [ps_pt0, ps_pt1]

        w_qkv = sb("w_qkv", [P, 3 * C])
        w_proj = sb("w_proj", [P, C])
        w_up = sb("w_up", [P, F])
        w_down = sb("w_down", [P, 2, C])
        b_down = sb("b_down", [1, C])
        ones1 = sb("ones1", [1, P])
        norm_g = sb("norm_g", [C, 2])
        norm_b = sb("norm_b", [C, 2])
        folded = sb("folded", [1, 3 * C + F])
        bias_in = sb("bias_in", [1, 3 * C + F])
        ident = sb("ident", [P, P])
        neghalf = sb("neghalf", [P, PAIRS])
        head_mask = sb("head_mask", [C, NH])
        masks = sb("masks", [HALF + N, 3, N])
        w_pe = sb("w_pe", [PIX + 1, C])
        pe_gain = sb("pe_gain", [P, C])
        pe_shift = sb("pe_shift", [P, C])
        patches = sb("patches", [PIX + 1, 2, NW, HALF]) if k == 0 else None
        xa = sb("xa", [P, 2, PAIRS, C])
        xr = sb("xr", [P, 2, PAIRS, C])
        xt = sb("xt", [P, 512])
        kt = sb("kt", [C, 512])
        q_rows = sb("q_rows", [P, 2, NW, HALF])
        k_rows = sb("k_rows", [P, 2, NW, NH, N])
        v_blk = sb("v_blk", [P, 2, NW, NH // 2, 2 * HV])
        probs = sb("probs", [P, 2, NH, HALF])
        probs_t = sb("probs_t", [P, 2, NH // 2, P])
        row_max = sb("row_max", [P, 2, NH])
        rec = sb("rec", [P, PAIRS * NH])
        oa = sb("oa", [P, PAIRS, C])
        ot = sb("ot", [P, 512])
        x1 = sb("x1", [P, PAIRS, C])
        xt2 = sb("xt2", [P, 512])
        hid = sb("hid", [P, 2, 512])
        xo = sb("xo", [P, 2, PAIRS, C])
        norms = {}
        for name in ("pe", "ln1", "ln2"):
            norms[name] = dict(
                xc=sb(f"{name}_xc", [P, PAIRS, C]), sq=sb(f"{name}_sq", [P, PAIRS, C]),
                xn=sb(f"{name}_xn", [P, PAIRS, C]), s=sb(f"{name}_s", [P, PAIRS]),
                m=sb(f"{name}_m", [P, PAIRS]), ss=sb(f"{name}_ss", [P, PAIRS]),
                var=sb(f"{name}_var", [P, PAIRS]), rstd=sb(f"{name}_rstd", [P, PAIRS]),
                chain=Steps(sem(f"{name}_chain"), 9 if name == "pe" else 7), rstd_ready=sem(f"{name}_rstd"))

        loaded, zeroed = sem("loaded"), sem("zeroed")
        prep = sem("prep")
        prep_pe = sem("prep_pe")
        prep_act = sem("prep_act")
        row_moved = sem("row_moved")
        x_in = [sem("x_in0"), sem("x_in1")]
        xp_psum = sem("xp_psum")
        xr_ready, xt_psum, xt_ready = sem("xr_ready"), sem("xt_psum"), sem("xt_ready")
        qk_psum, qk_ready, v_psum = sem("qk_psum"), sem("qk_ready"), sem("v_psum")
        v_ready, k_ready = sem("v_ready"), sem("k_ready")
        s_psum, max_ready, shifted, exp_ready = sem("s_psum"), sem("max_ready"), sem("shifted"), sem("exp_ready")
        p_psum, pt_ready, pv_done = sem("p_psum"), sem("pt_ready"), sem("pv_done")
        rec_ready, oa_ready, ot_psum, ot_ready = sem("rec_ready"), sem("oa_ready"), sem("ot_psum"), sem("ot_ready")
        proj_psum, x1_ready, t2_psum, xt2_ready = sem("proj_psum"), sem("x1_ready"), sem("t2_psum"), sem("xt2_ready")
        h_psum, h_ready, y_psum, out_ready = sem("h_psum"), sem("h_ready"), sem("y_psum"), sem("out_ready")
        stored = [sem("stored0"), sem("stored1")]
        bias_set = sem("bias_set")

        pe_fold = sem("pe_fold")
        bias_step = sem("bias_step")

        def fill_bias(dve, last_row):
            first = k_rows[HALF:HALF + N, 0, 0, :, :]
            n = 0
            for u in range(2):
                for w in range(NW):
                    kind = (2 if last_row else 0) + (1 if w == NW - 1 else 0)
                    if (u, w) == (0, 0):
                        continue
                    out = k_rows[HALF:HALF + N, u, w, :, :]
                    if k == 0 or kind == 0:
                        nc.vector.tensor_copy(out, first).then_inc(bias_step, 1)
                    else:
                        m = masks[HALF:HALF + N, kind - 1, :].unsqueeze(1).broadcast_to([N, NH, N])
                        nc.vector.tensor_tensor(out, first, m, ALU.add).then_inc(bias_step, 1)
                    n += 1
            if last_row:
                dve.wait_ge(bias_step, 2 * n)
                m = masks[HALF:HALF + N, 1, :].unsqueeze(1).broadcast_to([N, NH, N])
                nc.vector.tensor_tensor(first, first, m, ALU.add).then_inc(bias_step, 1)

        with nc.Block() as block:
            n_loads = 12 if k else 15

            @block.sync
            def _(sp):
                def load(out, in_):
                    sp.dma_start(out, in_).then_inc(loaded, 16)
                sp.wait_ge(zeroed, 3)
                load(w_qkv[0:C, :], V["qkv_t"][k])
                load(w_proj[0:C, :], V["proj_t"][k])
                load(w_proj[C:C + 1, :], V["proj_b"][k:k + 1, :])
                load(w_up[0:C, :], V["w1_t"][k])
                load(w_down[:, :, :], V["w2_t"][k].rearrange("(f p) c -> p f c", p=P))
                load(b_down[:, :], V["b2"][k:k + 1, :])
                load(bias_in[:, 0:3 * C], V["qkv_b"][k:k + 1, :])
                load(bias_in[:, 3 * C:], V["b1"][k:k + 1, :])
                with nc.allow_non_contiguous_dma(reason="a column of 64"):
                    load(norm_g[:, 0:1], V["n1g"][k:k + 1, :].rearrange("a c -> c a"))
                    load(norm_g[:, 1:2], V["n2g"][k:k + 1, :].rearrange("a c -> c a"))
                    load(norm_b[:, 0:1], V["n1b"][k:k + 1, :].rearrange("a c -> c a"))
                    load(norm_b[:, 1:2], V["n2b"][k:k + 1, :].rearrange("a c -> c a"))
                if k == 0:
                    load(w_pe[0:PIX, :], V["pe_t"][:, :])
                    load(w_pe[PIX:PIX + 1, :], V["pe_b"].rearrange("(a c) -> a c", a=1))
                    load(pe_gain[:, :], V["pe_ng"].rearrange("(a c) -> a c", a=1).broadcast_to([P, C]))
                    sp.dma_start(pe_shift[:, :], V["pe_nb"].rearrange("(a c) -> a c", a=1).broadcast_to([P, C])).then_inc(loaded, 16)
                sp.wait_ge(prep_act, 1)
                for w in range(1):
                    for rq in range(WS):
                        for h in range(NH):
                            base = V["rpb_t"][k, h, :]
                            row0 = HALF + rq * WS
                            src_ap = bass.AP(tensor=base.tensor, offset=base.offset + 13 * rq,
                                             ap=[[1, WS], [13, WS], [1, WS]])
                            sp.dma_start(k_rows[row0:row0 + WS, 0, 0, h, :].rearrange("p (a b) -> p a b", a=WS),
                                         src_ap).then_inc(bias_set, 16)
                if k == 1:
                    sp.dma_start(masks[HALF:HALF + N, :, :], V["masks"].rearrange("m q k -> q m k")).then_inc(bias_set, 16)
                sp.wait_ge(prep, 8)
                sp.dma_start(ones_row(w_qkv), folded[:, 0:3 * C]).then_inc(row_moved, 16)
                sp.dma_start(ones_row(w_up), folded[:, 3 * C:]).then_inc(row_moved, 16)

            @block.gpsimd
            def _(pool):
                nc.gpsimd.memset(ident[:, :], 0.0).then_inc(prep_pe, 1)
                nc.gpsimd.memset(q_rows[:, :, :, :], 0.0).then_inc(prep_pe, 1)
                nc.gpsimd.memset(neghalf[:, :], -0.5).then_inc(prep_pe, 1)
                nc.gpsimd.memset(head_mask[:, :], 1.0).then_inc(prep_pe, 1)
                pool.wait_ge(prep_pe, 4)
                nc.gpsimd.affine_select(out=ident[:, :], in_=ident[:, :], compare_op=ALU.not_equal, fill=1.0,
                                        base=0, pattern=[[-1, P]], channel_multiplier=1).then_inc(prep_pe, 1)
                nc.gpsimd.affine_select(out=head_mask[:, :], in_=head_mask[:, :], compare_op=ALU.is_ge, fill=0.0,
                                        base=0, pattern=[[-HD, NH]], channel_multiplier=1).then_inc(prep_pe, 1)
                pool.wait_ge(prep_pe, 6)
                nc.gpsimd.affine_select(out=head_mask[:, :], in_=head_mask[:, :], compare_op=ALU.is_ge, fill=0.0,
                                        base=HD - 1, pattern=[[HD, NH]], channel_multiplier=-1).then_inc(prep_pe, 1)
                q2 = q_rows[HALF:P, :, :, :].rearrange("p u w q -> p (u w) q")
                nc.gpsimd.affine_select(out=q2, in_=q2, compare_op=ALU.not_equal, fill=1.0, base=-(N - 1),
                                        pattern=[[0, 2 * NW], [1, HALF]], channel_multiplier=1).then_inc(prep_pe, 1)

            @block.vector
            def _(dve):
                for t in (w_qkv, w_proj, w_up):
                    nc.vector.memset(t[:, :], 0.0).then_inc(zeroed, 1)
                nc.vector.memset(ones1[:, :], 1.0)
                nc.vector.memset(k_rows[:, :, :, :, :], 0.0).then_inc(prep_act, 1)
                nc.vector.memset(v_blk[0:HALF, :, :, :, :], 0.0).then_inc(prep, 1)
                nc.vector.memset(v_blk[HALF:P, :, :, :, :], 0.0).then_inc(prep, 1)
                nc.vector.memset(probs[:, :, :, :], 0.0)
                nc.vector.memset(xa[:, :, :, :], 0.0)
                for t in (xt, ot, xt2):
                    nc.vector.memset(t[C:P, :], 1.0)
                if k == 0:
                    nc.vector.memset(patches[:, :, :, :], 0.0).then_inc(prep, 1)
                    dve.wait_ge(prep, 3)
                    nc.vector.memset(patches[:, :, :, :], 1.0).then_inc(prep, 1)
                    dve.wait_ge(prep, 4)
                    nc.vector.memset(patches[0:PIX, :, :, :], 0.0)
                else:
                    nc.vector.memset(masks[0:HALF, :, :], 0.0).then_inc(prep, 1)
                    nc.vector.memset(rec[:, :], 0.0).then_inc(prep, 1)
                dve.wait_ge(prep, 4)
                nc.vector.memset(v_blk[0:HALF, :, :, :, HD:HD + 1], 1.0)
                nc.vector.memset(v_blk[HALF:P, :, :, :, HV + HD:HV + HD + 1], 1.0)
                dve.wait_ge(loaded, 16 * (16 if k == 0 else 12))
                dve.wait_ge(pe_fold, 1)
                nc.vector.tensor_tensor(folded[:, 0:3 * C], ps_a[0:1, 0:3 * C], bias_in[:, 0:3 * C], ALU.add).then_inc(prep, 1)
                nc.vector.tensor_tensor(folded[:, 3 * C:], ps_c[0:1, 0:F], bias_in[:, 3 * C:], ALU.add).then_inc(prep, 1)
                nc.vector.tensor_scalar(w_qkv[0:C, :], w_qkv[0:C, :], norm_g[:, 0:1], None, ALU.mult).then_inc(prep, 1)
                nc.vector.tensor_scalar(w_up[0:C, :], w_up[0:C, :], norm_g[:, 1:2], None, ALU.mult).then_inc(prep, 1)
                dve.wait_ge(prep, 8)
                dve.wait_ge(row_moved, 32)
                nc.vector.tensor_scalar(w_qkv[:, 0:C], w_qkv[:, 0:C], float(HD) ** -0.5, None, ALU.mult)
                dve.wait_ge(bias_set, 16 * (WS * NH + (k == 1)))
                fill_bias(dve, last_row=False)

            @block.tensor
            def _(pe):
                pe.wait_ge(loaded, 16 * (16 if k == 0 else 12))
                nc.tensor.matmul(ps_a[0:1, 0:3 * C], norm_b[:, 0:1], w_qkv[0:C, :], start=True, stop=True)
                nc.tensor.matmul(ps_c[0:1, 0:F], norm_b[:, 1:2], w_up[0:C, :], start=True, stop=True).then_inc(pe_fold, 1)

        def norm(eng, name, group, x, affine=False, x_wait=None):
            T, g = norms[name], group.g
            c = T["chain"]
            c.start(g)
            c.did(nc.vector.tensor_reduce(T["s"][:, :], x, AX.X, ALU.add))
            c.wait(eng)
            c.did(nc.vector.tensor_scalar(T["m"][:, :], T["s"][:, :], 1.0 / C, None, ALU.mult))
            c.wait(eng)
            c.did(nc.vector.tensor_tensor(T["xc"][:, :, :], x, T["m"][:, :].unsqueeze(2).broadcast_to([P, PAIRS, C]), ALU.subtract))
            c.wait(eng)
            c.did(nc.vector.tensor_tensor(T["sq"][:, :, :], T["xc"][:, :, :], T["xc"][:, :, :], ALU.mult))
            c.wait(eng)
            c.did(nc.vector.tensor_reduce(T["ss"][:, :], T["sq"][:, :, :], AX.X, ALU.add))
            c.wait(eng)
            c.did(nc.vector.tensor_scalar(T["var"][:, :], T["ss"][:, :], 1.0 / C, EPS, ALU.mult, ALU.add))
            eng.wait_ge(T["rstd_ready"], g + 1)
            out = T["xn"][:, :, :]
            c.did(nc.vector.tensor_tensor(out, T["xc"][:, :, :], T["rstd"][:, :].unsqueeze(2).broadcast_to([P, PAIRS, C]), ALU.mult))
            if affine:
                c.wait(eng)
                c.did(nc.vector.tensor_tensor(out, out, pe_gain[:, :].unsqueeze(1).broadcast_to([P, PAIRS, C]), ALU.mult))
                c.wait(eng)
                c.did(nc.vector.tensor_tensor(xa[:, group.odd, :, :], out, pe_shift[:, :].unsqueeze(1).broadcast_to([P, PAIRS, C]), ALU.add))
            c.end()

        def rsqrt(eng, name, g):
            T = norms[name]
            eng.wait_ge(T["chain"].sem, g * T["chain"].per + 6)
            nc.gpsimd.tensor_tensor(T["rstd"][:, :], T["var"][:, :], neghalf[:, :], ALU.pow).then_inc(T["rstd_ready"], 1)

        PE_N, LN_N = norms["pe"]["chain"].per, 7

        def x_present(eng, group):
            if k == 0:
                eng.wait_ge(norms["pe"]["chain"].sem, group.g * PE_N + PE_N)
            else:
                eng.wait_ge(x_in[group.odd], group.half * 32 + 32)

        def sync_load(sp, group):
            g, u = group.g, group.odd
            if k == 0:
                after(sp, xp_psum, g - 1)
                sp.dma_start(patches[0:PIX, u, :, 0:N],
                             src[:, bass.ds(g, 1), :, :].rearrange("x g w t -> x (g w) t")).then_inc(x_in[u], 16)
            else:
                after(sp, norms["ln1"]["chain"].sem, (g - 2) * LN_N + LN_N)
                settle(sp)
                after(sp, xr_ready, g - 1)
                for half in range(2):
                    sp.dma_start(xa[HALF * half:HALF * half + N, u, :, :],
                                 tokens(src[bass.ds(g, 1)].rearrange("g w t c -> (g w) t c"), half)).then_inc(x_in[u], 16)

        def sync_store(sp, group):
            g, u = group.g, group.odd
            sp.wait_ge(out_ready, g + 1)
            for half in range(2):
                sp.dma_start(tokens(dst[bass.ds(g, 1)].rearrange("g w t c -> (g w) t c"), half),
                             xo[HALF * half:HALF * half + N, u, :, :]).then_inc(stored[u], 16)

        def pe_patch(pe, group):
            g, u = group.g, group.odd
            pe.wait_ge(x_in[u], group.half * 16 + 16)
            after(pe, v_ready, g)
            for p in range(PAIRS):
                i = nc.tensor.matmul(ps_a[:, p * C:(p + 1) * C], patches[:, u, 2 * p:2 * p + 2, :], w_pe[:, :],
                                     start=True, stop=True)
            i.then_inc(xp_psum, 1)

        def pe_transpose(pe, out, x):
            settle(pe)
            for p in range(PAIRS):
                i = nc.tensor.transpose(out[0:C, p * P:(p + 1) * P], x[:, p, :], ident[:, :])
            return i

        def pe_xt(pe, group):
            g = group.g
            pe.wait_ge(norms["ln1"]["chain"].sem, g * LN_N + LN_N)
            after(pe, v_ready, g)
            pe_transpose(pe, ps_a, norms["ln1"]["xn"]).then_inc(xt_psum, 1)

        def pe_qk(pe, group):
            pe.wait_ge(xt_ready, group.g + 1)
            nc.tensor.matmul(ps_a[:, :], w_qkv[:, 0:2 * C], xt[:, :], start=True, stop=True).then_inc(qk_psum, 1)

        def pe_v(pe, group):
            pe.wait_ge(qk_ready, group.g * 2 + 2)
            for p in range(PAIRS):
                i = nc.tensor.matmul(ps_a[:, p * C:(p + 1) * C], xt[:, p * P:(p + 1) * P], w_qkv[:, 2 * C:3 * C],
                                     start=True, stop=True)
            i.then_inc(v_psum, 1)

        def pe_scores(pe, group, p):
            g, u = group.g, group.odd
            if p == 0:
                pe.wait_ge(qk_ready, g * 2 + 2)
                pe.wait_ge(k_ready, g + 1)
            after(pe, shifted, g * 4 + (p - 1))
            for half in range(2):
                w = 2 * p + half
                i = nc.tensor.matmul(ps_s[p % 2][HALF * half:HALF * half + HALF, 0:KEYS],
                                     q_rows[:, u, w, :],
                                     k_rows[:, u, w, :, :].rearrange("p h n -> p (h n)"),
                                     start=True, stop=True)
            i.then_inc(s_psum, 1)

        def pe_probs_t(pe, group, p):
            g = group.g
            pe.wait_ge(exp_ready, g * 4 + (p + 1))
            after(pe, pt_ready, g * 4 + (p - 1))
            for hp in range(NH // 2):
                i = nc.tensor.transpose(ps_pt[p % 2][:, hp * P:(hp + 1) * P],
                                        probs[:, p % 2, 2 * hp:2 * hp + 2, :].rearrange("p a b -> p (a b)"), ident[:, :])
            i.then_inc(p_psum, 1)

        def pe_pv(pe, group, p):
            g, u = group.g, group.odd
            pe.wait_ge(pt_ready, g * 4 + (p + 1))
            if p == 0:
                pe.wait_ge(v_ready, g + 1)
                after(pe, oa_ready, g)
            for half in range(2):
                for hp in range(NH // 2):
                    at = (p * 4 + hp) * 2 * HV
                    i = nc.tensor.matmul(ps_o[HALF * half:HALF * half + HALF, at:at + 2 * HV],
                                         probs_t[:, p % 2, hp, HALF * half:HALF * half + HALF],
                                         v_blk[:, u, 2 * p + half, hp, :], start=True, stop=True)
            i.then_inc(pv_done, 1)

        def pe_ot(pe, group):
            g = group.g
            pe.wait_ge(oa_ready, g + 1)
            after(pe, out_ready, g)
            pe_transpose(pe, ps_c, oa).then_inc(ot_psum, 1)

        def pe_proj(pe, group):
            g = group.g
            pe.wait_ge(ot_ready, g + 1)
            after(pe, h_ready, g * 2)
            for p in range(PAIRS):
                i = nc.tensor.matmul(ps_d[:, p * C:(p + 1) * C], ot[:, p * P:(p + 1) * P], w_proj[:, :],
                                     start=True, stop=True)
            i.then_inc(proj_psum, 1)

        def pe_xt2(pe, group):
            pe.wait_ge(norms["ln2"]["chain"].sem, group.g * LN_N + LN_N)
            pe_transpose(pe, ps_c, norms["ln2"]["xn"]).then_inc(t2_psum, 1)

        def pe_up(pe, group):
            pe.wait_ge(xt2_ready, group.g + 1)
            for f, bank in enumerate((ps_c, ps_d)):
                nc.tensor.matmul(bank[:, :], w_up[:, f * P:(f + 1) * P], xt2[:, :], start=True, stop=True).then_inc(h_psum, 1)

        def pe_down(pe, group):
            pe.wait_ge(h_ready, group.g * 2 + 2)
            for p in range(PAIRS):
                out = ps_c[:, p * C:(p + 1) * C]
                for f in range(2):
                    nc.tensor.matmul(out, hid[:, f, p * P:(p + 1) * P], w_down[:, f, :], start=(f == 0), stop=False)
                i = nc.tensor.matmul(out, ones1[:, :], b_down[:, :], start=False, stop=True)
            i.then_inc(y_psum, 1)

        def act_xt(act, group):
            g = group.g
            act.wait_ge(xt_psum, g + 1)
            after(act, v_psum, g)
            nc.scalar.copy(xt[0:C, :], ps_a[0:C, :]).then_inc(xt_ready, 1)

        def act_qk(act, group):
            g, u = group.g, group.odd
            act.wait_ge(qk_psum, g + 1)
            after(act, s_psum, g * 4 - 4)
            nc.scalar.copy(q_rows[0:C, u, :, :].rearrange("p w q -> p (w q)"), ps_a[0:C, :]).then_inc(qk_ready, 1)
            after(act, k_ready, g)
            nc.scalar.copy(kt[:, :], ps_a[C:2 * C, :]).then_inc(qk_ready, 1)

        def act_exp(act, group, p):
            act.wait_ge(shifted, group.g * 4 + (p + 1))
            nc.scalar.activation(probs[:, p % 2, :, 0:N], probs[:, p % 2, :, 0:N], ACT.Exp).then_inc(exp_ready, 1)

        def act_pt(act, group, p):
            g = group.g
            act.wait_ge(p_psum, g * 4 + (p + 1))
            after(act, pv_done, g * 4 + (p - 1))
            nc.scalar.copy(probs_t[:, p % 2, :, :].rearrange("p a b -> p (a b)"), ps_pt[p % 2][:, :]).then_inc(pt_ready, 1)

        def act_ot(act, group):
            g = group.g
            act.wait_ge(ot_psum, g + 1)
            after(act, proj_psum, g)
            nc.scalar.copy(ot[0:C, :], ps_c[0:C, :]).then_inc(ot_ready, 1)

        def act_xt2(act, group):
            g = group.g
            act.wait_ge(t2_psum, g + 1)
            after(act, h_psum, g * 2)
            nc.scalar.copy(xt2[0:C, :], ps_c[0:C, :]).then_inc(xt2_ready, 1)

        def act_gelu(act, group):
            g = group.g
            after(act, y_psum, g)
            for f, bank in enumerate((ps_c, ps_d)):
                act.wait_ge(h_psum, g * 2 + (f + 1))
                nc.scalar.activation(hid[:, f, :], bank[:, :], ACT.Gelu).then_inc(h_ready, 1)

        def dve_pe_norm(dve, group):
            g = group.g
            dve.wait_ge(xp_psum, g + 1)
            after(dve, xr_ready, g - 1)
            norm(dve, "pe", group, ps_a[:, 0:PAIRS * C].rearrange("p (a c) -> p a c", a=PAIRS), affine=True)

        def dve_ln1(dve, group):
            x_present(dve, group)
            after(dve, xt_psum, group.g)
            norm(dve, "ln1", group, xa[:, group.odd, :, :])

        def dve_shift(dve, group, p):
            g = group.g
            dve.wait_ge(s_psum, g * 4 + (p + 1))
            s = ps_s[p % 2][:, 0:KEYS].rearrange("p (h n) -> p h n", h=NH)
            nc.vector.tensor_reduce(row_max[:, p % 2, :], s, AX.X, ALU.max).then_inc(max_ready, 1)
            after(dve, p_psum, g * 4 + (p - 1))
            dve.wait_ge(max_ready, g * 4 + (p + 1))
            nc.vector.tensor_tensor(probs[:, p % 2, :, 0:N], s, row_max[:, p % 2, :].unsqueeze(2).broadcast_to([P, NH, N]),
                                    ALU.subtract).then_inc(shifted, 1)

        def dve_v(dve, group):
            g, u = group.g, group.odd
            dve.wait_ge(v_psum, g + 1)
            after(dve, pv_done, g * 4 - 4)
            v = ps_a[:, 0:PAIRS * C].rearrange("p (a h d) -> p a h d", a=PAIRS, d=HD)
            blk = v_blk[:, u, :, :, :].rearrange("p (a w) h d -> p w a h d", w=2)
            for half in range(2):
                rows = v[HALF * half:HALF * half + HALF]
                nc.vector.tensor_copy(blk[0:HALF, half, :, :, 0:HD], rows[:, :, 0:NH:2, :])
                i = nc.vector.tensor_copy(blk[HALF:P, half, :, :, HV:HV + HD], rows[:, :, 1:NH:2, :])
            i.then_inc(v_ready, 1)

        def dve_oa(dve, group):
            g = group.g
            dve.wait_ge(pv_done, g * 4 + 4)
            o = ps_o[:, 0:PAIRS * NH * HV].rearrange("p (a v) -> p a v", v=HV)
            nc.vector.reciprocal(rec[:, :].unsqueeze(2), o[:, :, HD:HV]).then_inc(rec_ready, 1)
            dve.wait_ge(rec_ready, g + 1)
            after(dve, ot_psum, g)
            nc.vector.tensor_tensor(oa[:, :, :].rearrange("p a (h d) -> p (a h) d", d=HD), o[:, :, 0:HD],
                                    rec[:, :].unsqueeze(2).broadcast_to([P, PAIRS * NH, HD]), ALU.mult).then_inc(oa_ready, 1)

        def dve_x1(dve, group):
            g = group.g
            dve.wait_ge(proj_psum, g + 1)
            dve.wait_ge(xr_ready, g + 1)
            nc.vector.tensor_tensor(x1[:, :, :], xr[:, group.odd, :, :], ps_d[:, 0:PAIRS * C].rearrange("p (a c) -> p a c", a=PAIRS),
                                    ALU.add).then_inc(x1_ready, 1)
            dve.wait_ge(x1_ready, g + 1)
            after(dve, t2_psum, g)
            norm(dve, "ln2", group, x1[:, :, :])

        def dve_out(dve, group):
            g, u = group.g, group.odd
            dve.wait_ge(y_psum, g + 1)
            after(dve, stored[u], group.half * 32)
            nc.vector.tensor_tensor(xo[:, u, :, :], x1[:, :, :], ps_c[:, 0:PAIRS * C].rearrange("p (a c) -> p a c", a=PAIRS),
                                    ALU.add).then_inc(out_ready, 1)

        def pool_residual(pool, group):
            x_present(pool, group)
            after(pool, x1_ready, group.g - 1)
            settle(pool)
            nc.gpsimd.tensor_copy(xr[:, group.odd, :, :], xa[:, group.odd, :, :]).then_inc(xr_ready, 1)

        def pool_keys(pool, group):
            g, u = group.g, group.odd
            pool.wait_ge(qk_ready, g * 2 + 2)
            after(pool, s_psum, g * 4 - 4)
            settle(pool)
            src_k = kt[:, :].rearrange("p (w q) -> p w q", w=NW)[:, :, 0:N]
            for h in range(NH):
                i = nc.gpsimd.tensor_scalar(k_rows[0:C, u, :, h, :], src_k, head_mask[:, h:h + 1], 1.0, ALU.mult, ALU.mult)
            i.then_inc(k_ready, 1)

        def run(first, last):
            def steps(eng, step, a_only, c_only):
                f = Group(first // 2, 0)
                a_only(eng, f)
                step(eng, f, True, False)
                with eng.Fori(first // 2, last // 2 - 1) as i:
                    step(eng, Group(i, 1), True, True)
                    step(eng, Group(i + 1, 0), True, True)
                end = Group(last // 2 - 1, 1)
                step(eng, end, False, True)
                c_only(eng, end)

            with nc.Block() as block:
                @block.sync
                def _(sp):
                    def step(sp, group, a, c):
                        if a:
                            sync_load(sp, group.next())
                        if c:
                            sync_store(sp, group.prev())

                    steps(sp, step, sync_load, sync_store)
                    for u in range(2):
                        sp.wait_ge(stored[u], last // 2 * 32)

                @block.tensor
                def _(pe):
                    def a_only(pe, group):
                        if k == 0:
                            pe_patch(pe, group)
                        pe_xt(pe, group)
                        pe_qk(pe, group)
                        pe_v(pe, group)

                    def step(pe, group, a, c):
                        nxt = group.next() if a else None
                        prv = group.prev() if c else None
                        if a and k == 0:
                            pe_patch(pe, nxt)
                        pe_scores(pe, group, 0)
                        if c:
                            pe_ot(pe, prv)
                        pe_scores(pe, group, 1)
                        pe_probs_t(pe, group, 0)
                        if c:
                            pe_proj(pe, prv)
                        if a:
                            pe_xt(pe, nxt)
                        pe_pv(pe, group, 0)
                        pe_scores(pe, group, 2)
                        pe_probs_t(pe, group, 1)
                        if a:
                            pe_qk(pe, nxt)
                        pe_pv(pe, group, 1)
                        pe_scores(pe, group, 3)
                        if c:
                            pe_xt2(pe, prv)
                        pe_probs_t(pe, group, 2)
                        if a:
                            pe_v(pe, nxt)
                        pe_pv(pe, group, 2)
                        if c:
                            pe_up(pe, prv)
                        pe_probs_t(pe, group, 3)
                        pe_pv(pe, group, 3)
                        if c:
                            pe_down(pe, prv)

                    def c_only(pe, group):
                        pe_ot(pe, group)
                        pe_proj(pe, group)
                        pe_xt2(pe, group)
                        pe_up(pe, group)
                        pe_down(pe, group)

                    steps(pe, step, a_only, c_only)

                @block.scalar
                def _(act):
                    def a_only(act, group):
                        act_xt(act, group)
                        act_qk(act, group)

                    def step(act, group, a, c):
                        nxt = group.next() if a else None
                        prv = group.prev() if c else None
                        if c:
                            act_ot(act, prv)
                        act_exp(act, group, 0)
                        if a:
                            act_xt(act, nxt)
                        act_pt(act, group, 0)
                        act_exp(act, group, 1)
                        if a:
                            act_qk(act, nxt)
                        act_pt(act, group, 1)
                        act_exp(act, group, 2)
                        if c:
                            act_xt2(act, prv)
                        act_pt(act, group, 2)
                        act_exp(act, group, 3)
                        act_pt(act, group, 3)
                        if c:
                            act_gelu(act, prv)

                    def c_only(act, group):
                        act_ot(act, group)
                        act_xt2(act, group)
                        act_gelu(act, group)

                    steps(act, step, a_only, c_only)

                @block.vector
                def _(dve):
                    def a_only(dve, group):
                        if k == 0:
                            dve_pe_norm(dve, group)
                        dve_ln1(dve, group)
                        dve_v(dve, group)

                    def step(dve, group, a, c):
                        nxt = group.next() if a else None
                        prv = group.prev() if c else None
                        if a and k == 0:
                            dve_pe_norm(dve, nxt)
                        dve_shift(dve, group, 0)
                        if a:
                            dve_ln1(dve, nxt)
                        dve_shift(dve, group, 1)
                        if c:
                            dve_x1(dve, prv)
                        dve_shift(dve, group, 2)
                        dve_shift(dve, group, 3)
                        if a:
                            dve_v(dve, nxt)
                        dve_oa(dve, group)
                        if c:
                            dve_out(dve, prv)

                    def c_only(dve, group):
                        dve_x1(dve, group)
                        dve_out(dve, group)

                    steps(dve, step, a_only, c_only)

                @block.gpsimd
                def _(pool):
                    def a_only(pool, group):
                        if k == 0:
                            rsqrt(pool, "pe", group.g)
                        rsqrt(pool, "ln1", group.g)
                        pool_keys(pool, group)

                    def step(pool, group, a, c):
                        nxt = group.next() if a else None
                        prv = group.prev() if c else None
                        pool_residual(pool, group)
                        if a and k == 0:
                            rsqrt(pool, "pe", nxt.g)
                        if a:
                            rsqrt(pool, "ln1", nxt.g)
                        if c:
                            rsqrt(pool, "ln2", prv.g)
                        if a:
                            pool_keys(pool, nxt)

                    def c_only(pool, group):
                        rsqrt(pool, "ln2", group.g)

                    steps(pool, step, a_only, c_only)

        if k == 0:
            run(0, GROUPS)
        else:
            run(0, UNCUT)
            with nc.Block() as block:
                @block.vector
                def _(dve):
                    fill_bias(dve, last_row=True)
            run(UNCUT, GROUPS)

def fast_weights(nc, V, x, scratch):
    with ExitStack() as ctx:
        def sb(name, shape, dt=F32):
            return ctx.enter_context(nc.sbuf_tensor("f_" + name, shape, dt))

        def sem(name):
            return ctx.enter_context(nc.semaphore("f_" + name))

        ps_t, ps_p0, ps_p1, ps_pred, ps_out, ps_flag = [
            ctx.enter_context(nc.psum_tensor(f"f_bank{i}", [P, 512], F32)) for i in range(6)]
        ps_p = [ps_p0, ps_p1]

        w_f = sb("w_f", [C, QKV3])
        ident = sb("ident", [P, P])
        same_image = sb("same_image", [P, P])
        ones = sb("ones", [P, P])
        neghalf = sb("neghalf", [P, 4])
        st = [sb(n, [P, FI, C]) for n in ("s0", "m0", "s1", "m1")]
        s0, m0, s1, m1 = st
        wp = sb("wp", [P, 2, FI, C])
        xs = sb("xs", [P, 2, C])
        xc = sb("xc", [P, 2, C])
        sq = sb("sq", [P, 2, 2 * C])
        small = sb("small", [P, 8, 4])
        xn = sb("xn", [P, 2, C])
        xnt = sb("xnt", [C, 2 * P])
        sg = sb("sg", [P, 2, QKV3])
        pr = sb("pr", [P, 2, QKV3])
        rows = sb("rows", [P, CH, QKV3])
        res = sb("res", [P, CH, C])
        now = sb("now", [P, 2, QKV3])
        prod_a = sb("prod_a", [P, FI, C])
        prod_b = sb("prod_b", [P, FI, C])
        prod_e = sb("prod_e", [P, FI, C])
        prod_f = sb("prod_f", [P, FI, C])
        prod_g = sb("prod_g", [P, FI, C])
        h, sig, act_, om, ds, da, dhs, h2, sig2, a2 = [sb(n, [P, FI]) for n in
                                                    ("h", "sig", "act", "om", "ds", "da", "dhs", "h2", "sig2", "a2")]
        pred, dp, dps, o_row = [sb(n, [P, C]) for n in ("pred", "dp", "dps", "o_row")]
        nz = sb("nz", [P, 8])
        flag = sb("flag", [P, 1], I32)

        loaded, prep, flag_ready = sem("loaded"), sem("prep"), sem("flag_ready")
        x_in, rows_in, kept, saved = sem("x_in"), sem("rows_in"), sem("kept"), sem("saved")
        pre = Steps(sem("pre"), 16)
        xt_psum, xt_ready, p_psum = sem("xt_psum"), sem("xt_ready"), sem("p_psum")
        sg_ready, rs_ready, row_ready = sem("sg_ready"), sem("rs_ready"), sem("row_ready")
        per_step = Steps(sem("dve"), 22)
        gate_ready, ds_ready, e_ready, pred_psum = sem("gate_ready"), sem("ds_ready"), sem("e_ready"), sem("pred_psum")
        f_ready, g_ready, gate2_ready, out_psum = sem("f_ready"), sem("g_ready"), sem("gate2_ready"), sem("out_psum")
        pool_ds = sem("pool_ds")
        flag_psum, now_ready = sem("flag_psum"), sem("now_ready")
        flag_step = Steps(sem("flag_step"), 6)

        with nc.Block() as block:
            @block.sync
            def _(sp):
                sp.dma_start(w_f[:, :], V["w_fused_t"]).then_inc(loaded, 16)
                for j, (a, b) in enumerate((("W0_t", "P0_t"), ("W1", "P1"))):
                    for t, n in ((st[2 * j], a), (wp[:, j], b)):
                        src = V[n].rearrange("(s f) c -> s (f c)", s=FS).unsqueeze(0).broadcast_to([B, FS, FI * C])
                        sp.dma_start(t[:, :, :].rearrange("p f c -> p (f c)") , src).then_inc(loaded, 16)

            @block.gpsimd
            def _(pool):
                nc.gpsimd.memset(ident[:, :], 0.0).then_inc(prep, 1)
                nc.gpsimd.memset(same_image[:, :], 1.0).then_inc(prep, 1)
                nc.gpsimd.memset(neghalf[:, :], -0.5).then_inc(prep, 1)
                nc.gpsimd.memset(ones[:, :], 1.0).then_inc(prep, 1)
                pool.wait_ge(prep, 4)
                nc.gpsimd.affine_select(out=ident[:, :], in_=ident[:, :], compare_op=ALU.not_equal, fill=1.0,
                                        base=0, pattern=[[-1, P]], channel_multiplier=1).then_inc(prep, 1)
                blocks = same_image[:, :].rearrange("p (b s) -> p b s", s=FS)
                nc.gpsimd.affine_select(out=blocks, in_=blocks, compare_op=ALU.is_ge, fill=0.0, base=0,
                                        pattern=[[-FS, B], [0, FS]], channel_multiplier=1).then_inc(prep, 1)
                pool.wait_ge(prep, 6)
                nc.gpsimd.affine_select(out=blocks, in_=blocks, compare_op=ALU.is_ge, fill=0.0, base=FS - 1,
                                        pattern=[[FS, B], [0, FS]], channel_multiplier=-1).then_inc(prep, 1)

            @block.vector
            def _(dve):
                nc.vector.memset(m0[:, :, :], 0.0)
                nc.vector.memset(m1[:, :, :], 0.0)
                nc.vector.memset(flag[:, :], 1).then_inc(flag_ready, 1)
                dve.wait_ge(loaded, 16 * 5)
                nc.vector.tensor_tensor(s0[:, :, :], s0[:, :, :], wp[:, 0], ALU.add)
                nc.vector.tensor_tensor(s1[:, :, :], s1[:, :, :], wp[:, 1], ALU.add)

        def chunks(eng, chunk, skipped=None):
            with eng.Fori(0, CHUNKS) as i:
                eng.wait_ge(flag_ready, i + 1)
                settle(eng)
                live = eng.value_load(flag[0:1, 0:1], min_val=0, max_val=P)
                with eng.If(live > 0):
                    chunk(eng, i)
                with eng.Else():
                    if skipped:
                        skipped(eng)
                    else:
                        eng.nop()

        def wide(ap, axis):
            return ap.unsqueeze(axis).broadcast_to([P, FI, C])

        def eights(ap):
            return [ap[:, 8 * j:8 * j + 8, :].rearrange("p f c -> p (f c)") for j in range(FI // 8)]

        with nc.Block() as block:
            @block.sync
            def _(sp):
                def chunk(sp, i):
                    at = i * CH
                    after_saved = saved
                    for j in range(2):
                        sp.dma_start(xs[:, j, :], x[:, bass.ds(at + 8 * j, 8), :]).then_inc(x_in, 16)
                    sp.wait_ge(row_ready, 8 * 0 + i + 1)
                    for j in range(2):
                        sp.dma_start(scratch[:, 8 * j:8 * j + 8, :], pr[:, j, :]).then_inc(kept, 16)
                    sp.wait_ge(kept, i * 32 + 32)
                    sp.dma_start(rows[:, :, :].rearrange("p t c -> p (t c)"),
                                 scratch.rearrange("b t c -> b (t c)").unsqueeze(1).broadcast_to([B, FS, CH * QKV3])).then_inc(rows_in, 16)
                    sp.dma_start(res[:, :, :].rearrange("p t c -> p (t c)"),
                                 x[:, bass.ds(at, CH), :].rearrange("b t c -> b (t c)").unsqueeze(1).broadcast_to([B, FS, CH * C])).then_inc(rows_in, 16)
                    sp.wait_ge(per_step.sem, (i * CH + CH) * per_step.per)
                    sp.dma_start(x[:, bass.ds(at, CH), :].rearrange("b t c -> b (t c)"),
                                 res[0:P:FS, :, :].rearrange("p t c -> p (t c)")).then_inc(saved, 16)
                    sp.wait_ge(saved, i * 16 + 16)
                    settle(sp)
                chunks(sp, chunk)

            @block.tensor
            def _(pe):
                def chunk(pe, i):
                    pe.wait_ge(pre.sem, i * pre.per + 7)
                    settle(pe)
                    for j in range(2):
                        nc.tensor.transpose(ps_t[0:C, j * P:(j + 1) * P], xn[:, j, :], ident[:, :]).then_inc(xt_psum, 1)
                    pe.wait_ge(xt_ready, i + 1)
                    settle(pe)
                    for j in range(2):
                        nc.tensor.matmul(ps_p[j][:, 0:QKV3], xnt[:, j * P:(j + 1) * P], w_f[:, :], start=True, stop=True).then_inc(p_psum, 1)
                    with pe.Fori(0, CH) as t:
                        n = i * CH + t
                        pe.wait_ge(per_step.sem, n * per_step.per + 4)
                        for j, e in enumerate(eights(prod_b)):
                            last = nc.tensor.matmul(ps_pred[:, :], same_image[:, :], e, start=(j == 0), stop=(j == 3))
                        last.then_inc(pred_psum, 1)
                        pe.wait_ge(g_ready, n + 1)
                        for j, e in enumerate(eights(prod_g)):
                            last = nc.tensor.matmul(ps_out[:, :], same_image[:, :], e, start=(j == 0), stop=(j == 3))
                        last.then_inc(out_psum, 1)
                    pe.wait_ge(flag_step.sem, i * 6 + 5)
                    nc.tensor.matmul(ps_flag[:, 0:1], ones[:, :], nz[:, 4:5], start=True, stop=True).then_inc(flag_psum, 1)
                chunks(pe, chunk)

            @block.scalar
            def _(act):
                def chunk(act, i):
                    act.wait_ge(xt_psum, i * 2 + 2)
                    nc.scalar.copy(xnt[:, :], ps_t[0:C, 0:2 * P]).then_inc(xt_ready, 1)
                    act.wait_ge(p_psum, i * 2 + 2)
                    for j in range(2):
                        nc.scalar.activation(sg[:, j, 0:3 * C], ps_p[j][:, 0:3 * C], ACT.Sigmoid).then_inc(sg_ready, 1)
                        nc.scalar.activation(pr[:, j, 3 * C:3 * C + 1], ps_p[j][:, 3 * C:3 * C + 1], ACT.Sigmoid, scale=-1.0).then_inc(sg_ready, 1)
                        nc.scalar.activation(pr[:, j, 3 * C + 1:QKV3], ps_p[j][:, 3 * C + 1:QKV3], ACT.Sigmoid).then_inc(sg_ready, 1)
                    act.wait_ge(rows_in, i * 32 + 32)
                    with act.Fori(0, CH // 2) as t2:
                        for u in range(2):
                            t = t2 * 2 + u
                            n = i * CH + t
                            act.wait_ge(per_step.sem, n * per_step.per - per_step.per + 0) if False else None
                            nc.scalar.copy(now[:, u, :], rows[:, bass.ds(t, 1), :].rearrange("p t c -> p (t c)")).then_inc(now_ready, 1)
                            act.wait_ge(per_step.sem, n * per_step.per + 2)
                            nc.scalar.activation(sig[:, :], h[:, :], ACT.Sigmoid).then_inc(gate_ready, 1)
                            act.wait_ge(per_step.sem, n * per_step.per + 18)
                            nc.scalar.activation(sig2[:, :], h2[:, :], ACT.Sigmoid).then_inc(gate2_ready, 1)
                chunks(act, chunk)

        

            @block.vector
            def _(dve):
                tt, ts, red = nc.vector.tensor_tensor, nc.vector.tensor_scalar, nc.vector.tensor_reduce

                def norms(c, i):
                    def pair(ap):
                        return ap.unsqueeze(2).broadcast_to([P, 2, C])
                    c.start(i)
                    dve.wait_ge(x_in, i * 32 + 32)
                    c.did(red(small[:, 0, 0:2], xs[:, :, :], AX.X, ALU.add))
                    c.wait(dve)
                    c.did(ts(small[:, 1, 0:2], small[:, 0, 0:2], 1.0 / C, None, ALU.mult))
                    c.wait(dve)
                    c.did(tt(xc[:, :, :], xs[:, :, :], pair(small[:, 1, 0:2]), ALU.subtract))
                    c.wait(dve)
                    c.did(tt(sq[:, :, 0:C], xc[:, :, :], xc[:, :, :], ALU.mult))
                    c.wait(dve)
                    c.did(red(small[:, 2, 0:2], sq[:, :, 0:C], AX.X, ALU.add))
                    c.wait(dve)
                    c.did(ts(small[:, 3, 0:2], small[:, 2, 0:2], 1.0 / C, EPS, ALU.mult, ALU.add))
                    dve.wait_ge(rs_ready, i * 2 + 1)
                    c.did(tt(xn[:, :, :], xc[:, :, :], pair(small[:, 4, 0:2]), ALU.mult))
                    dve.wait_ge(sg_ready, i * 6 + 6)
                    for j in range(2):
                        c.did(tt(pr[:, j, 0:3 * C], ps_p[j][:, 0:3 * C], sg[:, j, 0:3 * C], ALU.mult))
                    c.wait(dve)
                    c.did(tt(sq[:, :, :], pr[:, :, 0:2 * C], pr[:, :, 0:2 * C], ALU.mult))
                    c.wait(dve)
                    c.did(red(small[:, 5, 0:4], sq[:, :, :].rearrange("p j (a c) -> p (j a) c", a=2), AX.X, ALU.add))
                    c.did(ts(pr[:, :, 2 * C:3 * C], pr[:, :, 2 * C:3 * C], 2.0 / C, None, ALU.mult))
                    c.did(ts(pr[:, :, 3 * C + 1:3 * C + 2], pr[:, :, 3 * C + 1:3 * C + 2], -2.0 * LR, None, ALU.mult))
                    dve.wait_ge(rs_ready, i * 2 + 2)
                    c.did(ts(small[:, 7, 0:4], small[:, 6, 0:4], L2_LIMIT, None, ALU.min))
                    c.wait(dve)
                    for j in range(2):
                        v = pr[:, j, 0:2 * C].rearrange("p (a c) -> p a c", a=2)
                        c.did(tt(v, v, small[:, 7, 2 * j:2 * j + 2].unsqueeze(2).broadcast_to([P, 2, C]), ALU.mult))
                    c.end()
                    c.wait(dve)
                    nc.vector.tensor_copy(nz[:, 6:7], pr[:, 0, 0:1]).then_inc(row_ready, 1)

                def one(c, n, t, u):
                    q, kk, v = (now[:, u, j * C:(j + 1) * C] for j in range(3))
                    keep, theta, eta = (now[:, u, 3 * C + j:3 * C + j + 1] for j in range(3))
                    c.start(n)
                    dve.wait_ge(now_ready, n + 1)
                    c.did(tt(prod_a[:, :, :], s0[:, :, :], wide(kk, 1), ALU.mult))
                    c.wait(dve)
                    c.did(red(h[:, :], prod_a[:, :, :], AX.X, ALU.add))
                    dve.wait_ge(gate_ready, n + 1)
                    c.did(tt(act_[:, :], h[:, :], sig[:, :], ALU.mult))
                    c.wait(dve)
                    c.did(tt(prod_b[:, :, :], s1[:, :, :], wide(act_[:, :], 2), ALU.mult))
                    dve.wait_ge(pred_psum, n + 1)
                    c.did(red(pred[:, :], ps_pred[:, :].rearrange("p (f c) -> p c f", c=C), AX.X, ALU.add))
                    c.wait(dve)
                    c.did(nc.vector.scalar_tensor_tensor(out=dp[:, :], in0=pred[:, :], scalar=2.0 / C, in1=v,
                                                         op0=ALU.mult, op1=ALU.subtract))
                    c.wait(dve)
                    c.did(ts(dps[:, :], dp[:, :], theta, None, ALU.mult))
                    c.did(tt(prod_a[:, :, :], s1[:, :, :], wide(dp[:, :], 1), ALU.mult))
                    c.wait(dve)
                    c.did(red(da[:, :], prod_a[:, :, :], AX.X, ALU.add))
                    c.wait(dve)
                    dve.wait_ge(ds_ready, n + 1)
                    c.did(nc.vector.scalar_tensor_tensor(out=dhs[:, :], in0=da[:, :], scalar=theta, in1=ds[:, :],
                                                         op0=ALU.mult, op1=ALU.mult))
                    c.wait(dve)
                    c.did(tt(prod_a[:, :, :], wide(dhs[:, :], 2), wide(kk, 1), ALU.mult))
                    c.wait(dve)
                    stt = nc.vector.scalar_tensor_tensor
                    c.did(stt(out=m0[:, :, :], in0=m0[:, :, :], scalar=eta, in1=prod_a[:, :, :], op0=ALU.mult, op1=ALU.add))
                    c.wait(dve)
                    c.did(stt(out=s0[:, :, :], in0=s0[:, :, :], scalar=keep, in1=m0[:, :, :], op0=ALU.mult, op1=ALU.add))
                    dve.wait_ge(e_ready, n + 1)
                    c.did(stt(out=m1[:, :, :], in0=m1[:, :, :], scalar=eta, in1=prod_e[:, :, :], op0=ALU.mult, op1=ALU.add))
                    c.wait(dve)
                    c.did(stt(out=s1[:, :, :], in0=s1[:, :, :], scalar=keep, in1=m1[:, :, :], op0=ALU.mult, op1=ALU.add))
                    c.did(nc.vector.memset(pred[:, 0:1], 0.0))
                    dve.wait_ge(f_ready, n + 1)
                    c.did(red(h2[:, :], prod_f[:, :, :], AX.X, ALU.add))
                    c.did(nc.vector.memset(pred[:, 1:2], 0.0))
                    dve.wait_ge(gate2_ready, n + 1)
                    c.did(tt(a2[:, :], h2[:, :], sig2[:, :], ALU.mult))
                    dve.wait_ge(out_psum, n + 1)
                    c.did(red(o_row[:, :], ps_out[:, :].rearrange("p (f c) -> p c f", c=C), AX.X, ALU.add))
                    c.wait(dve)
                    r = res[:, bass.ds(t, 1), :].rearrange("p t c -> p (t c)")
                    c.did(tt(r, r, o_row[:, :], ALU.add))
                    c.wait(dve)
                    c.did(nc.vector.memset(pred[:, 2:3], 0.0))
                    c.end()

                def chunk(dve, i):
                    norms(pre, i)
                    dve.wait_ge(rows_in, i * 32 + 32)
                    settle(dve)
                    with dve.Fori(0, CH // 2) as t2:
                        for u in range(2):
                            one(per_step, i * CH + t2 * 2 + u, t2 * 2 + u, u)
                    c = flag_step
                    c.start(i)
                    dve.wait_ge(per_step.sem, (i * CH + CH) * per_step.per)
                    for j, s in enumerate(st):
                        c.did(nc.vector.tensor_scalar(prod_a[:, :, :], s[:, :, :], 0.0, None, ALU.not_equal, ALU.max, accum_out=nz[:, j:j + 1]))
                        c.wait(dve)
                    c.did(red(nz[:, 4:5], nz[:, 0:4], AX.X, ALU.max))
                    dve.wait_ge(flag_psum, i + 1)
                    dve.wait_ge(saved, i * 16 + 16)
                    c.did(nc.vector.tensor_copy(nz[:, 5:6], ps_flag[:, 0:1]))
                    c.end()
                    c.wait(dve)
                    nc.vector.tensor_copy(flag[:, :], nz[:, 5:6]).then_inc(flag_ready, 1)
                chunks(dve, chunk, lambda dve: dve.sem_inc(flag_ready, 1))

            @block.gpsimd
            def _(pool):
                def chunk(pool, i):
                    pool.wait_ge(pre.sem, i * pre.per + 6)
                    nc.gpsimd.tensor_tensor(small[:, 4, 0:2], small[:, 3, 0:2], neghalf[:, 0:2], ALU.pow).then_inc(rs_ready, 1)
                    pool.wait_ge(pre.sem, i * pre.per + 11)
                    nc.gpsimd.tensor_tensor(small[:, 6, 0:4], small[:, 5, 0:4], neghalf[:, 0:4], ALU.pow).then_inc(rs_ready, 1)
                    with pool.Fori(0, CH // 2) as t2:
                        for u in range(2):
                            n = i * CH + t2 * 2 + u
                            at = n * per_step.per
                            q = now[:, u, 0:C]
                            pool.wait_ge(per_step.sem, at + 3)
                            settle(pool)
                            nc.gpsimd.tensor_scalar(om[:, :], sig[:, :], -1.0, 1.0, ALU.mult, ALU.add).then_inc(pool_ds, 1)
                            pool.wait_ge(pool_ds, n * 2 + 1)
                            nc.gpsimd.tensor_tensor(ds[:, :], om[:, :], act_[:, :], ALU.mult).then_inc(pool_ds, 1)
                            pool.wait_ge(pool_ds, n * 2 + 2)
                            nc.gpsimd.tensor_tensor(ds[:, :], ds[:, :], sig[:, :], ALU.add).then_inc(ds_ready, 1)
                            pool.wait_ge(per_step.sem, at + 7)
                            nc.gpsimd.tensor_tensor(prod_e[:, :, :], wide(act_[:, :], 2), wide(dps[:, :], 1), ALU.mult).then_inc(e_ready, 1)
                            pool.wait_ge(per_step.sem, at + 13)
                            nc.gpsimd.tensor_tensor(prod_f[:, :, :], s0[:, :, :], wide(q, 1), ALU.mult).then_inc(f_ready, 1)
                            pool.wait_ge(per_step.sem, at + 19)
                            nc.gpsimd.tensor_tensor(prod_g[:, :, :], s1[:, :, :], wide(a2[:, :], 2), ALU.mult).then_inc(g_ready, 1)
                chunks(pool, chunk)


def experts(nc, V, x, out):
    with ExitStack() as ctx:
        def sb(name, shape, dt=F32):
            return ctx.enter_context(nc.sbuf_tensor("e_" + name, shape, dt))

        def sem(name):
            return ctx.enter_context(nc.semaphore("e_" + name))

        banks = [ctx.enter_context(nc.psum_tensor(f"e_bank{i}", [P, 512], F32)) for i in range(8)]
        ps_t, ps_small, ps_choice, ps_h0, ps_h1, ps_h2, ps_y0, ps_y1 = banks
        ps_h, ps_y = [ps_h0, ps_h1, ps_h2], [ps_y0, ps_y1]
        ps_logit, ps_cum, ps_tot = (ps_small[:, j * TILES * E:(j + 1) * TILES * E].rearrange("p (t e) -> p t e", e=E)
                                    for j in range(3))

        w1 = sb("w1", [P, E, F])
        w2 = sb("w2", [P, E, 2, C])
        b2 = sb("b2", [P, C])
        w_gate = sb("w_gate", [C, E])
        b_gate = sb("b_gate", [1, E])
        ones1 = sb("ones1", [1, P])
        ident = sb("ident", [P, P])
        upto = sb("upto", [P, P])
        ones = sb("ones", [P, P])
        rank = sb("rank", [P, TILES, E])
        neghalf = sb("neghalf", [P, TILES])
        xg = sb("xg", [P, 2, TILES, C])
        xr = sb("xr", [P, 2, TILES, C])
        xc, sq, xn = sb("xc", [P, TILES, C]), sb("sq", [P, TILES, C]), sb("xn", [P, TILES, C])
        s, m, ss, var, rstd = [sb(n, [P, TILES]) for n in ("s", "m", "ss", "var", "rstd")]
        xt = sb("xt", [P, 2, SIZE])
        top, low, first, total, share, pos, kept = [sb(n, [P, TILES]) for n in
                                                    ("top", "low", "first", "total", "share", "pos", "kept")]
        z, ez, eq, choice, place = [sb(n, [P, TILES, E]) for n in ("z", "ez", "eq", "choice", "place")]
        before = sb("before", [P, TILES + 1, E])
        weight = sb("weight", [P, 2, TILES])
        hid = sb("hid", [P, 3, 512])
        y, over, under = [sb(n, [P, TILES, C]) for n in ("y", "over", "under")]
        finite = sb("finite", [P, TILES, C], I32)
        res = sb("res", [P, 2, TILES, C])

        loaded, prep, zeroed = sem("loaded"), sem("prep"), sem("zeroed")
        x_in, stored = [sem("x_in0"), sem("x_in1")], [sem("stored0"), sem("stored1")]
        ln = Steps(sem("ln"), 7)
        pick = Steps(sem("pick"), 17)
        end = Steps(sem("end"), 7)
        rstd_ready, xt_psum, xt_ready, logit_psum, ez_ready = [sem(n) for n in (
            "rstd_ready", "xt_psum", "xt_ready", "logit_psum", "ez_ready")]
        choice_psum, count_psum, choice_ready = sem("choice_psum"), sem("count_psum"), sem("choice_ready")
        xr_ready = sem("xr_ready")
        h_psum, y_psum = sem("h_psum"), sem("y_psum")
        hid_act, hid_dve, hid_used = sem("hid_act"), sem("hid_dve"), sem("hid_used")
        UNITS = E * 2

        with nc.Block() as block:
            @block.sync
            def _(sp):
                def load(o, i):
                    sp.dma_start(o, i).then_inc(loaded, 16)
                sp.wait_ge(zeroed, 3)
                load(w1[0:C, :, :], V["moe_w1"].rearrange("e d f -> d e f"))
                load(w2[:, :, :, :], V["moe_w2"].rearrange("e (h p) d -> p e h d", p=P))
                load(w_gate[:, :], V["gate_w"])
                load(b_gate[:, :], V["gate_b"].rearrange("(a e) -> a e", a=1))
                load(w1[K1 - 1:K1, :, :], V["moe_b1"].unsqueeze(0))
                load(b2[C:C + E, :], V["moe_b2"])
                sp.wait_ge(loaded, 16 * 6)

            @block.gpsimd
            def _(pool):
                nc.gpsimd.memset(ident[:, :], 0.0).then_inc(prep, 1)
                nc.gpsimd.memset(upto[:, :], 1.0).then_inc(prep, 1)
                nc.gpsimd.memset(ones[:, :], 1.0).then_inc(prep, 1)
                nc.gpsimd.memset(neghalf[:, :], -0.5).then_inc(prep, 1)
                nc.gpsimd.memset(before[:, :, :], 0.0).then_inc(prep, 1)
                nc.gpsimd.memset(ones1[:, :], 1.0).then_inc(prep, 1)
                pool.wait_ge(prep, 6)
                nc.gpsimd.affine_select(out=ident[:, :], in_=ident[:, :], compare_op=ALU.not_equal, fill=1.0,
                                        base=0, pattern=[[-1, P]], channel_multiplier=1).then_inc(prep, 1)
                nc.gpsimd.affine_select(out=upto[:, :], in_=upto[:, :], compare_op=ALU.is_ge, fill=0.0,
                                        base=0, pattern=[[1, P]], channel_multiplier=-1).then_inc(prep, 1)
                pool.wait_ge(prep, 8)
                pool.wait_ge(zeroed, 3)
                own = w1[C:C + E, :, :]
                nc.gpsimd.affine_select(out=own, in_=own, compare_op=ALU.not_equal, fill=0.0,
                                        base=0, pattern=[[-1, E], [0, F]], channel_multiplier=1).then_inc(prep, 1)

            @block.vector
            def _(dve):
                nc.vector.memset(w1[C:P, :, :], 0.0).then_inc(zeroed, 1)
                dve.wait_ge(zeroed, 1)
                nc.vector.memset(w1[C:C + E, :, :], OFF).then_inc(zeroed, 1)
                nc.vector.memset(b2[:, :], 0.0).then_inc(zeroed, 1)
                nc.vector.memset(xt[C:P, :, :], 1.0)
                for e in range(E):
                    nc.vector.memset(rank[:, :, e:e + 1], float(E - e))

        def tiles(ap, g):
            return ap[bass.ds(g, 1)].rearrange("g t p c -> p (g t) c")

        x_t = x.rearrange("b t c -> (b t) c").rearrange("(g t p) c -> g t p c", t=TILES, p=P)
        out_t = out.rearrange("b t c -> (b t) c").rearrange("(g t p) c -> g t p c", t=TILES, p=P)

        def on_tiles(ap, n):
            return ap.unsqueeze(2).broadcast_to([P, TILES, n])

        def sync_load(sp, group):
            u = group.odd
            after(sp, ln.sem, (group.g - 2) * ln.per + ln.per)
            settle(sp)
            after(sp, xr_ready, group.g - 1)
            settle(sp)
            sp.dma_start(xg[:, u, :, :], tiles(x_t, group.g)).then_inc(x_in[u], 16)

        def sync_store(sp, group):
            u = group.odd
            sp.wait_ge(end.sem, group.g * end.per + end.per)
            settle(sp)
            sp.dma_start(tiles(out_t, group.g), res[:, u, :, :]).then_inc(stored[u], 16)

        def pe_xt(pe, group):
            pe.wait_ge(ln.sem, group.g * ln.per + ln.per)
            settle(pe)
            for t in range(TILES):
                i = nc.tensor.transpose(ps_t[0:C, t * P:(t + 1) * P], xn[:, t, :], ident[:, :])
            i.then_inc(xt_psum, 1)

        def pe_logits(pe, group):
            pe.wait_ge(xt_ready, group.g + 1)
            after(pe, pick.sem, (group.g - 1) * pick.per + pick.per)
            settle(pe)
            for t in range(TILES):
                nc.tensor.matmul(ps_logit[:, t, :], xt[0:C, group.odd, t * P:(t + 1) * P], w_gate[:, :], start=True, stop=False)
                i = nc.tensor.matmul(ps_logit[:, t, :], ones1[:, :], b_gate[:, :], start=False, stop=True)
            i.then_inc(logit_psum, 1)

        def pe_choice(pe, group):
            g = group.g
            pe.wait_ge(pick.sem, g * pick.per + 6)
            after(pe, choice_ready, g)
            settle(pe)
            for t in range(TILES):
                i = nc.tensor.transpose(ps_choice[0:E, t * P:(t + 1) * P], choice[:, t, :], ident[:, :])
            i.then_inc(choice_psum, 1)
            flat = choice[:, :, :].rearrange("p t e -> p (t e)")
            nc.tensor.matmul(ps_cum.rearrange("p t e -> p (t e)"), upto[:, :], flat, start=True, stop=True)
            nc.tensor.matmul(ps_tot.rearrange("p t e -> p (t e)"), ones[:, :], flat, start=True, stop=True).then_inc(count_psum, 1)

        def pe_hidden(pe, group, n):
            g, u = group.g, group.odd
            e, half = n // 2, n % 2
            if n == 0:
                pe.wait_ge(choice_ready, g + 1)
                pe.wait_ge(xt_ready, g + 1)
            relu_of(pe, group, n - 3)
            nc.tensor.matmul(ps_h[n % 3][:, :], w1[:, e, half * P:(half + 1) * P], xt[:, u, :], start=True, stop=True).then_inc(h_psum, 1)

        def relu_of(eng, group, n):
            g = group.g
            if n < 0:
                if isinstance(g, int) and g == 0:
                    return
                n, g = n + UNITS, g - 1
            eng.wait_ge((hid_act, hid_dve)[n % 2], g * (UNITS // 2) + (n // 2 + 1))

        def pe_out(pe, group, n):
            g, u = group.g, group.odd
            e, half = n // 2, n % 2
            if n == 0:
                after(pe, end.sem, (g - 2) * end.per + end.per)
                for t in range(TILES):
                    nc.tensor.matmul(ps_y[u][:, t * C:(t + 1) * C], xt[:, u, t * P:(t + 1) * P], b2[:, :],
                                     start=(t == 0), stop=False, skip_group_check=True)
            relu_of(pe, group, n)
            for t in range(TILES):
                i = nc.tensor.matmul(ps_y[u][:, t * C:(t + 1) * C], hid[:, n % 3, t * P:(t + 1) * P], w2[:, e, half, :],
                                     start=False, stop=(n == UNITS - 1), skip_group_check=True)
            i.then_inc(hid_used, 1)

        def relu(eng, group, n):
            g = group.g
            eng.wait_ge(h_psum, g * UNITS + (n + 1))
            after(eng, hid_used, g * UNITS + (n - 2))
            if n % 2 == 0:
                nc.scalar.activation(hid[:, n % 3, :], ps_h[n % 3][:, :], ACT.Relu).then_inc(hid_act, 1)
            else:
                nc.vector.tensor_scalar(hid[:, n % 3, :], ps_h[n % 3][:, :], 0.0, None, ALU.max).then_inc(hid_dve, 1)

        def act_xt(act, group):
            act.wait_ge(xt_psum, group.g + 1)
            after(act, hid_used, group.g * UNITS - UNITS)
            nc.scalar.copy(xt[0:C, group.odd, :], ps_t[0:C, :]).then_inc(xt_ready, 1)

        def act_exp(act, group):
            act.wait_ge(pick.sem, group.g * pick.per + 2)
            nc.scalar.activation(ez[:, :, :], z[:, :, :], ACT.Exp).then_inc(ez_ready, 1)

        def act_choice(act, group):
            act.wait_ge(choice_psum, group.g + 1)
            nc.scalar.copy(xt[C:C + E, group.odd, :], ps_choice[0:E, :]).then_inc(choice_ready, 1)

        tt, ts, red = nc.vector.tensor_tensor, nc.vector.tensor_scalar, nc.vector.tensor_reduce

        def dve_norm(dve, group):
            u, g, c = group.odd, group.g, ln
            c.start(g)
            dve.wait_ge(x_in[u], group.half * 16 + 16)
            c.did(red(s[:, :], xg[:, u, :, :], AX.X, ALU.add))
            c.wait(dve)
            c.did(ts(m[:, :], s[:, :], 1.0 / C, None, ALU.mult))
            c.wait(dve)
            c.did(tt(xc[:, :, :], xg[:, u, :, :], on_tiles(m[:, :], C), ALU.subtract))
            c.wait(dve)
            c.did(tt(sq[:, :, :], xc[:, :, :], xc[:, :, :], ALU.mult))
            c.wait(dve)
            c.did(red(ss[:, :], sq[:, :, :], AX.X, ALU.add))
            c.wait(dve)
            c.did(ts(var[:, :], ss[:, :], 1.0 / C, EPS, ALU.mult, ALU.add))
            dve.wait_ge(rstd_ready, g + 1)
            after(dve, xt_psum, g)
            c.did(tt(xn[:, :, :], xc[:, :, :], on_tiles(rstd[:, :], C), ALU.mult))
            c.end()

        def dve_choose(dve, group):
            g, c = group.g, pick
            c.start(g)
            dve.wait_ge(logit_psum, g + 1)
            c.did(red(top[:, :], ps_logit, AX.X, ALU.max))
            c.wait(dve)
            c.did(tt(z[:, :, :], ps_logit, on_tiles(top[:, :], E), ALU.subtract))
            c.wait(dve)
            c.did(ts(eq[:, :, :], z[:, :, :], 0.0, None, ALU.is_equal))
            c.wait(dve)
            c.did(tt(eq[:, :, :], eq[:, :, :], rank[:, :, :], ALU.mult))
            c.wait(dve)
            c.did(red(first[:, :], eq[:, :, :], AX.X, ALU.max))
            c.wait(dve)
            after(dve, count_psum, g)
            c.did(tt(choice[:, :, :], eq[:, :, :], on_tiles(first[:, :], E), ALU.is_equal))
            dve.wait_ge(ez_ready, g + 1)
            c.did(red(total[:, :], ez[:, :, :], AX.X, ALU.add))
            c.wait(dve)
            c.did(nc.vector.reciprocal(share[:, :], total[:, :]))

        def dve_count(dve, group):
            g, c = group.g, pick
            c.start(g)
            c.n = 8
            dve.wait_ge(count_psum, g + 1)
            for t in range(TILES):
                c.did(tt(before[:, t + 1, :], before[:, t, :], ps_tot[:, t, :], ALU.add))
                c.wait(dve)
            c.did(tt(place[:, :, :], before[:, 0:TILES, :], ps_cum, ALU.add))
            c.wait(dve)
            c.did(tt(place[:, :, :], place[:, :, :], choice[:, :, :], ALU.mult))
            c.wait(dve)
            c.did(red(pos[:, :], place[:, :, :], AX.X, ALU.add))
            c.wait(dve)
            c.did(nc.vector.scalar_tensor_tensor(out=weight[:, group.odd, :], in0=pos[:, :], scalar=float(CAPACITY),
                                                 in1=share[:, :], op0=ALU.is_le, op1=ALU.mult))
            c.did(nc.vector.tensor_copy(before[:, 0, :], before[:, TILES, :]))
            c.end()

        def dve_end(dve, group):
            g, u, c = group.g, group.odd, end
            c.start(g)
            dve.wait_ge(hid_used, g * UNITS + UNITS)
            dve.wait_ge(pick.sem, g * pick.per + pick.per)
            c.did(tt(y[:, :, :], ps_y[u][:, 0:TILES * C].rearrange("p (t c) -> p t c", t=TILES),
                     on_tiles(weight[:, u, :], C), ALU.mult))
            c.wait(dve)
            c.did(ts(over[:, :, :], y[:, :, :], HUGE, CLIP, ALU.is_gt, ALU.mult))
            c.did(ts(under[:, :, :], y[:, :, :], -HUGE, -CLIP, ALU.is_lt, ALU.mult))
            c.did(ts(finite[:, :, :], y[:, :, :], 0.0, 0.0, ALU.mult, ALU.is_equal))
            c.wait(dve)
            c.did(tt(over[:, :, :], over[:, :, :], under[:, :, :], ALU.add))
            c.wait(dve)
            settle(dve)
            c.did(nc.vector.copy_predicated(over[:, :, :], finite[:, :, :], y[:, :, :]))
            c.wait(dve)
            after(dve, stored[u], group.half * 16)
            dve.wait_ge(xr_ready, g + 1)
            c.did(tt(res[:, u, :, :], over[:, :, :], xr[:, u, :, :], ALU.add))
            c.end()

        def pool_rstd(pool, group):
            u = group.odd
            pool.wait_ge(ln.sem, group.g * ln.per + 6)
            nc.gpsimd.tensor_tensor(rstd[:, :], var[:, :], neghalf[:, :], ALU.pow).then_inc(rstd_ready, 1)
            pool.wait_ge(x_in[u], group.half * 16 + 16)
            after(pool, end.sem, (group.g - 2) * end.per + end.per)
            settle(pool)
            nc.gpsimd.tensor_copy(xr[:, u, :, :], xg[:, u, :, :]).then_inc(xr_ready, 1)

        def steps(eng, step, a_only, c_only):
            f = Group(0, 0)
            a_only(eng, f)
            step(eng, f, True, False)
            with eng.Fori(0, SETS // 2 - 1) as i:
                step(eng, Group(i, 1), True, True)
                step(eng, Group(i + 1, 0), True, True)
            last = Group(SETS // 2 - 1, 1)
            step(eng, last, False, True)
            c_only(eng, last)

        with nc.Block() as block:
            @block.sync
            def _(sp):
                def step(sp, group, a, c):
                    if a:
                        sync_load(sp, group.next())
                    if c:
                        sync_store(sp, group.prev())
                steps(sp, step, sync_load, sync_store)
                for u in range(2):
                    sp.wait_ge(stored[u], SETS // 2 * 16)

            @block.tensor
            def _(pe):
                def a_only(pe, group):
                    pe_xt(pe, group)
                    pe_logits(pe, group)
                    pe_choice(pe, group)

                def step(pe, group, a, c):
                    pe_hidden(pe, group, 0)
                    pe_hidden(pe, group, 1)
                    for n in range(UNITS):
                        if n + 2 < UNITS:
                            pe_hidden(pe, group, n + 2)
                        pe_out(pe, group, n)
                        if a and n == 3:
                            pe_xt(pe, group.next())
                        if a and n == 6:
                            pe_logits(pe, group.next())
                        if a and n == 10:
                            pe_choice(pe, group.next())
                steps(pe, step, a_only, lambda pe, group: None)

            @block.scalar
            def _(act):
                def a_only(act, group):
                    act_xt(act, group)
                    act_exp(act, group)
                    act_choice(act, group)

                def step(act, group, a, c):
                    for n in range(0, UNITS, 2):
                        relu(act, group, n)
                        if a and n == 4:
                            act_xt(act, group.next())
                        if a and n == 8:
                            act_exp(act, group.next())
                        if a and n == 12:
                            act_choice(act, group.next())
                steps(act, step, a_only, lambda act, group: None)

            @block.vector
            def _(dve):
                def a_only(dve, group):
                    dve_norm(dve, group)
                    dve_choose(dve, group)
                    dve_count(dve, group)

                def step(dve, group, a, c):
                    for n in range(1, UNITS, 2):
                        relu(dve, group, n)
                        if a and n == 1:
                            dve_norm(dve, group.next())
                        if c and n == 5:
                            dve_end(dve, group.prev())
                        if a and n == 7:
                            dve_choose(dve, group.next())
                        if a and n == 13:
                            dve_count(dve, group.next())
                steps(dve, step, a_only, dve_end)

            @block.gpsimd
            def _(pool):
                steps(pool, lambda pool, group, a, c: pool_rstd(pool, group.next()) if a else None,
                      pool_rstd, lambda pool, group: None)


def shift_windows(nc, src, dst):
    old = src.rearrange("(b h) w (r c) d -> b h w r (c d)", b=B, r=WS)
    upper = dst[0:UNCUT].rearrange("(b h) w (r c) d -> b h w r (c d)", b=B, r=WS)
    lower = dst[UNCUT:GROUPS].rearrange("b w (r c) d -> b w r (c d)", r=WS)
    left, right = slice(0, KEEP * C), slice(KEEP * C, WS * C)
    old_left, old_right = slice(SHIFT * C, WS * C), slice(0, SHIFT * C)
    last = NW - 1

    def image(b):
        o, up, lo = (a[bass.ds(b, 1)].rearrange(f"z {s} -> (z {t}) {u}") for a, s, t, u in (
            (old, "h w r x", "h", "w r x"), (upper, "h w r x", "h", "w r x"), (lower, "w r x", "w", "r x")))
        moves = []
        for rows, old_rows, down in ((slice(0, KEEP), slice(SHIFT, WS), 0), (slice(KEEP, WS), slice(0, SHIFT), 1)):
            h, h_last = slice(down, last + down), last if not down else 0
            moves += [(up[:, :, rows, left].rearrange("h w r x -> (h w) r x"),
                       o[h, :, old_rows, old_left].rearrange("h w r x -> (h w) r x")),
                      (up[:, last, rows, right], o[h, 0, old_rows, old_right]),
                      (lo[:, rows, left], o[h_last, :, old_rows, old_left]),
                      (lo[0:last, rows, right], o[h_last, 1:NW, old_rows, old_right]),
                      (lo[last, rows, right], o[h_last, 0, old_rows, old_right])]
            moves += [(up[:, 0:last, rows.start + r, right], o[h, 1:NW, old_rows.start + r, old_right])
                      for r in range(rows.stop - rows.start)]
        return moves

    move_images(nc, "shift", image)


def unshift_windows(nc, src, dst):
    img = dst.rearrange("b (i j) c -> b i (j c)", i=SIDE)
    upper = src[0:UNCUT].rearrange("(b h) w (r c) d -> b h w r (c d)", b=B, r=WS)
    lower = src[UNCUT:GROUPS].rearrange("b w (r c) d -> b w r (c d)", r=WS)
    left, right = slice(0, KEEP * C), slice(KEEP * C, WS * C)
    last = NW - 1
    inner = slice(SHIFT, SIDE - KEEP)
    edge = slice((SIDE - KEEP) * C, SIDE * C)
    wrapped = slice(0, SHIFT * C)

    def image(b):
        im, up, lo = (a[bass.ds(b, 1)].rearrange(f"z {s} -> (z {t}) {u}") for a, s, t, u in (
            (img, "i x", "i", "x"), (upper, "h w r x", "h", "w r x"), (lower, "w r x", "w", "r x")))
        mid = im[inner].rearrange("(h r) x -> h r x", r=WS)
        moves = [(mid[:, :, edge], up[:, last, :, left]), (mid[:, :, wrapped], up[:, last, :, right])]
        moves += [(mid[:, r, SHIFT * C:(SIDE - KEEP) * C].rearrange("h (w x) -> h w x", w=last), up[:, 0:last, r, :])
                  for r in range(WS)]
        for rows, at in ((slice(0, KEEP), slice(SIDE - KEEP, SIDE)), (slice(KEEP, WS), slice(0, SHIFT))):
            moves += [(im[at, SHIFT * C:(SIDE - KEEP) * C].rearrange("r (w x) -> r w x", w=last),
                       lo[0:last, rows, :].rearrange("w r x -> r w x")),
                      (im[at, edge], lo[last, rows, left]), (im[at, wrapped], lo[last, rows, right])]
        return moves

    move_images(nc, "unshift", image)


def move_images(nc, name, image):
    with nc.semaphore(name + "_0") as s0, nc.semaphore(name + "_1") as s1, nc.Block() as block:
        def half(eng, sem, first):
            with eng.Fori(first, first + B // 2) as b:
                moves = image(b)
                for out, in_ in moves:
                    eng.dma_start(out, in_).then_inc(sem, 16)
            eng.wait_ge(sem, B // 2 * len(moves) * 16)

        @block.sync
        def _(sp):
            half(sp, s0, 0)

        @block.scalar
        def _(act):
            half(act, s1, B // 2)


def vit_tower(nc, V, out):
    def dram(name, shape):
        return nc.dram_tensor(name, shape, F32, kind="Internal").ap()

    windows = [GROUPS, NW, N, C]
    first, shifted, second = dram("first", windows), dram("shifted_in", windows), dram("second", windows)
    x = dram("x_tokens", [B, T, C])
    swin_block(nc, 0, V, V["patches"], first)
    shift_windows(nc, first, shifted)
    swin_block(nc, 1, V, shifted, second)
    unshift_windows(nc, second, x)
    fast_weights(nc, V, x, dram("rows_kept", [B, CH, QKV3]))
    experts(nc, V, x, out)


def kernel(**inputs):
    import numpy as np
    import concourse.bacc as bacc
    from concourse.bass_utils import run_bass_kernel_spmd

    a = {n: np.asarray(v) for n, v in inputs.items()}
    tok = {n[7:]: v for n, v in a.items() if n.startswith("L0_tok_")}
    att = {n[8:]: v for n, v in a.items() if n.startswith("L0_attn_")}
    ffn = {n[7:]: v for n, v in a.items() if n.startswith("L0_ffn_")}
    px = a["x"].reshape(B, NW, WS, 4, NW, WS, 4).transpose(3, 6, 0, 1, 4, 2, 5).reshape(PIX, GROUPS, NW, N)
    part = np.zeros((SIDE, SIDE), np.int32)
    cuts = (slice(0, -WS), slice(-WS, -SHIFT), slice(-SHIFT, None))
    for i, rows in enumerate(cuts):
        for j, cols in enumerate(cuts):
            part[rows, cols] = 3 * i + j
    part = part.reshape(NW, WS, NW, WS).transpose(0, 2, 1, 3).reshape(NW, NW, N)
    masks = np.stack([np.where(part[w][:, None] != part[w][None, :], np.float32(-100), np.float32(0))[::-1]
                      for w in ((0, NW - 1), (NW - 1, 0), (NW - 1, NW - 1))])
    arrays = {
        "patches": px, "masks": masks, "pe_t": tok["pe_w"].reshape(C, PIX).T,
        "qkv_t": tok["qkv_w"].transpose(0, 2, 1), "proj_t": tok["proj_w"].transpose(0, 2, 1),
        "w1_t": tok["w1"].transpose(0, 2, 1), "w2_t": tok["w2"].transpose(0, 2, 1),
        "rpb_t": tok["rpb"].transpose(0, 2, 1)[:, :, ::-1],
        "w_fused_t": att["W_fused"].T, "W0_t": att["W0"].T, "P0_t": att["P0"].T, "W1": att["W1"], "P1": att["P1"],
        "gate_w": ffn["gate_w"], "gate_b": ffn["gate_b"], "moe_w1": ffn["w1"], "moe_b1": ffn["b1"],
        "moe_w2": ffn["w2"], "moe_b2": ffn["b2"],
    }
    for n in ("pe_b", "pe_ng", "pe_nb", "n1g", "n1b", "qkv_b", "proj_b", "n2g", "n2b", "b1", "b2"):
        arrays[n] = tok[n]
    arrays = {n: np.ascontiguousarray(v) for n, v in arrays.items()}
    nc = bacc.Bacc("TRN2", target_bir_lowering=False, num_devices=1)
    V = {n: nc.dram_tensor("in_" + n, v.shape, mybir.dt.from_np(v.dtype), kind="ExternalInput").ap()
         for n, v in arrays.items()}
    out = nc.dram_tensor("out", (B, T, C), F32, kind="ExternalOutput").ap()
    vit_tower(nc, V, out)
    r = run_bass_kernel_spmd(nc, [{"in_" + n: v for n, v in arrays.items()}], core_ids=[0])
    return r.results[0]["out"]
```

```python
from contextlib import ExitStack

import concourse.bass as bass
from concourse import mybir

F32 = mybir.dt.float32
I32 = mybir.dt.int32
ALU = mybir.AluOpType
ACT = mybir.ActivationFunctionType
AX = mybir.AxisListType

B = 16
C = 64
WS = 7
NW = 8
N = WS * WS
SIDE = NW * WS
NH = 8
HD = C // NH
SHIFT = WS // 2
KEEP = WS - SHIFT
PAIRS = NW // 2
HALF = 64
P = 128
GROUPS = B * NW
UNCUT = B * (NW - 1)
KEYS = NH * N
HV = HD + 1
F = 4 * C
EPS = 1e-5
PIX = 16

T = SIDE * SIDE
CH = 16
CHUNKS = T // CH
QKV3 = 3 * C + 3
FS = P // B
FI = F // FS
LR = 0.1
L2_LIMIT = 1e12
TOKENS = B * T
TILES = 4
SIZE = TILES * P
SETS = TOKENS // SIZE
E = 8
CAPACITY = -(-5 * TOKENS // (4 * E))
K1 = C + E + 1
OFF = -1e18
HUGE = 3.4028234663852886e38
CLIP = 1e4

class Steps:

    def __init__(self, sem, per):
        self.sem, self.per, self.base, self.n = sem, per, 0, 0

    def start(self, group, done=0):
        self.base, self.n = group * self.per, done

    def did(self, instruction):
        instruction.then_inc(self.sem, 1)
        self.n += 1

    def wait(self, engine):
        engine.wait_ge(self.sem, self.base + self.n)

    def end(self):
        assert self.n == self.per, (self.n, self.per)


class Group:

    def __init__(self, half, odd):
        self.half, self.odd, self.g = half, odd, half * 2 + odd

    def on(self, by):
        return Group(self.half + (self.odd + by) // 2, (self.odd + by) % 2)

    def next(self):
        return self.on(1)

    def prev(self):
        return self.on(-1)


def after(engine, sem, value):
    if not isinstance(value, int) or value > 0:
        engine.wait_ge(sem, value)


def settle(engine):
    engine.nop(nofuse=True)


def ones_row(ap):
    return ap[C:C + 1]


def tokens(ap, half):
    return ap.rearrange("(p w) t c -> w t p c", w=2)[half]


def swin_block(nc, k, V, src, dst):
    with ExitStack() as ctx:
        def sb(name, shape, dt=F32):
            return ctx.enter_context(nc.sbuf_tensor(f"{name}_{k}", shape, dt))

        def sem(name):
            return ctx.enter_context(nc.semaphore(f"{name}_{k}"))

        banks = [ctx.enter_context(nc.psum_tensor(f"bank{i}_{k}", [P, 512], F32)) for i in range(8)]
        ps_a, ps_pt1, ps_c, ps_d, ps_s0, ps_s1, ps_pt0, ps_o = banks
        ps_s, ps_pt = [ps_s0, ps_s1], [ps_pt0, ps_pt1]

        w_qkv = sb("w_qkv", [P, 3 * C])
        w_proj = sb("w_proj", [P, C])
        w_up = sb("w_up", [P, F])
        w_down = sb("w_down", [P, 2, C])
        b_down = sb("b_down", [P, C])
        norm_g = sb("norm_g", [C, 2])
        norm_b = sb("norm_b", [C, 2])
        folded = sb("folded", [1, 3 * C + F])
        bias_in = sb("bias_in", [1, 3 * C + F])
        ident = sb("ident", [P, P])
        neghalf = sb("neghalf", [P, PAIRS])
        head_mask = sb("head_mask", [C, NH])
        masks = sb("masks", [HALF + N, 3, N])
        w_pe = sb("w_pe", [PIX + 1, C])
        pe_gain = sb("pe_gain", [P, C])
        pe_shift = sb("pe_shift", [P, C])
        patches = sb("patches", [PIX + 1, 2, NW, HALF]) if k == 0 else None
        xa = sb("xa", [P, 2, PAIRS, C])
        xr = sb("xr", [P, 2, PAIRS, C])
        xt = sb("xt", [P, 512])
        kt = sb("kt", [C, 512])
        q_rows = sb("q_rows", [P, 2, NW, HALF])
        k_rows = sb("k_rows", [P, 2, NW, NH, N])
        low_k_rows = sb("low_k_rows", [P, 2, NW, NH, N]) if k else None
        v_blk = sb("v_blk", [P, 2, NW, NH // 2, 2 * HV])
        probs = sb("probs", [P, 2, NH, HALF])
        probs_t = sb("probs_t", [P, 2, NH // 2, P])
        row_max = sb("row_max", [P, 2, NH])
        rec = sb("rec", [P, PAIRS * NH])
        oa = sb("oa", [P, PAIRS, C])
        ot = sb("ot", [P, 512])
        x1 = sb("x1", [P, 2, PAIRS, C])
        x1b = sb("x1b", [P, 2, PAIRS, C])
        xt2 = sb("xt2", [P, 512])
        hid = sb("hid", [P, 2, 512])
        xo = sb("xo", [P, 2, PAIRS, C])
        norms = {}
        for name in ("pe", "ln1", "ln2"):
            norms[name] = dict(
                xc=sb(f"{name}_xc", [P, PAIRS, C]), sq=sb(f"{name}_sq", [P, PAIRS, C]),
                xn=sb(f"{name}_xn", [P, PAIRS, C]), s=sb(f"{name}_s", [P, PAIRS]),
                m=sb(f"{name}_m", [P, PAIRS]), ss=sb(f"{name}_ss", [P, PAIRS]),
                var=sb(f"{name}_var", [P, PAIRS]), rstd=sb(f"{name}_rstd", [P, PAIRS]),
                chain=Steps(sem(f"{name}_chain"), 9 if name == "pe" else 7), rstd_ready=sem(f"{name}_rstd"))

        loaded, zeroed = sem("loaded"), sem("zeroed")
        prep = sem("prep")
        prep_pe = sem("prep_pe")
        prep_act = sem("prep_act")
        row_moved = sem("row_moved")
        x_in = [sem("x_in0"), sem("x_in1")]
        xp_psum = sem("xp_psum")
        xr_ready, xt_psum, xt_ready = sem("xr_ready"), sem("xt_psum"), sem("xt_ready")
        qk_psum, qk_ready, v_psum = sem("qk_psum"), sem("qk_ready"), sem("v_psum")
        v_ready, k_ready = sem("v_ready"), sem("k_ready")
        s_psum, max_ready, shifted, exp_ready = sem("s_psum"), sem("max_ready"), sem("shifted"), sem("exp_ready")
        p_psum, pt_ready, pv_done = sem("p_psum"), sem("pt_ready"), sem("pv_done")
        rec_ready, oa_ready, ot_psum, ot_ready = sem("rec_ready"), sem("oa_ready"), sem("ot_psum"), sem("ot_ready")
        proj_psum, x1_ready, t2_psum, xt2_ready = sem("proj_psum"), sem("x1_ready"), sem("t2_psum"), sem("xt2_ready")
        h_psum, h_ready, y_psum, out_ready = sem("h_psum"), sem("h_ready"), sem("y_psum"), sem("out_ready")
        x1b_ready = sem("x1b_ready")
        stored = [sem("stored0"), sem("stored1")]
        bias_set = sem("bias_set")

        pe_fold = sem("pe_fold")

        def fill_bias():
            first = k_rows[HALF:HALF + N, 0, 0, :, :]
            for u in range(2):
                for w in range(NW):
                    for low, rows in enumerate((k_rows, low_k_rows)[:k + 1]):
                        kind = 2 * low + (w == NW - 1)
                        out = rows[HALF:HALF + N, u, w, :, :]
                        if k and kind:
                            m = masks[HALF:HALF + N, kind - 1, :].unsqueeze(1).broadcast_to([N, NH, N])
                            nc.vector.tensor_tensor(out, first, m, ALU.add)
                        elif (u, w) != (0, 0):
                            nc.vector.tensor_copy(out, first)

        with nc.Block() as block:
            n_loads = 12 if k else 15

            @block.sync
            def _(sp):
                def load(out, in_):
                    sp.dma_start(out, in_).then_inc(loaded, 16)
                sp.wait_ge(zeroed, 3)
                load(w_qkv[0:C, :], V["qkv_t"][k])
                load(w_proj[0:C, :], V["proj_t"][k])
                load(w_proj[C:C + 1, :], V["proj_b"][k:k + 1, :])
                load(w_up[0:C, :], V["w1_t"][k])
                load(w_down[:, :, :], V["w2_t"][k].rearrange("(f p) c -> p f c", p=P))
                load(b_down[:, :], V["b2"][k:k + 1, :].broadcast_to([P, C]))
                load(bias_in[:, 0:3 * C], V["qkv_b"][k:k + 1, :])
                load(bias_in[:, 3 * C:], V["b1"][k:k + 1, :])
                with nc.allow_non_contiguous_dma(reason="a column of 64"):
                    load(norm_g[:, 0:1], V["n1g"][k:k + 1, :].rearrange("a c -> c a"))
                    load(norm_g[:, 1:2], V["n2g"][k:k + 1, :].rearrange("a c -> c a"))
                    load(norm_b[:, 0:1], V["n1b"][k:k + 1, :].rearrange("a c -> c a"))
                    load(norm_b[:, 1:2], V["n2b"][k:k + 1, :].rearrange("a c -> c a"))
                if k == 0:
                    load(w_pe[0:PIX, :], V["pe_t"][:, :])
                    load(w_pe[PIX:PIX + 1, :], V["pe_b"].rearrange("(a c) -> a c", a=1))
                    load(pe_gain[:, :], V["pe_ng"].rearrange("(a c) -> a c", a=1).broadcast_to([P, C]))
                    sp.dma_start(pe_shift[:, :], V["pe_nb"].rearrange("(a c) -> a c", a=1).broadcast_to([P, C])).then_inc(loaded, 16)
                sp.wait_ge(prep_act, 1)
                for w in range(1):
                    for rq in range(WS):
                        for h in range(NH):
                            base = V["rpb_t"][k, h, :]
                            row0 = HALF + rq * WS
                            src_ap = bass.AP(tensor=base.tensor, offset=base.offset + 13 * rq,
                                             ap=[[1, WS], [13, WS], [1, WS]])
                            sp.dma_start(k_rows[row0:row0 + WS, 0, 0, h, :].rearrange("p (a b) -> p a b", a=WS),
                                         src_ap).then_inc(bias_set, 16)
                if k == 1:
                    sp.dma_start(masks[HALF:HALF + N, :, :], V["masks"].rearrange("m q k -> q m k")).then_inc(bias_set, 16)
                sp.wait_ge(prep, 8)
                sp.dma_start(ones_row(w_qkv), folded[:, 0:3 * C]).then_inc(row_moved, 16)
                sp.dma_start(ones_row(w_up), folded[:, 3 * C:]).then_inc(row_moved, 16)

            @block.gpsimd
            def _(pool):
                nc.gpsimd.memset(ident[:, :], 0.0).then_inc(prep_pe, 1)
                nc.gpsimd.memset(q_rows[:, :, :, :], 0.0).then_inc(prep_pe, 1)
                nc.gpsimd.memset(neghalf[:, :], -0.5).then_inc(prep_pe, 1)
                nc.gpsimd.memset(head_mask[:, :], 1.0).then_inc(prep_pe, 1)
                pool.wait_ge(prep_pe, 4)
                nc.gpsimd.affine_select(out=ident[:, :], in_=ident[:, :], compare_op=ALU.not_equal, fill=1.0,
                                        base=0, pattern=[[-1, P]], channel_multiplier=1).then_inc(prep_pe, 1)
                nc.gpsimd.affine_select(out=head_mask[:, :], in_=head_mask[:, :], compare_op=ALU.is_ge, fill=0.0,
                                        base=0, pattern=[[-HD, NH]], channel_multiplier=1).then_inc(prep_pe, 1)
                pool.wait_ge(prep_pe, 6)
                nc.gpsimd.affine_select(out=head_mask[:, :], in_=head_mask[:, :], compare_op=ALU.is_ge, fill=0.0,
                                        base=HD - 1, pattern=[[HD, NH]], channel_multiplier=-1).then_inc(prep_pe, 1)
                q2 = q_rows[HALF:P, :, :, :].rearrange("p u w q -> p (u w) q")
                nc.gpsimd.affine_select(out=q2, in_=q2, compare_op=ALU.not_equal, fill=1.0, base=-(N - 1),
                                        pattern=[[0, 2 * NW], [1, HALF]], channel_multiplier=1).then_inc(prep_pe, 1)

            @block.vector
            def _(dve):
                for t in (w_qkv, w_proj, w_up):
                    nc.vector.memset(t[:, :], 0.0).then_inc(zeroed, 1)
                nc.vector.memset(k_rows[:, :, :, :, :], 0.0).then_inc(prep_act, 1)
                if k:
                    nc.vector.memset(low_k_rows[:, :, :, :, :], 0.0).then_inc(prep_act, 1)
                    dve.wait_ge(prep_act, 2)
                nc.vector.memset(v_blk[0:HALF, :, :, :, :], 0.0).then_inc(prep, 1)
                nc.vector.memset(v_blk[HALF:P, :, :, :, :], 0.0).then_inc(prep, 1)
                nc.vector.memset(probs[:, :, :, :], 0.0)
                nc.vector.memset(xa[:, :, :, :], 0.0)
                for t in (xt, ot, xt2):
                    nc.vector.memset(t[C:P, :], 1.0)
                if k == 0:
                    nc.vector.memset(patches[:, :, :, :], 0.0).then_inc(prep, 1)
                    dve.wait_ge(prep, 3)
                    nc.vector.memset(patches[:, :, :, :], 1.0).then_inc(prep, 1)
                    dve.wait_ge(prep, 4)
                    nc.vector.memset(patches[0:PIX, :, :, :], 0.0)
                else:
                    nc.vector.memset(masks[0:HALF, :, :], 0.0).then_inc(prep, 1)
                    nc.vector.memset(rec[:, :], 0.0).then_inc(prep, 1)
                dve.wait_ge(prep, 4)
                nc.vector.memset(v_blk[0:HALF, :, :, :, HD:HD + 1], 1.0)
                nc.vector.memset(v_blk[HALF:P, :, :, :, HV + HD:HV + HD + 1], 1.0)
                dve.wait_ge(loaded, 16 * (16 if k == 0 else 12))
                dve.wait_ge(pe_fold, 1)
                nc.vector.tensor_tensor(folded[:, 0:3 * C], ps_a[0:1, 0:3 * C], bias_in[:, 0:3 * C], ALU.add).then_inc(prep, 1)
                nc.vector.tensor_tensor(folded[:, 3 * C:], ps_c[0:1, 0:F], bias_in[:, 3 * C:], ALU.add).then_inc(prep, 1)
                nc.vector.tensor_scalar(w_qkv[0:C, :], w_qkv[0:C, :], norm_g[:, 0:1], None, ALU.mult).then_inc(prep, 1)
                nc.vector.tensor_scalar(w_up[0:C, :], w_up[0:C, :], norm_g[:, 1:2], None, ALU.mult).then_inc(prep, 1)
                dve.wait_ge(prep, 8)
                dve.wait_ge(row_moved, 32)
                nc.vector.tensor_scalar(w_qkv[:, 0:C], w_qkv[:, 0:C], float(HD) ** -0.5, None, ALU.mult)
                dve.wait_ge(bias_set, 16 * (WS * NH + (k == 1)))
                fill_bias()

            @block.tensor
            def _(pe):
                pe.wait_ge(loaded, 16 * (16 if k == 0 else 12))
                nc.tensor.matmul(ps_a[0:1, 0:3 * C], norm_b[:, 0:1], w_qkv[0:C, :], start=True, stop=True)
                nc.tensor.matmul(ps_c[0:1, 0:F], norm_b[:, 1:2], w_up[0:C, :], start=True, stop=True).then_inc(pe_fold, 1)

        def norm_stats(eng, name, group, x):
            T = norms[name]
            c = T["chain"]
            c.start(group.g)
            c.did(nc.vector.tensor_reduce(T["s"][:, :], x, AX.X, ALU.add))
            c.wait(eng)
            c.did(nc.vector.tensor_scalar(T["m"][:, :], T["s"][:, :], 1.0 / C, None, ALU.mult))
            c.wait(eng)
            c.did(nc.vector.tensor_tensor(T["xc"][:, :, :], x, T["m"][:, :].unsqueeze(2).broadcast_to([P, PAIRS, C]), ALU.subtract))
            c.wait(eng)
            c.did(nc.vector.tensor_tensor(T["sq"][:, :, :], T["xc"][:, :, :], T["xc"][:, :, :], ALU.mult))
            c.wait(eng)
            c.did(nc.vector.tensor_reduce(T["ss"][:, :], T["sq"][:, :, :], AX.X, ALU.add))
            c.wait(eng)
            c.did(nc.vector.tensor_scalar(T["var"][:, :], T["ss"][:, :], 1.0 / C, EPS, ALU.mult, ALU.add))

        def norm_apply(eng, name, group, affine=False):
            T = norms[name]
            c = T["chain"]
            c.start(group.g, 6)
            eng.wait_ge(T["rstd_ready"], group.g + 1)
            out = T["xn"][:, :, :]
            c.did(nc.vector.tensor_tensor(out, T["xc"][:, :, :], T["rstd"][:, :].unsqueeze(2).broadcast_to([P, PAIRS, C]), ALU.mult))
            if affine:
                c.wait(eng)
                c.did(nc.vector.tensor_tensor(out, out, pe_gain[:, :].unsqueeze(1).broadcast_to([P, PAIRS, C]), ALU.mult))
                c.wait(eng)
                after(eng, xr_ready, group.g - 1)
                after(eng, norms["ln1"]["chain"].sem, (group.g - 2) * LN_N + 3)
                c.did(nc.vector.tensor_tensor(xa[:, group.odd, :, :], out, pe_shift[:, :].unsqueeze(1).broadcast_to([P, PAIRS, C]), ALU.add))
            c.end()

        def rsqrt(eng, name, g):
            T = norms[name]
            eng.wait_ge(T["chain"].sem, g * T["chain"].per + 6)
            nc.gpsimd.tensor_tensor(T["rstd"][:, :], T["var"][:, :], neghalf[:, :], ALU.pow).then_inc(T["rstd_ready"], 1)

        PE_N, LN_N = norms["pe"]["chain"].per, 7

        def x_present(eng, group):
            if k == 0:
                eng.wait_ge(norms["pe"]["chain"].sem, group.g * PE_N + PE_N)
            else:
                eng.wait_ge(x_in[group.odd], group.half * 32 + 32)

        def rows_of(group):
            return low_k_rows if k and group.low else k_rows

        def sync_load(sp, group):
            g, u = group.g, group.odd
            if k == 0:
                after(sp, xp_psum, g - 1)
                sp.dma_start(patches[0:PIX, u, :, 0:N],
                             src[:, bass.ds(g, 1), :, :].rearrange("x g w t -> x (g w) t")).then_inc(x_in[u], 16)
            else:
                after(sp, norms["ln1"]["chain"].sem, (g - 2) * LN_N + LN_N)
                settle(sp)
                after(sp, xr_ready, g - 1)
                for half in range(2):
                    sp.dma_start(xa[HALF * half:HALF * half + N, u, :, :],
                                 tokens(src[bass.ds(g, 1)].rearrange("g w t c -> (g w) t c"), half)).then_inc(x_in[u], 16)

        def sync_store(sp, group):
            g, u = group.g, group.odd
            sp.wait_ge(out_ready, g + 1)
            for half in range(2):
                sp.dma_start(tokens(dst[bass.ds(g, 1)].rearrange("g w t c -> (g w) t c"), half),
                             xo[HALF * half:HALF * half + N, u, :, :]).then_inc(stored[u], 16)

        def pe_patch(pe, group):
            g, u = group.g, group.odd
            pe.wait_ge(x_in[u], group.half * 16 + 16)
            after(pe, v_ready, g - 1)
            if isinstance(g, int) and g == 1:
                pe.wait_ge(norms["pe"]["chain"].sem, 3)
            for p in range(PAIRS):
                i = nc.tensor.matmul(ps_a[:, p * C:(p + 1) * C], patches[:, u, 2 * p:2 * p + 2, :], w_pe[:, :],
                                     start=True, stop=True)
            i.then_inc(xp_psum, 1)

        def pe_transpose(pe, out, x):
            settle(pe)
            for p in range(PAIRS):
                i = nc.tensor.transpose(out[0:C, p * P:(p + 1) * P], x[:, p, :], ident[:, :])
            return i

        def pe_xt(pe, group):
            g = group.g
            pe.wait_ge(norms["ln1"]["chain"].sem, g * LN_N + LN_N)
            after(pe, v_ready, g)
            if k == 0 and not (isinstance(g, int) and g + 1 >= GROUPS):
                pe.wait_ge(norms["pe"]["chain"].sem, (g + 1) * PE_N + 3)
            pe_transpose(pe, ps_a, norms["ln1"]["xn"]).then_inc(xt_psum, 1)

        def pe_qk(pe, group):
            pe.wait_ge(xt_ready, group.g + 1)
            nc.tensor.matmul(ps_a[:, :], w_qkv[:, 0:2 * C], xt[:, :], start=True, stop=True).then_inc(qk_psum, 1)

        def pe_v(pe, group):
            pe.wait_ge(qk_ready, group.g * 2 + 2)
            for p in range(PAIRS):
                i = nc.tensor.matmul(ps_a[:, p * C:(p + 1) * C], xt[:, p * P:(p + 1) * P], w_qkv[:, 2 * C:3 * C],
                                     start=True, stop=True)
            i.then_inc(v_psum, 1)

        def pe_scores(pe, group, p):
            g, u = group.g, group.odd
            if p == 0:
                pe.wait_ge(qk_ready, g * 2 + 2)
            if p % 2 == 0:
                pe.wait_ge(k_ready, g * 2 + (p // 2 + 1))
            after(pe, shifted, g * 4 + (p - 1))
            for half in range(2):
                w = 2 * p + half
                i = nc.tensor.matmul(ps_s[p % 2][HALF * half:HALF * half + HALF, 0:KEYS],
                                     q_rows[:, u, w, :],
                                     rows_of(group)[:, u, w, :, :].rearrange("p h n -> p (h n)"),
                                     start=True, stop=True)
            i.then_inc(s_psum, 1)

        def pe_probs_t(pe, group, p):
            g = group.g
            pe.wait_ge(exp_ready, g * 4 + (p + 1))
            after(pe, pt_ready, g * 4 + (p - 1))
            for hp in range(NH // 2):
                i = nc.tensor.transpose(ps_pt[p % 2][:, hp * P:(hp + 1) * P],
                                        probs[:, p % 2, 2 * hp:2 * hp + 2, :].rearrange("p a b -> p (a b)"), ident[:, :])
            i.then_inc(p_psum, 1)

        def pe_pv(pe, group, p):
            g, u = group.g, group.odd
            pe.wait_ge(pt_ready, g * 4 + (p + 1))
            if p == 0:
                pe.wait_ge(v_ready, g + 1)
                after(pe, oa_ready, g)
            for half in range(2):
                for hp in range(NH // 2):
                    at = (p * 4 + hp) * 2 * HV
                    i = nc.tensor.matmul(ps_o[HALF * half:HALF * half + HALF, at:at + 2 * HV],
                                         probs_t[:, p % 2, hp, HALF * half:HALF * half + HALF],
                                         v_blk[:, u, 2 * p + half, hp, :], start=True, stop=True)
            i.then_inc(pv_done, 1)

        def pe_ot(pe, group):
            g = group.g
            pe.wait_ge(oa_ready, g + 1)
            after(pe, h_ready, g * 2)
            pe_transpose(pe, ps_d, oa).then_inc(ot_psum, 1)

        def pe_proj(pe, group):
            g = group.g
            pe.wait_ge(ot_ready, g + 1)
            for p in range(PAIRS):
                i = nc.tensor.matmul(ps_d[:, p * C:(p + 1) * C], ot[:, p * P:(p + 1) * P], w_proj[:, :],
                                     start=True, stop=True)
            i.then_inc(proj_psum, 1)

        def pe_xt2(pe, group):
            pe.wait_ge(norms["ln2"]["chain"].sem, group.g * LN_N + LN_N)
            pe_transpose(pe, ps_d, norms["ln2"]["xn"]).then_inc(t2_psum, 1)

        def pe_up(pe, group):
            pe.wait_ge(xt2_ready, group.g + 1)
            after(pe, out_ready, group.g)
            for f, bank in enumerate((ps_c, ps_d)):
                nc.tensor.matmul(bank[:, :], w_up[:, f * P:(f + 1) * P], xt2[:, :], start=True, stop=True).then_inc(h_psum, 1)

        def pe_down(pe, group):
            pe.wait_ge(h_ready, group.g * 2 + 2)
            for p in range(PAIRS):
                out = ps_c[:, p * C:(p + 1) * C]
                for f in range(2):
                    i = nc.tensor.matmul(out, hid[:, f, p * P:(p + 1) * P], w_down[:, f, :], start=(f == 0),
                                         stop=(f == 1))
            i.then_inc(y_psum, 1)

        def act_xt(act, group):
            g = group.g
            act.wait_ge(xt_psum, g + 1)
            after(act, v_psum, g)
            nc.scalar.copy(xt[0:C, :], ps_a[0:C, :]).then_inc(xt_ready, 1)

        def act_qk(act, group):
            g, u = group.g, group.odd
            act.wait_ge(qk_psum, g + 1)
            after(act, s_psum, g * 4 - 4)
            nc.scalar.copy(q_rows[0:C, u, :, :].rearrange("p w q -> p (w q)"), ps_a[0:C, :]).then_inc(qk_ready, 1)
            after(act, k_ready, g * 2)
            nc.scalar.copy(kt[:, :], ps_a[C:2 * C, :]).then_inc(qk_ready, 1)

        def act_exp(act, group, p):
            act.wait_ge(shifted, group.g * 4 + (p + 1))
            nc.scalar.activation(probs[:, p % 2, :, 0:N], probs[:, p % 2, :, 0:N], ACT.Exp).then_inc(exp_ready, 1)

        def act_pt(act, group, p):
            g = group.g
            act.wait_ge(p_psum, g * 4 + (p + 1))
            after(act, pv_done, g * 4 + (p - 1))
            nc.scalar.copy(probs_t[:, p % 2, :, :].rearrange("p a b -> p (a b)"), ps_pt[p % 2][:, :]).then_inc(pt_ready, 1)

        def act_ot(act, group):
            g = group.g
            act.wait_ge(ot_psum, g + 1)
            after(act, proj_psum, g)
            nc.scalar.copy(ot[0:C, :], ps_d[0:C, :]).then_inc(ot_ready, 1)

        def act_xt2(act, group):
            g = group.g
            act.wait_ge(t2_psum, g + 1)
            after(act, h_psum, g * 2)
            nc.scalar.copy(xt2[0:C, :], ps_d[0:C, :]).then_inc(xt2_ready, 1)

        def act_gelu(act, group):
            g = group.g
            after(act, y_psum, g)
            for f, bank in enumerate((ps_c, ps_d)):
                act.wait_ge(h_psum, g * 2 + (f + 1))
                nc.scalar.activation(hid[:, f, :], bank[:, :], ACT.Gelu).then_inc(h_ready, 1)

        def dve_pe_stats(dve, group):
            dve.wait_ge(xp_psum, group.g + 1)
            norm_stats(dve, "pe", group, ps_a[:, 0:PAIRS * C].rearrange("p (a c) -> p a c", a=PAIRS))

        def dve_ln1_stats(dve, group):
            x_present(dve, group)
            norm_stats(dve, "ln1", group, xa[:, group.odd, :, :])

        def dve_ln1_apply(dve, group):
            after(dve, xt_psum, group.g)
            norm_apply(dve, "ln1", group)

        def dve_shift(dve, group, p):
            g = group.g
            dve.wait_ge(s_psum, g * 4 + (p + 1))
            s = ps_s[p % 2][:, 0:KEYS].rearrange("p (h n) -> p h n", h=NH)
            nc.vector.tensor_reduce(row_max[:, p % 2, :], s, AX.X, ALU.max).then_inc(max_ready, 1)
            after(dve, p_psum, g * 4 + (p - 1))
            dve.wait_ge(max_ready, g * 4 + (p + 1))
            nc.vector.tensor_tensor(probs[:, p % 2, :, 0:N], s, row_max[:, p % 2, :].unsqueeze(2).broadcast_to([P, NH, N]),
                                    ALU.subtract).then_inc(shifted, 1)

        def dve_v(dve, group):
            g, u = group.g, group.odd
            dve.wait_ge(v_psum, g + 1)
            after(dve, pv_done, g * 4 - 4)
            v = ps_a[:, 0:PAIRS * C].rearrange("p (a h d) -> p a h d", a=PAIRS, d=HD)
            blk = v_blk[:, u, :, :, :].rearrange("p (a w) h d -> p w a h d", w=2)
            for half in range(2):
                rows = v[HALF * half:HALF * half + HALF]
                nc.vector.tensor_copy(blk[0:HALF, half, :, :, 0:HD], rows[:, :, 0:NH:2, :])
                i = nc.vector.tensor_copy(blk[HALF:P, half, :, :, HV:HV + HD], rows[:, :, 1:NH:2, :])
            i.then_inc(v_ready, 1)

        def dve_oa(dve, group):
            g = group.g
            dve.wait_ge(pv_done, g * 4 + 4)
            o = ps_o[:, 0:PAIRS * NH * HV].rearrange("p (a v) -> p a v", v=HV)
            nc.vector.reciprocal(rec[:, :].unsqueeze(2), o[:, :, HD:HV]).then_inc(rec_ready, 1)
            dve.wait_ge(rec_ready, g + 1)
            after(dve, ot_psum, g)
            nc.vector.tensor_tensor(oa[:, :, :].rearrange("p a (h d) -> p (a h) d", d=HD), o[:, :, 0:HD],
                                    rec[:, :].unsqueeze(2).broadcast_to([P, PAIRS * NH, HD]), ALU.mult).then_inc(oa_ready, 1)

        def dve_x1(dve, group):
            g, u = group.g, group.odd
            dve.wait_ge(proj_psum, g + 1)
            dve.wait_ge(xr_ready, g + 1)
            after(dve, x1b_ready, g - 1)
            nc.vector.tensor_tensor(x1[:, u, :, :], xr[:, u, :, :], ps_d[:, 0:PAIRS * C].rearrange("p (a c) -> p a c", a=PAIRS),
                                    ALU.add).then_inc(x1_ready, 1)
            dve.wait_ge(x1_ready, g + 1)
            norm_stats(dve, "ln2", group, x1[:, u, :, :])

        def dve_ln2_apply(dve, group):
            after(dve, t2_psum, group.g)
            norm_apply(dve, "ln2", group)

        def dve_out(dve, group):
            g, u = group.g, group.odd
            dve.wait_ge(y_psum, g + 1)
            after(dve, stored[u], group.half * 32)
            dve.wait_ge(x1b_ready, g + 1)
            nc.vector.tensor_tensor(xo[:, u, :, :], x1b[:, u, :, :], ps_c[:, 0:PAIRS * C].rearrange("p (a c) -> p a c", a=PAIRS),
                                    ALU.add).then_inc(out_ready, 1)

        def pool_residual(pool, group):
            x_present(pool, group)
            after(pool, x1_ready, group.g - 1)
            settle(pool)
            nc.gpsimd.tensor_copy(xr[:, group.odd, :, :], xa[:, group.odd, :, :]).then_inc(xr_ready, 1)

        def pool_x1b(pool, group):
            g, u = group.g, group.odd
            pool.wait_ge(x1_ready, g + 1)
            after(pool, out_ready, g - 1)
            settle(pool)
            nc.gpsimd.tensor_tensor(x1b[:, u, :, :], x1[:, u, :, :],
                                    b_down[:, :].unsqueeze(1).broadcast_to([P, PAIRS, C]), ALU.add).then_inc(x1b_ready, 1)

        def pool_keys(pool, group, part):
            g, u = group.g, group.odd
            if part == 0:
                pool.wait_ge(qk_ready, g * 2 + 2)
                after(pool, s_psum, g * 4 - 4)
                settle(pool)
            windows = slice(part * NW // 2, (part + 1) * NW // 2)
            src_k = kt[:, :].rearrange("p (w q) -> p w q", w=NW)[:, windows, 0:N]
            for h in range(NH):
                i = nc.gpsimd.tensor_scalar(rows_of(group)[0:C, u, windows, h, :], src_k, head_mask[:, h:h + 1], 1.0, ALU.mult, ALU.mult)
            i.then_inc(k_ready, 1)

        BACK, AHEAD = 2, 3

        def steps(eng, step):
            def one(group, low):
                def do(piece, by, *rest):
                    other = group.on(by)
                    if isinstance(other.g, int):
                        if not 0 <= other.g < GROUPS:
                            return
                        other.low = other.g >= UNCUT
                    else:
                        other.low = low
                    piece(eng, other, *rest)
                step(do)

            def run(first, last, low=False):
                with eng.Fori(first // 2, last // 2) as i:
                    one(Group(i, 0), low)
                    one(Group(i, 1), low)

            def peel(first, last):
                for g in range(first, last):
                    one(Group(g // 2, g % 2), None)

            start = 2 * BACK
            if k == 0:
                stop = GROUPS - AHEAD - 1
                peel(-AHEAD, start)
                run(start, stop)
                peel(stop, GROUPS + BACK)
            else:
                stop, again, stop2 = UNCUT - AHEAD - 1, UNCUT, GROUPS - AHEAD - 1
                peel(-AHEAD, start)
                run(start, stop)
                peel(stop, again)
                run(again, stop2, low=True)
                peel(stop2, GROUPS + BACK)

        with nc.Block() as block:
            @block.sync
            def _(sp):
                def step(do):
                    do(sync_load, 3)
                    do(sync_store, -2)
                steps(sp, step)
                for u in range(2):
                    sp.wait_ge(stored[u], GROUPS // 2 * 32)

            @block.tensor
            def _(pe):
                def step(do):
                    do(pe_scores, 0, 2)
                    do(pe_up, -2)
                    do(pe_qk, 1)
                    do(pe_probs_t, 0, 1)
                    do(pe_pv, 0, 0)

                    do(pe_scores, 0, 3)
                    do(pe_v, 1)
                    do(pe_probs_t, 0, 2)
                    do(pe_ot, -1)
                    do(pe_pv, 0, 1)

                    do(pe_scores, 1, 0)
                    do(pe_proj, -1)
                    do(pe_probs_t, 0, 3)
                    if k == 0:
                        do(pe_patch, 3)
                    do(pe_pv, 0, 2)

                    do(pe_scores, 1, 1)
                    do(pe_down, -2)
                    do(pe_probs_t, 1, 0)
                    do(pe_pv, 0, 3)
                    do(pe_xt2, -1)
                    do(pe_xt, 2)
                steps(pe, step)

            @block.scalar
            def _(act):
                def step(do):
                    do(act_gelu, -2)
                    do(act_qk, 1)
                    do(act_exp, 0, 2)
                    do(act_pt, 0, 1)

                    do(act_pt, 0, 2)
                    do(act_ot, -1)
                    do(act_exp, 0, 3)

                    do(act_pt, 0, 3)
                    do(act_exp, 1, 0)

                    do(act_pt, 1, 0)
                    do(act_xt2, -1)
                    do(act_exp, 1, 1)
                    do(act_xt, 2)
                steps(act, step)

            @block.vector
            def _(dve):
                def step(do):
                    do(dve_shift, 0, 2)
                    do(dve_oa, -1)
                    if k == 0:
                        do(lambda dve, group: norm_apply(dve, "pe", group, affine=True), 2)

                    do(dve_shift, 0, 3)
                    do(dve_v, 1)
                    do(dve_ln1_stats, 2)

                    do(dve_shift, 1, 0)
                    do(dve_x1, -1)
                    do(dve_ln1_apply, 2)

                    do(dve_shift, 1, 1)
                    do(dve_ln2_apply, -1)
                    if k == 0:
                        do(dve_pe_stats, 3)
                    do(dve_out, -2)
                steps(dve, step)

            @block.gpsimd
            def _(pool):
                def rstd(name):
                    return lambda pool, group: rsqrt(pool, name, group.g)

                def step(do):
                    do(pool_keys, 1, 0)
                    do(rstd("ln1"), 2)
                    do(pool_keys, 1, 1)
                    do(rstd("ln2"), -1)
                    do(pool_residual, 1)
                    if k == 0:
                        do(rstd("pe"), 3)
                    do(pool_x1b, -1)
                steps(pool, step)


def fast_weights(nc, V, x, scratch):
    with ExitStack() as ctx:
        def sb(name, shape, dt=F32):
            return ctx.enter_context(nc.sbuf_tensor("f_" + name, shape, dt))

        def sem(name):
            return ctx.enter_context(nc.semaphore("f_" + name))

        ps_t, ps_p0, ps_p1, ps_pred, ps_out, ps_flag = [
            ctx.enter_context(nc.psum_tensor(f"f_bank{i}", [P, 512], F32)) for i in range(6)]
        ps_p = [ps_p0, ps_p1]

        w_f = sb("w_f", [C, QKV3])
        ident = sb("ident", [P, P])
        same_image = sb("same_image", [P, P])
        ones = sb("ones", [P, P])
        neghalf = sb("neghalf", [P, 4])
        st = [sb(n, [P, FI, C]) for n in ("s0", "m0", "s1", "m1")]
        s0, m0, s1, m1 = st
        wp = sb("wp", [P, 2, FI, C])
        xs = sb("xs", [P, 2, C])
        xc = sb("xc", [P, 2, C])
        sq = sb("sq", [P, 2, 2 * C])
        small = sb("small", [P, 8, 4])
        xn = sb("xn", [P, 2, C])
        xnt = sb("xnt", [C, 2 * P])
        sg = sb("sg", [P, 2, QKV3])
        pr = sb("pr", [P, 2, QKV3])
        rows = sb("rows", [P, CH, QKV3])
        res = sb("res", [P, CH, C])
        now = sb("now", [P, 2, QKV3])
        prod_a = sb("prod_a", [P, FI, C])
        prod_b = sb("prod_b", [P, FI, C])
        prod_e = sb("prod_e", [P, FI, C])
        prod_f = sb("prod_f", [P, FI, C])
        prod_g = sb("prod_g", [P, FI, C])
        h, sig, act_, om, ds, da, dhs, h2, sig2, a2 = [sb(n, [P, FI]) for n in
                                                    ("h", "sig", "act", "om", "ds", "da", "dhs", "h2", "sig2", "a2")]
        pred, dp, dps, o_row = [sb(n, [P, C]) for n in ("pred", "dp", "dps", "o_row")]
        nz = sb("nz", [P, 8])
        flag = sb("flag", [P, 1], I32)

        loaded, prep, flag_ready = sem("loaded"), sem("prep"), sem("flag_ready")
        x_in, rows_in, kept, saved = sem("x_in"), sem("rows_in"), sem("kept"), sem("saved")
        pre = Steps(sem("pre"), 16)
        xt_psum, xt_ready, p_psum = sem("xt_psum"), sem("xt_ready"), sem("p_psum")
        sg_ready, rs_ready, row_ready = sem("sg_ready"), sem("rs_ready"), sem("row_ready")
        per_step = Steps(sem("dve"), 22)
        gate_ready, ds_ready, e_ready, pred_psum = sem("gate_ready"), sem("ds_ready"), sem("e_ready"), sem("pred_psum")
        f_ready, g_ready, gate2_ready, out_psum = sem("f_ready"), sem("g_ready"), sem("gate2_ready"), sem("out_psum")
        pool_ds = sem("pool_ds")
        flag_psum, now_ready = sem("flag_psum"), sem("now_ready")
        flag_step = Steps(sem("flag_step"), 6)

        with nc.Block() as block:
            @block.sync
            def _(sp):
                sp.dma_start(w_f[:, :], V["w_fused_t"]).then_inc(loaded, 16)
                for j, (a, b) in enumerate((("W0_t", "P0_t"), ("W1", "P1"))):
                    for t, n in ((st[2 * j], a), (wp[:, j], b)):
                        src = V[n].rearrange("(s f) c -> s (f c)", s=FS).unsqueeze(0).broadcast_to([B, FS, FI * C])
                        sp.dma_start(t[:, :, :].rearrange("p f c -> p (f c)") , src).then_inc(loaded, 16)

            @block.gpsimd
            def _(pool):
                nc.gpsimd.memset(ident[:, :], 0.0).then_inc(prep, 1)
                nc.gpsimd.memset(same_image[:, :], 1.0).then_inc(prep, 1)
                nc.gpsimd.memset(neghalf[:, :], -0.5).then_inc(prep, 1)
                nc.gpsimd.memset(ones[:, :], 1.0).then_inc(prep, 1)
                pool.wait_ge(prep, 4)
                nc.gpsimd.affine_select(out=ident[:, :], in_=ident[:, :], compare_op=ALU.not_equal, fill=1.0,
                                        base=0, pattern=[[-1, P]], channel_multiplier=1).then_inc(prep, 1)
                blocks = same_image[:, :].rearrange("p (b s) -> p b s", s=FS)
                nc.gpsimd.affine_select(out=blocks, in_=blocks, compare_op=ALU.is_ge, fill=0.0, base=0,
                                        pattern=[[-FS, B], [0, FS]], channel_multiplier=1).then_inc(prep, 1)
                pool.wait_ge(prep, 6)
                nc.gpsimd.affine_select(out=blocks, in_=blocks, compare_op=ALU.is_ge, fill=0.0, base=FS - 1,
                                        pattern=[[FS, B], [0, FS]], channel_multiplier=-1).then_inc(prep, 1)

            @block.vector
            def _(dve):
                nc.vector.memset(m0[:, :, :], 0.0)
                nc.vector.memset(m1[:, :, :], 0.0)
                nc.vector.memset(flag[:, :], 1).then_inc(flag_ready, 1)
                dve.wait_ge(loaded, 16 * 5)
                nc.vector.tensor_tensor(s0[:, :, :], s0[:, :, :], wp[:, 0], ALU.add)
                nc.vector.tensor_tensor(s1[:, :, :], s1[:, :, :], wp[:, 1], ALU.add)

        def chunks(eng, chunk, skipped=None):
            with eng.Fori(0, CHUNKS) as i:
                eng.wait_ge(flag_ready, i + 1)
                settle(eng)
                live = eng.value_load(flag[0:1, 0:1], min_val=0, max_val=P)
                with eng.If(live > 0):
                    chunk(eng, i)
                with eng.Else():
                    if skipped:
                        skipped(eng)
                    else:
                        eng.nop()

        def wide(ap, axis):
            return ap.unsqueeze(axis).broadcast_to([P, FI, C])

        def eights(ap):
            return [ap[:, 8 * j:8 * j + 8, :].rearrange("p f c -> p (f c)") for j in range(FI // 8)]

        with nc.Block() as block:
            @block.sync
            def _(sp):
                def chunk(sp, i):
                    at = i * CH
                    after_saved = saved
                    for j in range(2):
                        sp.dma_start(xs[:, j, :], x[:, bass.ds(at + 8 * j, 8), :]).then_inc(x_in, 16)
                    sp.wait_ge(row_ready, 8 * 0 + i + 1)
                    for j in range(2):
                        sp.dma_start(scratch[:, 8 * j:8 * j + 8, :], pr[:, j, :]).then_inc(kept, 16)
                    sp.wait_ge(kept, i * 32 + 32)
                    sp.dma_start(rows[:, :, :].rearrange("p t c -> p (t c)"),
                                 scratch.rearrange("b t c -> b (t c)").unsqueeze(1).broadcast_to([B, FS, CH * QKV3])).then_inc(rows_in, 16)
                    sp.dma_start(res[:, :, :].rearrange("p t c -> p (t c)"),
                                 x[:, bass.ds(at, CH), :].rearrange("b t c -> b (t c)").unsqueeze(1).broadcast_to([B, FS, CH * C])).then_inc(rows_in, 16)
                    sp.wait_ge(per_step.sem, (i * CH + CH) * per_step.per)
                    sp.dma_start(x[:, bass.ds(at, CH), :].rearrange("b t c -> b (t c)"),
                                 res[0:P:FS, :, :].rearrange("p t c -> p (t c)")).then_inc(saved, 16)
                    sp.wait_ge(saved, i * 16 + 16)
                    settle(sp)
                chunks(sp, chunk)

            @block.tensor
            def _(pe):
                def chunk(pe, i):
                    pe.wait_ge(pre.sem, i * pre.per + 7)
                    settle(pe)
                    for j in range(2):
                        nc.tensor.transpose(ps_t[0:C, j * P:(j + 1) * P], xn[:, j, :], ident[:, :]).then_inc(xt_psum, 1)
                    pe.wait_ge(xt_ready, i + 1)
                    settle(pe)
                    for j in range(2):
                        nc.tensor.matmul(ps_p[j][:, 0:QKV3], xnt[:, j * P:(j + 1) * P], w_f[:, :], start=True, stop=True).then_inc(p_psum, 1)
                    with pe.Fori(0, CH) as t:
                        n = i * CH + t
                        pe.wait_ge(per_step.sem, n * per_step.per + 4)
                        for j, e in enumerate(eights(prod_b)):
                            last = nc.tensor.matmul(ps_pred[:, :], same_image[:, :], e, start=(j == 0), stop=(j == 3))
                        last.then_inc(pred_psum, 1)
                        pe.wait_ge(g_ready, n + 1)
                        for j, e in enumerate(eights(prod_g)):
                            last = nc.tensor.matmul(ps_out[:, :], same_image[:, :], e, start=(j == 0), stop=(j == 3))
                        last.then_inc(out_psum, 1)
                    pe.wait_ge(flag_step.sem, i * 6 + 5)
                    nc.tensor.matmul(ps_flag[:, 0:1], ones[:, :], nz[:, 4:5], start=True, stop=True).then_inc(flag_psum, 1)
                chunks(pe, chunk)

            @block.scalar
            def _(act):
                def chunk(act, i):
                    act.wait_ge(xt_psum, i * 2 + 2)
                    nc.scalar.copy(xnt[:, :], ps_t[0:C, 0:2 * P]).then_inc(xt_ready, 1)
                    act.wait_ge(p_psum, i * 2 + 2)
                    for j in range(2):
                        nc.scalar.activation(sg[:, j, 0:3 * C], ps_p[j][:, 0:3 * C], ACT.Sigmoid).then_inc(sg_ready, 1)
                        nc.scalar.activation(pr[:, j, 3 * C:3 * C + 1], ps_p[j][:, 3 * C:3 * C + 1], ACT.Sigmoid, scale=-1.0).then_inc(sg_ready, 1)
                        nc.scalar.activation(pr[:, j, 3 * C + 1:QKV3], ps_p[j][:, 3 * C + 1:QKV3], ACT.Sigmoid).then_inc(sg_ready, 1)
                    act.wait_ge(rows_in, i * 32 + 32)
                    with act.Fori(0, CH // 2) as t2:
                        for u in range(2):
                            t = t2 * 2 + u
                            n = i * CH + t
                            act.wait_ge(per_step.sem, n * per_step.per - per_step.per + 0) if False else None
                            nc.scalar.copy(now[:, u, :], rows[:, bass.ds(t, 1), :].rearrange("p t c -> p (t c)")).then_inc(now_ready, 1)
                            act.wait_ge(per_step.sem, n * per_step.per + 2)
                            nc.scalar.activation(sig[:, :], h[:, :], ACT.Sigmoid).then_inc(gate_ready, 1)
                            act.wait_ge(per_step.sem, n * per_step.per + 18)
                            nc.scalar.activation(sig2[:, :], h2[:, :], ACT.Sigmoid).then_inc(gate2_ready, 1)
                chunks(act, chunk)

        

            @block.vector
            def _(dve):
                tt, ts, red = nc.vector.tensor_tensor, nc.vector.tensor_scalar, nc.vector.tensor_reduce

                def norms(c, i):
                    def pair(ap):
                        return ap.unsqueeze(2).broadcast_to([P, 2, C])
                    c.start(i)
                    dve.wait_ge(x_in, i * 32 + 32)
                    c.did(red(small[:, 0, 0:2], xs[:, :, :], AX.X, ALU.add))
                    c.wait(dve)
                    c.did(ts(small[:, 1, 0:2], small[:, 0, 0:2], 1.0 / C, None, ALU.mult))
                    c.wait(dve)
                    c.did(tt(xc[:, :, :], xs[:, :, :], pair(small[:, 1, 0:2]), ALU.subtract))
                    c.wait(dve)
                    c.did(tt(sq[:, :, 0:C], xc[:, :, :], xc[:, :, :], ALU.mult))
                    c.wait(dve)
                    c.did(red(small[:, 2, 0:2], sq[:, :, 0:C], AX.X, ALU.add))
                    c.wait(dve)
                    c.did(ts(small[:, 3, 0:2], small[:, 2, 0:2], 1.0 / C, EPS, ALU.mult, ALU.add))
                    dve.wait_ge(rs_ready, i * 2 + 1)
                    c.did(tt(xn[:, :, :], xc[:, :, :], pair(small[:, 4, 0:2]), ALU.mult))
                    dve.wait_ge(sg_ready, i * 6 + 6)
                    for j in range(2):
                        c.did(tt(pr[:, j, 0:3 * C], ps_p[j][:, 0:3 * C], sg[:, j, 0:3 * C], ALU.mult))
                    c.wait(dve)
                    c.did(tt(sq[:, :, :], pr[:, :, 0:2 * C], pr[:, :, 0:2 * C], ALU.mult))
                    c.wait(dve)
                    c.did(red(small[:, 5, 0:4], sq[:, :, :].rearrange("p j (a c) -> p (j a) c", a=2), AX.X, ALU.add))
                    c.did(ts(pr[:, :, 2 * C:3 * C], pr[:, :, 2 * C:3 * C], 2.0 / C, None, ALU.mult))
                    c.did(ts(pr[:, :, 3 * C + 1:3 * C + 2], pr[:, :, 3 * C + 1:3 * C + 2], -2.0 * LR, None, ALU.mult))
                    dve.wait_ge(rs_ready, i * 2 + 2)
                    c.did(ts(small[:, 7, 0:4], small[:, 6, 0:4], L2_LIMIT, None, ALU.min))
                    c.wait(dve)
                    for j in range(2):
                        v = pr[:, j, 0:2 * C].rearrange("p (a c) -> p a c", a=2)
                        c.did(tt(v, v, small[:, 7, 2 * j:2 * j + 2].unsqueeze(2).broadcast_to([P, 2, C]), ALU.mult))
                    c.end()
                    c.wait(dve)
                    nc.vector.tensor_copy(nz[:, 6:7], pr[:, 0, 0:1]).then_inc(row_ready, 1)

                def one(c, n, t, u):
                    q, kk, v = (now[:, u, j * C:(j + 1) * C] for j in range(3))
                    keep, theta, eta = (now[:, u, 3 * C + j:3 * C + j + 1] for j in range(3))
                    c.start(n)
                    dve.wait_ge(now_ready, n + 1)
                    c.did(tt(prod_a[:, :, :], s0[:, :, :], wide(kk, 1), ALU.mult))
                    c.wait(dve)
                    c.did(red(h[:, :], prod_a[:, :, :], AX.X, ALU.add))
                    dve.wait_ge(gate_ready, n + 1)
                    c.did(tt(act_[:, :], h[:, :], sig[:, :], ALU.mult))
                    c.wait(dve)
                    c.did(tt(prod_b[:, :, :], s1[:, :, :], wide(act_[:, :], 2), ALU.mult))
                    dve.wait_ge(pred_psum, n + 1)
                    c.did(red(pred[:, :], ps_pred[:, :].rearrange("p (f c) -> p c f", c=C), AX.X, ALU.add))
                    c.wait(dve)
                    c.did(nc.vector.scalar_tensor_tensor(out=dp[:, :], in0=pred[:, :], scalar=2.0 / C, in1=v,
                                                         op0=ALU.mult, op1=ALU.subtract))
                    c.wait(dve)
                    c.did(ts(dps[:, :], dp[:, :], theta, None, ALU.mult))
                    c.did(tt(prod_a[:, :, :], s1[:, :, :], wide(dp[:, :], 1), ALU.mult))
                    c.wait(dve)
                    c.did(red(da[:, :], prod_a[:, :, :], AX.X, ALU.add))
                    c.wait(dve)
                    dve.wait_ge(ds_ready, n + 1)
                    c.did(nc.vector.scalar_tensor_tensor(out=dhs[:, :], in0=da[:, :], scalar=theta, in1=ds[:, :],
                                                         op0=ALU.mult, op1=ALU.mult))
                    c.wait(dve)
                    c.did(tt(prod_a[:, :, :], wide(dhs[:, :], 2), wide(kk, 1), ALU.mult))
                    c.wait(dve)
                    stt = nc.vector.scalar_tensor_tensor
                    c.did(stt(out=m0[:, :, :], in0=m0[:, :, :], scalar=eta, in1=prod_a[:, :, :], op0=ALU.mult, op1=ALU.add))
                    c.wait(dve)
                    c.did(stt(out=s0[:, :, :], in0=s0[:, :, :], scalar=keep, in1=m0[:, :, :], op0=ALU.mult, op1=ALU.add))
                    dve.wait_ge(e_ready, n + 1)
                    c.did(stt(out=m1[:, :, :], in0=m1[:, :, :], scalar=eta, in1=prod_e[:, :, :], op0=ALU.mult, op1=ALU.add))
                    c.wait(dve)
                    c.did(stt(out=s1[:, :, :], in0=s1[:, :, :], scalar=keep, in1=m1[:, :, :], op0=ALU.mult, op1=ALU.add))
                    c.did(nc.vector.memset(pred[:, 0:1], 0.0))
                    dve.wait_ge(f_ready, n + 1)
                    c.did(red(h2[:, :], prod_f[:, :, :], AX.X, ALU.add))
                    c.did(nc.vector.memset(pred[:, 1:2], 0.0))
                    dve.wait_ge(gate2_ready, n + 1)
                    c.did(tt(a2[:, :], h2[:, :], sig2[:, :], ALU.mult))
                    dve.wait_ge(out_psum, n + 1)
                    c.did(red(o_row[:, :], ps_out[:, :].rearrange("p (f c) -> p c f", c=C), AX.X, ALU.add))
                    c.wait(dve)
                    r = res[:, bass.ds(t, 1), :].rearrange("p t c -> p (t c)")
                    c.did(tt(r, r, o_row[:, :], ALU.add))
                    c.wait(dve)
                    c.did(nc.vector.memset(pred[:, 2:3], 0.0))
                    c.end()

                def chunk(dve, i):
                    norms(pre, i)
                    dve.wait_ge(rows_in, i * 32 + 32)
                    settle(dve)
                    with dve.Fori(0, CH // 2) as t2:
                        for u in range(2):
                            one(per_step, i * CH + t2 * 2 + u, t2 * 2 + u, u)
                    c = flag_step
                    c.start(i)
                    dve.wait_ge(per_step.sem, (i * CH + CH) * per_step.per)
                    for j, s in enumerate(st):
                        c.did(nc.vector.tensor_scalar(prod_a[:, :, :], s[:, :, :], 0.0, None, ALU.not_equal, ALU.max, accum_out=nz[:, j:j + 1]))
                        c.wait(dve)
                    c.did(red(nz[:, 4:5], nz[:, 0:4], AX.X, ALU.max))
                    dve.wait_ge(flag_psum, i + 1)
                    dve.wait_ge(saved, i * 16 + 16)
                    c.did(nc.vector.tensor_copy(nz[:, 5:6], ps_flag[:, 0:1]))
                    c.end()
                    c.wait(dve)
                    nc.vector.tensor_copy(flag[:, :], nz[:, 5:6]).then_inc(flag_ready, 1)
                chunks(dve, chunk, lambda dve: dve.sem_inc(flag_ready, 1))

            @block.gpsimd
            def _(pool):
                def chunk(pool, i):
                    pool.wait_ge(pre.sem, i * pre.per + 6)
                    nc.gpsimd.tensor_tensor(small[:, 4, 0:2], small[:, 3, 0:2], neghalf[:, 0:2], ALU.pow).then_inc(rs_ready, 1)
                    pool.wait_ge(pre.sem, i * pre.per + 11)
                    nc.gpsimd.tensor_tensor(small[:, 6, 0:4], small[:, 5, 0:4], neghalf[:, 0:4], ALU.pow).then_inc(rs_ready, 1)
                    with pool.Fori(0, CH // 2) as t2:
                        for u in range(2):
                            n = i * CH + t2 * 2 + u
                            at = n * per_step.per
                            q = now[:, u, 0:C]
                            pool.wait_ge(per_step.sem, at + 3)
                            settle(pool)
                            nc.gpsimd.tensor_scalar(om[:, :], sig[:, :], -1.0, 1.0, ALU.mult, ALU.add).then_inc(pool_ds, 1)
                            pool.wait_ge(pool_ds, n * 2 + 1)
                            nc.gpsimd.tensor_tensor(ds[:, :], om[:, :], act_[:, :], ALU.mult).then_inc(pool_ds, 1)
                            pool.wait_ge(pool_ds, n * 2 + 2)
                            nc.gpsimd.tensor_tensor(ds[:, :], ds[:, :], sig[:, :], ALU.add).then_inc(ds_ready, 1)
                            pool.wait_ge(per_step.sem, at + 7)
                            nc.gpsimd.tensor_tensor(prod_e[:, :, :], wide(act_[:, :], 2), wide(dps[:, :], 1), ALU.mult).then_inc(e_ready, 1)
                            pool.wait_ge(per_step.sem, at + 13)
                            nc.gpsimd.tensor_tensor(prod_f[:, :, :], s0[:, :, :], wide(q, 1), ALU.mult).then_inc(f_ready, 1)
                            pool.wait_ge(per_step.sem, at + 19)
                            nc.gpsimd.tensor_tensor(prod_g[:, :, :], s1[:, :, :], wide(a2[:, :], 2), ALU.mult).then_inc(g_ready, 1)
                chunks(pool, chunk)


def experts(nc, V, x, out):
    with ExitStack() as ctx:
        def sb(name, shape, dt=F32):
            return ctx.enter_context(nc.sbuf_tensor("e_" + name, shape, dt))

        def sem(name):
            return ctx.enter_context(nc.semaphore("e_" + name))

        banks = [ctx.enter_context(nc.psum_tensor(f"e_bank{i}", [P, 512], F32)) for i in range(8)]
        ps_t, ps_small, ps_choice, ps_h0, ps_h1, ps_h2, ps_y0, ps_y1 = banks
        ps_h, ps_y = [ps_h0, ps_h1, ps_h2], [ps_y0, ps_y1]
        ps_logit, ps_cum, ps_tot = (ps_small[:, j * TILES * E:(j + 1) * TILES * E].rearrange("p (t e) -> p t e", e=E)
                                    for j in range(3))

        w1 = sb("w1", [P, E, F])
        w2 = sb("w2", [P, E, 2, C])
        b2 = sb("b2", [P, C])
        w_gate = sb("w_gate", [C, E])
        b_gate = sb("b_gate", [1, E])
        ones1 = sb("ones1", [1, P])
        ident = sb("ident", [P, P])
        upto = sb("upto", [P, P])
        ones = sb("ones", [P, P])
        rank = sb("rank", [P, TILES, E])
        neghalf = sb("neghalf", [P, TILES])
        xg = sb("xg", [P, 2, TILES, C])
        xr = sb("xr", [P, 2, TILES, C])
        xc, sq, xn = sb("xc", [P, TILES, C]), sb("sq", [P, TILES, C]), sb("xn", [P, TILES, C])
        s, m, ss, var, rstd = [sb(n, [P, TILES]) for n in ("s", "m", "ss", "var", "rstd")]
        xt = sb("xt", [P, 2, SIZE])
        top, low, first, total, share, pos, kept = [sb(n, [P, TILES]) for n in
                                                    ("top", "low", "first", "total", "share", "pos", "kept")]
        z, ez, eq, choice, place = [sb(n, [P, TILES, E]) for n in ("z", "ez", "eq", "choice", "place")]
        before = sb("before", [P, TILES + 1, E])
        weight = sb("weight", [P, 2, TILES])
        hid = sb("hid", [P, 3, 512])
        y, over, under = [sb(n, [P, TILES, C]) for n in ("y", "over", "under")]
        finite = sb("finite", [P, TILES, C], I32)
        res = sb("res", [P, 2, TILES, C])

        loaded, prep, zeroed = sem("loaded"), sem("prep"), sem("zeroed")
        x_in, stored = [sem("x_in0"), sem("x_in1")], [sem("stored0"), sem("stored1")]
        ln = Steps(sem("ln"), 7)
        pick = Steps(sem("pick"), 17)
        end = Steps(sem("end"), 7)
        rstd_ready, xt_psum, xt_ready, logit_psum, ez_ready = [sem(n) for n in (
            "rstd_ready", "xt_psum", "xt_ready", "logit_psum", "ez_ready")]
        choice_psum, count_psum, choice_ready = sem("choice_psum"), sem("count_psum"), sem("choice_ready")
        xr_ready = sem("xr_ready")
        h_psum, y_psum = sem("h_psum"), sem("y_psum")
        hid_act, hid_dve, hid_used = sem("hid_act"), sem("hid_dve"), sem("hid_used")
        UNITS = E * 2

        with nc.Block() as block:
            @block.sync
            def _(sp):
                def load(o, i):
                    sp.dma_start(o, i).then_inc(loaded, 16)
                sp.wait_ge(zeroed, 3)
                load(w1[0:C, :, :], V["moe_w1"].rearrange("e d f -> d e f"))
                load(w2[:, :, :, :], V["moe_w2"].rearrange("e (h p) d -> p e h d", p=P))
                load(w_gate[:, :], V["gate_w"])
                load(b_gate[:, :], V["gate_b"].rearrange("(a e) -> a e", a=1))
                load(w1[K1 - 1:K1, :, :], V["moe_b1"].unsqueeze(0))
                load(b2[C:C + E, :], V["moe_b2"])
                sp.wait_ge(loaded, 16 * 6)

            @block.gpsimd
            def _(pool):
                nc.gpsimd.memset(ident[:, :], 0.0).then_inc(prep, 1)
                nc.gpsimd.memset(upto[:, :], 1.0).then_inc(prep, 1)
                nc.gpsimd.memset(ones[:, :], 1.0).then_inc(prep, 1)
                nc.gpsimd.memset(neghalf[:, :], -0.5).then_inc(prep, 1)
                nc.gpsimd.memset(before[:, :, :], 0.0).then_inc(prep, 1)
                nc.gpsimd.memset(ones1[:, :], 1.0).then_inc(prep, 1)
                pool.wait_ge(prep, 6)
                nc.gpsimd.affine_select(out=ident[:, :], in_=ident[:, :], compare_op=ALU.not_equal, fill=1.0,
                                        base=0, pattern=[[-1, P]], channel_multiplier=1).then_inc(prep, 1)
                nc.gpsimd.affine_select(out=upto[:, :], in_=upto[:, :], compare_op=ALU.is_ge, fill=0.0,
                                        base=0, pattern=[[1, P]], channel_multiplier=-1).then_inc(prep, 1)
                pool.wait_ge(prep, 8)
                pool.wait_ge(zeroed, 3)
                own = w1[C:C + E, :, :]
                nc.gpsimd.affine_select(out=own, in_=own, compare_op=ALU.not_equal, fill=0.0,
                                        base=0, pattern=[[-1, E], [0, F]], channel_multiplier=1).then_inc(prep, 1)

            @block.vector
            def _(dve):
                nc.vector.memset(w1[C:P, :, :], 0.0).then_inc(zeroed, 1)
                dve.wait_ge(zeroed, 1)
                nc.vector.memset(w1[C:C + E, :, :], OFF).then_inc(zeroed, 1)
                nc.vector.memset(b2[:, :], 0.0).then_inc(zeroed, 1)
                nc.vector.memset(xt[C:P, :, :], 1.0)
                for e in range(E):
                    nc.vector.memset(rank[:, :, e:e + 1], float(E - e))

        def tiles(ap, g):
            return ap[bass.ds(g, 1)].rearrange("g t p c -> p (g t) c")

        x_t = x.rearrange("b t c -> (b t) c").rearrange("(g t p) c -> g t p c", t=TILES, p=P)
        out_t = out.rearrange("b t c -> (b t) c").rearrange("(g t p) c -> g t p c", t=TILES, p=P)

        def on_tiles(ap, n):
            return ap.unsqueeze(2).broadcast_to([P, TILES, n])

        def sync_load(sp, group):
            u = group.odd
            after(sp, ln.sem, (group.g - 2) * ln.per + ln.per)
            settle(sp)
            after(sp, xr_ready, group.g - 1)
            settle(sp)
            sp.dma_start(xg[:, u, :, :], tiles(x_t, group.g)).then_inc(x_in[u], 16)

        def sync_store(sp, group):
            u = group.odd
            sp.wait_ge(end.sem, group.g * end.per + end.per)
            settle(sp)
            sp.dma_start(tiles(out_t, group.g), res[:, u, :, :]).then_inc(stored[u], 16)

        def pe_xt(pe, group):
            pe.wait_ge(ln.sem, group.g * ln.per + ln.per)
            settle(pe)
            for t in range(TILES):
                i = nc.tensor.transpose(ps_t[0:C, t * P:(t + 1) * P], xn[:, t, :], ident[:, :])
            i.then_inc(xt_psum, 1)

        def pe_logits(pe, group):
            pe.wait_ge(xt_ready, group.g + 1)
            after(pe, pick.sem, (group.g - 1) * pick.per + pick.per)
            settle(pe)
            for t in range(TILES):
                nc.tensor.matmul(ps_logit[:, t, :], xt[0:C, group.odd, t * P:(t + 1) * P], w_gate[:, :], start=True, stop=False)
                i = nc.tensor.matmul(ps_logit[:, t, :], ones1[:, :], b_gate[:, :], start=False, stop=True)
            i.then_inc(logit_psum, 1)

        def pe_choice(pe, group):
            g = group.g
            pe.wait_ge(pick.sem, g * pick.per + 6)
            after(pe, choice_ready, g)
            settle(pe)
            for t in range(TILES):
                i = nc.tensor.transpose(ps_choice[0:E, t * P:(t + 1) * P], choice[:, t, :], ident[:, :])
            i.then_inc(choice_psum, 1)
            flat = choice[:, :, :].rearrange("p t e -> p (t e)")
            nc.tensor.matmul(ps_cum.rearrange("p t e -> p (t e)"), upto[:, :], flat, start=True, stop=True)
            nc.tensor.matmul(ps_tot.rearrange("p t e -> p (t e)"), ones[:, :], flat, start=True, stop=True).then_inc(count_psum, 1)

        def pe_hidden(pe, group, n):
            g, u = group.g, group.odd
            e, half = n // 2, n % 2
            if n == 0:
                pe.wait_ge(choice_ready, g + 1)
                pe.wait_ge(xt_ready, g + 1)
            relu_of(pe, group, n - 3)
            nc.tensor.matmul(ps_h[n % 3][:, :], w1[:, e, half * P:(half + 1) * P], xt[:, u, :], start=True, stop=True).then_inc(h_psum, 1)

        def relu_of(eng, group, n):
            g = group.g
            if n < 0:
                if isinstance(g, int) and g == 0:
                    return
                n, g = n + UNITS, g - 1
            eng.wait_ge((hid_act, hid_dve)[n % 2], g * (UNITS // 2) + (n // 2 + 1))

        def pe_out(pe, group, n):
            g, u = group.g, group.odd
            e, half = n // 2, n % 2
            if n == 0:
                after(pe, end.sem, (g - 2) * end.per + end.per)
                for t in range(TILES):
                    nc.tensor.matmul(ps_y[u][:, t * C:(t + 1) * C], xt[:, u, t * P:(t + 1) * P], b2[:, :],
                                     start=(t == 0), stop=False, skip_group_check=True)
            relu_of(pe, group, n)
            for t in range(TILES):
                i = nc.tensor.matmul(ps_y[u][:, t * C:(t + 1) * C], hid[:, n % 3, t * P:(t + 1) * P], w2[:, e, half, :],
                                     start=False, stop=(n == UNITS - 1), skip_group_check=True)
            i.then_inc(hid_used, 1)

        def relu(eng, group, n):
            g = group.g
            eng.wait_ge(h_psum, g * UNITS + (n + 1))
            after(eng, hid_used, g * UNITS + (n - 2))
            if n % 2 == 0:
                nc.scalar.activation(hid[:, n % 3, :], ps_h[n % 3][:, :], ACT.Relu).then_inc(hid_act, 1)
            else:
                nc.vector.tensor_scalar(hid[:, n % 3, :], ps_h[n % 3][:, :], 0.0, None, ALU.max).then_inc(hid_dve, 1)

        def act_xt(act, group):
            act.wait_ge(xt_psum, group.g + 1)
            after(act, hid_used, group.g * UNITS - UNITS)
            nc.scalar.copy(xt[0:C, group.odd, :], ps_t[0:C, :]).then_inc(xt_ready, 1)

        def act_exp(act, group):
            act.wait_ge(pick.sem, group.g * pick.per + 2)
            nc.scalar.activation(ez[:, :, :], z[:, :, :], ACT.Exp).then_inc(ez_ready, 1)

        def act_choice(act, group):
            act.wait_ge(choice_psum, group.g + 1)
            nc.scalar.copy(xt[C:C + E, group.odd, :], ps_choice[0:E, :]).then_inc(choice_ready, 1)

        tt, ts, red = nc.vector.tensor_tensor, nc.vector.tensor_scalar, nc.vector.tensor_reduce

        def dve_norm(dve, group):
            u, g, c = group.odd, group.g, ln
            c.start(g)
            dve.wait_ge(x_in[u], group.half * 16 + 16)
            c.did(red(s[:, :], xg[:, u, :, :], AX.X, ALU.add))
            c.wait(dve)
            c.did(ts(m[:, :], s[:, :], 1.0 / C, None, ALU.mult))
            c.wait(dve)
            c.did(tt(xc[:, :, :], xg[:, u, :, :], on_tiles(m[:, :], C), ALU.subtract))
            c.wait(dve)
            c.did(tt(sq[:, :, :], xc[:, :, :], xc[:, :, :], ALU.mult))
            c.wait(dve)
            c.did(red(ss[:, :], sq[:, :, :], AX.X, ALU.add))
            c.wait(dve)
            c.did(ts(var[:, :], ss[:, :], 1.0 / C, EPS, ALU.mult, ALU.add))
            dve.wait_ge(rstd_ready, g + 1)
            after(dve, xt_psum, g)
            c.did(tt(xn[:, :, :], xc[:, :, :], on_tiles(rstd[:, :], C), ALU.mult))
            c.end()

        def dve_choose(dve, group):
            g, c = group.g, pick
            c.start(g)
            dve.wait_ge(logit_psum, g + 1)
            c.did(red(top[:, :], ps_logit, AX.X, ALU.max))
            c.wait(dve)
            c.did(tt(z[:, :, :], ps_logit, on_tiles(top[:, :], E), ALU.subtract))
            c.wait(dve)
            c.did(ts(eq[:, :, :], z[:, :, :], 0.0, None, ALU.is_equal))
            c.wait(dve)
            c.did(tt(eq[:, :, :], eq[:, :, :], rank[:, :, :], ALU.mult))
            c.wait(dve)
            c.did(red(first[:, :], eq[:, :, :], AX.X, ALU.max))
            c.wait(dve)
            after(dve, count_psum, g)
            c.did(tt(choice[:, :, :], eq[:, :, :], on_tiles(first[:, :], E), ALU.is_equal))
            dve.wait_ge(ez_ready, g + 1)
            c.did(red(total[:, :], ez[:, :, :], AX.X, ALU.add))
            c.wait(dve)
            c.did(nc.vector.reciprocal(share[:, :], total[:, :]))

        def dve_count(dve, group):
            g, c = group.g, pick
            c.start(g)
            c.n = 8
            dve.wait_ge(count_psum, g + 1)
            for t in range(TILES):
                c.did(tt(before[:, t + 1, :], before[:, t, :], ps_tot[:, t, :], ALU.add))
                c.wait(dve)
            c.did(tt(place[:, :, :], before[:, 0:TILES, :], ps_cum, ALU.add))
            c.wait(dve)
            c.did(tt(place[:, :, :], place[:, :, :], choice[:, :, :], ALU.mult))
            c.wait(dve)
            c.did(red(pos[:, :], place[:, :, :], AX.X, ALU.add))
            c.wait(dve)
            c.did(nc.vector.scalar_tensor_tensor(out=weight[:, group.odd, :], in0=pos[:, :], scalar=float(CAPACITY),
                                                 in1=share[:, :], op0=ALU.is_le, op1=ALU.mult))
            c.did(nc.vector.tensor_copy(before[:, 0, :], before[:, TILES, :]))
            c.end()

        def dve_end(dve, group):
            g, u, c = group.g, group.odd, end
            c.start(g)
            dve.wait_ge(hid_used, g * UNITS + UNITS)
            dve.wait_ge(pick.sem, g * pick.per + pick.per)
            c.did(tt(y[:, :, :], ps_y[u][:, 0:TILES * C].rearrange("p (t c) -> p t c", t=TILES),
                     on_tiles(weight[:, u, :], C), ALU.mult))
            c.wait(dve)
            c.did(ts(over[:, :, :], y[:, :, :], HUGE, CLIP, ALU.is_gt, ALU.mult))
            c.did(ts(under[:, :, :], y[:, :, :], -HUGE, -CLIP, ALU.is_lt, ALU.mult))
            c.did(ts(finite[:, :, :], y[:, :, :], 0.0, 0.0, ALU.mult, ALU.is_equal))
            c.wait(dve)
            c.did(tt(over[:, :, :], over[:, :, :], under[:, :, :], ALU.add))
            c.wait(dve)
            settle(dve)
            c.did(nc.vector.copy_predicated(over[:, :, :], finite[:, :, :], y[:, :, :]))
            c.wait(dve)
            after(dve, stored[u], group.half * 16)
            dve.wait_ge(xr_ready, g + 1)
            c.did(tt(res[:, u, :, :], over[:, :, :], xr[:, u, :, :], ALU.add))
            c.end()

        def pool_rstd(pool, group):
            u = group.odd
            pool.wait_ge(ln.sem, group.g * ln.per + 6)
            nc.gpsimd.tensor_tensor(rstd[:, :], var[:, :], neghalf[:, :], ALU.pow).then_inc(rstd_ready, 1)
            pool.wait_ge(x_in[u], group.half * 16 + 16)
            after(pool, end.sem, (group.g - 2) * end.per + end.per)
            settle(pool)
            nc.gpsimd.tensor_copy(xr[:, u, :, :], xg[:, u, :, :]).then_inc(xr_ready, 1)

        def steps(eng, step, a_only, c_only):
            f = Group(0, 0)
            a_only(eng, f)
            step(eng, f, True, False)
            with eng.Fori(0, SETS // 2 - 1) as i:
                step(eng, Group(i, 1), True, True)
                step(eng, Group(i + 1, 0), True, True)
            last = Group(SETS // 2 - 1, 1)
            step(eng, last, False, True)
            c_only(eng, last)

        with nc.Block() as block:
            @block.sync
            def _(sp):
                def step(sp, group, a, c):
                    if a:
                        sync_load(sp, group.next())
                    if c:
                        sync_store(sp, group.prev())
                steps(sp, step, sync_load, sync_store)
                for u in range(2):
                    sp.wait_ge(stored[u], SETS // 2 * 16)

            @block.tensor
            def _(pe):
                def a_only(pe, group):
                    pe_xt(pe, group)
                    pe_logits(pe, group)
                    pe_choice(pe, group)

                def step(pe, group, a, c):
                    pe_hidden(pe, group, 0)
                    pe_hidden(pe, group, 1)
                    for n in range(UNITS):
                        if n + 2 < UNITS:
                            pe_hidden(pe, group, n + 2)
                        pe_out(pe, group, n)
                        if a and n == 3:
                            pe_xt(pe, group.next())
                        if a and n == 6:
                            pe_logits(pe, group.next())
                        if a and n == 10:
                            pe_choice(pe, group.next())
                steps(pe, step, a_only, lambda pe, group: None)

            @block.scalar
            def _(act):
                def a_only(act, group):
                    act_xt(act, group)
                    act_exp(act, group)
                    act_choice(act, group)

                def step(act, group, a, c):
                    for n in range(0, UNITS, 2):
                        relu(act, group, n)
                        if a and n == 4:
                            act_xt(act, group.next())
                        if a and n == 8:
                            act_exp(act, group.next())
                        if a and n == 12:
                            act_choice(act, group.next())
                steps(act, step, a_only, lambda act, group: None)

            @block.vector
            def _(dve):
                def a_only(dve, group):
                    dve_norm(dve, group)
                    dve_choose(dve, group)
                    dve_count(dve, group)

                def step(dve, group, a, c):
                    for n in range(1, UNITS, 2):
                        relu(dve, group, n)
                        if a and n == 1:
                            dve_norm(dve, group.next())
                        if c and n == 5:
                            dve_end(dve, group.prev())
                        if a and n == 7:
                            dve_choose(dve, group.next())
                        if a and n == 13:
                            dve_count(dve, group.next())
                steps(dve, step, a_only, dve_end)

            @block.gpsimd
            def _(pool):
                steps(pool, lambda pool, group, a, c: pool_rstd(pool, group.next()) if a else None,
                      pool_rstd, lambda pool, group: None)


def shift_windows(nc, src, dst):
    old = src.rearrange("(b h) w (r c) d -> b h w r (c d)", b=B, r=WS)
    upper = dst[0:UNCUT].rearrange("(b h) w (r c) d -> b h w r (c d)", b=B, r=WS)
    lower = dst[UNCUT:GROUPS].rearrange("b w (r c) d -> b w r (c d)", r=WS)
    left, right = slice(0, KEEP * C), slice(KEEP * C, WS * C)
    old_left, old_right = slice(SHIFT * C, WS * C), slice(0, SHIFT * C)
    last = NW - 1

    def image(b):
        o, up, lo = (a[bass.ds(b, 1)].rearrange(f"z {s} -> (z {t}) {u}") for a, s, t, u in (
            (old, "h w r x", "h", "w r x"), (upper, "h w r x", "h", "w r x"), (lower, "w r x", "w", "r x")))
        moves = []
        for rows, old_rows, down in ((slice(0, KEEP), slice(SHIFT, WS), 0), (slice(KEEP, WS), slice(0, SHIFT), 1)):
            h, h_last = slice(down, last + down), last if not down else 0
            moves += [(up[:, :, rows, left].rearrange("h w r x -> (h w) r x"),
                       o[h, :, old_rows, old_left].rearrange("h w r x -> (h w) r x")),
                      (up[:, last, rows, right], o[h, 0, old_rows, old_right]),
                      (lo[:, rows, left], o[h_last, :, old_rows, old_left]),
                      (lo[0:last, rows, right], o[h_last, 1:NW, old_rows, old_right]),
                      (lo[last, rows, right], o[h_last, 0, old_rows, old_right])]
            moves += [(up[:, 0:last, rows.start + r, right], o[h, 1:NW, old_rows.start + r, old_right])
                      for r in range(rows.stop - rows.start)]
        return moves

    move_images(nc, "shift", image)


def unshift_windows(nc, src, dst):
    img = dst.rearrange("b (i j) c -> b i (j c)", i=SIDE)
    upper = src[0:UNCUT].rearrange("(b h) w (r c) d -> b h w r (c d)", b=B, r=WS)
    lower = src[UNCUT:GROUPS].rearrange("b w (r c) d -> b w r (c d)", r=WS)
    left, right = slice(0, KEEP * C), slice(KEEP * C, WS * C)
    last = NW - 1
    inner = slice(SHIFT, SIDE - KEEP)
    edge = slice((SIDE - KEEP) * C, SIDE * C)
    wrapped = slice(0, SHIFT * C)

    def image(b):
        im, up, lo = (a[bass.ds(b, 1)].rearrange(f"z {s} -> (z {t}) {u}") for a, s, t, u in (
            (img, "i x", "i", "x"), (upper, "h w r x", "h", "w r x"), (lower, "w r x", "w", "r x")))
        mid = im[inner].rearrange("(h r) x -> h r x", r=WS)
        moves = [(mid[:, :, edge], up[:, last, :, left]), (mid[:, :, wrapped], up[:, last, :, right])]
        moves += [(mid[:, r, SHIFT * C:(SIDE - KEEP) * C].rearrange("h (w x) -> h w x", w=last), up[:, 0:last, r, :])
                  for r in range(WS)]
        for rows, at in ((slice(0, KEEP), slice(SIDE - KEEP, SIDE)), (slice(KEEP, WS), slice(0, SHIFT))):
            moves += [(im[at, SHIFT * C:(SIDE - KEEP) * C].rearrange("r (w x) -> r w x", w=last),
                       lo[0:last, rows, :].rearrange("w r x -> r w x")),
                      (im[at, edge], lo[last, rows, left]), (im[at, wrapped], lo[last, rows, right])]
        return moves

    move_images(nc, "unshift", image)


def move_images(nc, name, image):
    with nc.semaphore(name + "_0") as s0, nc.semaphore(name + "_1") as s1, nc.Block() as block:
        def half(eng, sem, first):
            with eng.Fori(first, first + B // 2) as b:
                moves = image(b)
                for out, in_ in moves:
                    eng.dma_start(out, in_).then_inc(sem, 16)
            eng.wait_ge(sem, B // 2 * len(moves) * 16)

        @block.sync
        def _(sp):
            half(sp, s0, 0)

        @block.scalar
        def _(act):
            half(act, s1, B // 2)


def vit_tower(nc, V, out):
    def dram(name, shape):
        return nc.dram_tensor(name, shape, F32, kind="Internal").ap()

    windows = [GROUPS, NW, N, C]
    first, shifted, second = dram("first", windows), dram("shifted_in", windows), dram("second", windows)
    x = dram("x_tokens", [B, T, C])
    swin_block(nc, 0, V, V["patches"], first)
    shift_windows(nc, first, shifted)
    swin_block(nc, 1, V, shifted, second)
    unshift_windows(nc, second, x)
    fast_weights(nc, V, x, dram("rows_kept", [B, CH, QKV3]))
    experts(nc, V, x, out)


def kernel(**inputs):
    import numpy as np
    import concourse.bacc as bacc
    from concourse.bass_utils import run_bass_kernel_spmd

    a = {n: np.asarray(v) for n, v in inputs.items()}
    tok = {n[7:]: v for n, v in a.items() if n.startswith("L0_tok_")}
    att = {n[8:]: v for n, v in a.items() if n.startswith("L0_attn_")}
    ffn = {n[7:]: v for n, v in a.items() if n.startswith("L0_ffn_")}
    px = a["x"].reshape(B, NW, WS, 4, NW, WS, 4).transpose(3, 6, 0, 1, 4, 2, 5).reshape(PIX, GROUPS, NW, N)
    part = np.zeros((SIDE, SIDE), np.int32)
    cuts = (slice(0, -WS), slice(-WS, -SHIFT), slice(-SHIFT, None))
    for i, rows in enumerate(cuts):
        for j, cols in enumerate(cuts):
            part[rows, cols] = 3 * i + j
    part = part.reshape(NW, WS, NW, WS).transpose(0, 2, 1, 3).reshape(NW, NW, N)
    masks = np.stack([np.where(part[w][:, None] != part[w][None, :], np.float32(-100), np.float32(0))[::-1]
                      for w in ((0, NW - 1), (NW - 1, 0), (NW - 1, NW - 1))])
    arrays = {
        "patches": px, "masks": masks, "pe_t": tok["pe_w"].reshape(C, PIX).T,
        "qkv_t": tok["qkv_w"].transpose(0, 2, 1), "proj_t": tok["proj_w"].transpose(0, 2, 1),
        "w1_t": tok["w1"].transpose(0, 2, 1), "w2_t": tok["w2"].transpose(0, 2, 1),
        "rpb_t": tok["rpb"].transpose(0, 2, 1)[:, :, ::-1],
        "w_fused_t": att["W_fused"].T, "W0_t": att["W0"].T, "P0_t": att["P0"].T, "W1": att["W1"], "P1": att["P1"],
        "gate_w": ffn["gate_w"], "gate_b": ffn["gate_b"], "moe_w1": ffn["w1"], "moe_b1": ffn["b1"],
        "moe_w2": ffn["w2"], "moe_b2": ffn["b2"],
    }
    for n in ("pe_b", "pe_ng", "pe_nb", "n1g", "n1b", "qkv_b", "proj_b", "n2g", "n2b", "b1", "b2"):
        arrays[n] = tok[n]
    arrays = {n: np.ascontiguousarray(v) for n, v in arrays.items()}
    nc = bacc.Bacc("TRN2", target_bir_lowering=False, num_devices=1)
    V = {n: nc.dram_tensor("in_" + n, v.shape, mybir.dt.from_np(v.dtype), kind="ExternalInput").ap()
         for n, v in arrays.items()}
    out = nc.dram_tensor("out", (B, T, C), F32, kind="ExternalOutput").ap()
    vit_tower(nc, V, out)
    r = run_bass_kernel_spmd(nc, [{"in_" + n: v for n, v in arrays.items()}], core_ids=[0])
    return r.results[0]["out"]
```

```python
from contextlib import ExitStack

import concourse.bass as bass
from concourse import mybir

F32 = mybir.dt.float32
I32 = mybir.dt.int32
ALU = mybir.AluOpType
ACT = mybir.ActivationFunctionType
AX = mybir.AxisListType

B = 16
C = 64
WS = 7
NW = 8
N = WS * WS
SIDE = NW * WS
NH = 8
HD = C // NH
SHIFT = WS // 2
KEEP = WS - SHIFT
PAIRS = NW // 2
HALF = 64
P = 128
GROUPS = B * NW
UNCUT = B * (NW - 1)
KEYS = NH * N
HV = HD + 1
F = 4 * C
EPS = 1e-5
PIX = 16

T = SIDE * SIDE
CH = 56
SHARE, DA_SHARE = 18, 24
FIRST = 4
J = CH // 8
CHUNKS = T // CH
QKV3 = 3 * C + 3
FS = P // B
FI = F // FS
LR = 0.1
L2_LIMIT = 1e12
TOKENS = B * T
TILES = 4
SIZE = TILES * P
SETS = TOKENS // SIZE
E = 8
CAPACITY = -(-5 * TOKENS // (4 * E))
K1 = C + E + 1
OFF = -1e18
HUGE = 3.4028234663852886e38
CLIP = 1e4

class Steps:

    def __init__(self, sem, per):
        self.sem, self.per, self.base, self.n = sem, per, 0, 0

    def start(self, group, done=0):
        self.base, self.n = group * self.per, done

    def did(self, instruction):
        instruction.then_inc(self.sem, 1)
        self.n += 1

    def wait(self, engine):
        engine.wait_ge(self.sem, self.base + self.n)

    def end(self):
        assert self.n == self.per, (self.n, self.per)


class Group:

    def __init__(self, half, odd):
        self.half, self.odd, self.g = half, odd, half * 2 + odd

    def on(self, by):
        return Group(self.half + (self.odd + by) // 2, (self.odd + by) % 2)

    def next(self):
        return self.on(1)

    def prev(self):
        return self.on(-1)


def after(engine, sem, value):
    if not isinstance(value, int) or value > 0:
        engine.wait_ge(sem, value)


def settle(engine):
    engine.nop(nofuse=True)


def ones_row(ap):
    return ap[C:C + 1]


def tokens(ap, half):
    return ap.rearrange("(p w) t c -> w t p c", w=2)[half]


def swin_block(nc, k, V, src, dst, moves_of):
    with ExitStack() as ctx:
        def sb(name, shape, dt=F32):
            return ctx.enter_context(nc.sbuf_tensor(f"{name}_{k}", shape, dt))

        def sem(name):
            return ctx.enter_context(nc.semaphore(f"{name}_{k}"))

        banks = [ctx.enter_context(nc.psum_tensor(f"bank{i}_{k}", [P, 512], F32)) for i in range(8)]
        ps_a, ps_pt1, ps_c, ps_d, ps_s0, ps_s1, ps_pt0, ps_o = banks
        ps_s, ps_pt = [ps_s0, ps_s1], [ps_pt0, ps_pt1]

        w_qkv = sb("w_qkv", [P, 3 * C])
        w_proj = sb("w_proj", [P, C])
        w_up = sb("w_up", [P, F])
        w_down = sb("w_down", [P, 2, C])
        b_down = sb("b_down", [P, C])
        norm_g = sb("norm_g", [C, 2])
        norm_b = sb("norm_b", [C, 2])
        folded = sb("folded", [1, 3 * C + F])
        bias_in = sb("bias_in", [1, 3 * C + F])
        ident = sb("ident", [P, P])
        neghalf = sb("neghalf", [P, PAIRS])
        head_mask = sb("head_mask", [C, NH])
        masks = sb("masks", [HALF + N, 3, N])
        w_pe = sb("w_pe", [PIX + 1, C])
        pe_gain = sb("pe_gain", [P, C])
        pe_shift = sb("pe_shift", [P, C])
        patches = sb("patches", [PIX + 1, 2, NW, HALF]) if k == 0 else None
        xa = sb("xa", [P, 2, PAIRS, C])
        xr = sb("xr", [P, 2, PAIRS, C])
        xt = sb("xt", [P, 512])
        kt = sb("kt", [C, 512])
        q_rows = sb("q_rows", [P, 2, NW, HALF])
        k_rows = sb("k_rows", [P, 2, NW, NH, N])
        low_k_rows = sb("low_k_rows", [P, 2, NW, NH, N]) if k else None
        v_blk = sb("v_blk", [P, 2, NW, NH // 2, 2 * HV])
        probs = sb("probs", [P, 2, NH, HALF])
        probs_t = sb("probs_t", [P, 2, NH // 2, P])
        row_max = sb("row_max", [P, 2, NH])
        rec = sb("rec", [P, PAIRS * NH])
        oa = sb("oa", [P, PAIRS, C])
        ot = sb("ot", [P, 512])
        x1 = sb("x1", [P, 2, PAIRS, C])
        x1b = sb("x1b", [P, 2, PAIRS, C])
        xt2 = sb("xt2", [P, 512])
        hid = sb("hid", [P, 2, 512])
        xo = sb("xo", [P, 2, PAIRS, C])
        norms = {}
        for name in ("pe", "ln1", "ln2"):
            norms[name] = dict(
                xc=sb(f"{name}_xc", [P, PAIRS, C]), sq=sb(f"{name}_sq", [P, PAIRS, C]),
                xn=sb(f"{name}_xn", [P, PAIRS, C]), s=sb(f"{name}_s", [P, PAIRS]),
                m=sb(f"{name}_m", [P, PAIRS]), ss=sb(f"{name}_ss", [P, PAIRS]),
                var=sb(f"{name}_var", [P, PAIRS]), rstd=sb(f"{name}_rstd", [P, PAIRS]),
                chain=Steps(sem(f"{name}_chain"), 9 if name == "pe" else 7), rstd_ready=sem(f"{name}_rstd"))

        loaded, zeroed = sem("loaded"), sem("zeroed")
        prep = sem("prep")
        prep_pe = sem("prep_pe")
        prep_act = sem("prep_act")
        row_moved = sem("row_moved")
        x_in = [sem("x_in0"), sem("x_in1")]
        xp_psum = sem("xp_psum")
        xr_ready, xt_psum, xt_ready = sem("xr_ready"), sem("xt_psum"), sem("xt_ready")
        qk_psum, qk_ready, v_psum = sem("qk_psum"), sem("qk_ready"), sem("v_psum")
        v_ready, k_ready = sem("v_ready"), sem("k_ready")
        s_psum, max_ready, shifted, exp_ready = sem("s_psum"), sem("max_ready"), sem("shifted"), sem("exp_ready")
        p_psum, pt_ready, pv_done = sem("p_psum"), sem("pt_ready"), sem("pv_done")
        rec_ready, oa_ready, ot_psum, ot_ready = sem("rec_ready"), sem("oa_ready"), sem("ot_psum"), sem("ot_ready")
        proj_psum, x1_ready, t2_psum, xt2_ready = sem("proj_psum"), sem("x1_ready"), sem("t2_psum"), sem("xt2_ready")
        h_psum, h_ready, y_psum, out_ready = sem("h_psum"), sem("h_ready"), sem("y_psum"), sem("out_ready")
        x1b_ready, moved = sem("x1b_ready"), sem("moved")
        stored = [sem("stored0"), sem("stored1")]
        bias_set = sem("bias_set")

        pe_fold = sem("pe_fold")

        def fill_bias():
            first = k_rows[HALF:HALF + N, 0, 0, :, :]
            for u in range(2):
                for w in range(NW):
                    for low, rows in enumerate((k_rows, low_k_rows)[:k + 1]):
                        kind = 2 * low + (w == NW - 1)
                        out = rows[HALF:HALF + N, u, w, :, :]
                        if k and kind:
                            m = masks[HALF:HALF + N, kind - 1, :].unsqueeze(1).broadcast_to([N, NH, N])
                            nc.vector.tensor_tensor(out, first, m, ALU.add)
                        elif (u, w) != (0, 0):
                            nc.vector.tensor_copy(out, first)

        with nc.Block() as block:
            n_loads = 12 if k else 15

            @block.sync
            def _(sp):
                def load(out, in_):
                    sp.dma_start(out, in_).then_inc(loaded, 16)
                sp.wait_ge(zeroed, 3)
                load(w_qkv[0:C, :], V["qkv_t"][k])
                load(w_proj[0:C, :], V["proj_t"][k])
                load(w_proj[C:C + 1, :], V["proj_b"][k:k + 1, :])
                load(w_up[0:C, :], V["w1_t"][k])
                load(w_down[:, :, :], V["w2_t"][k].rearrange("(f p) c -> p f c", p=P))
                load(b_down[:, :], V["b2"][k:k + 1, :].broadcast_to([P, C]))
                load(bias_in[:, 0:3 * C], V["qkv_b"][k:k + 1, :])
                load(bias_in[:, 3 * C:], V["b1"][k:k + 1, :])
                with nc.allow_non_contiguous_dma(reason="a column of 64"):
                    load(norm_g[:, 0:1], V["n1g"][k:k + 1, :].rearrange("a c -> c a"))
                    load(norm_g[:, 1:2], V["n2g"][k:k + 1, :].rearrange("a c -> c a"))
                    load(norm_b[:, 0:1], V["n1b"][k:k + 1, :].rearrange("a c -> c a"))
                    load(norm_b[:, 1:2], V["n2b"][k:k + 1, :].rearrange("a c -> c a"))
                if k == 0:
                    load(w_pe[0:PIX, :], V["pe_t"][:, :])
                    load(w_pe[PIX:PIX + 1, :], V["pe_b"].rearrange("(a c) -> a c", a=1))
                    load(pe_gain[:, :], V["pe_ng"].rearrange("(a c) -> a c", a=1).broadcast_to([P, C]))
                    sp.dma_start(pe_shift[:, :], V["pe_nb"].rearrange("(a c) -> a c", a=1).broadcast_to([P, C])).then_inc(loaded, 16)
                sp.wait_ge(prep_act, 1)
                for rq in range(WS):
                    for h in range(NH):
                        base = V["rpb_t"][k, h, :]
                        row0 = HALF + rq * WS
                        src_ap = bass.AP(tensor=base.tensor, offset=base.offset + 13 * rq,
                                         ap=[[1, WS], [13, WS], [1, WS]])
                        sp.dma_start(k_rows[row0:row0 + WS, 0, 0, h, :].rearrange("p (a b) -> p a b", a=WS),
                                     src_ap).then_inc(bias_set, 16)
                if k == 1:
                    sp.dma_start(masks[HALF:HALF + N, :, :], V["masks"].rearrange("m q k -> q m k")).then_inc(bias_set, 16)
                sp.wait_ge(prep, 8)
                sp.dma_start(ones_row(w_qkv), folded[:, 0:3 * C]).then_inc(row_moved, 16)
                sp.dma_start(ones_row(w_up), folded[:, 3 * C:]).then_inc(row_moved, 16)

            @block.gpsimd
            def _(pool):
                nc.gpsimd.memset(ident[:, :], 0.0).then_inc(prep_pe, 1)
                nc.gpsimd.memset(q_rows[:, :, :, :], 0.0).then_inc(prep_pe, 1)
                nc.gpsimd.memset(neghalf[:, :], -0.5).then_inc(prep_pe, 1)
                nc.gpsimd.memset(head_mask[:, :], 1.0).then_inc(prep_pe, 1)
                pool.wait_ge(prep_pe, 4)
                nc.gpsimd.affine_select(out=ident[:, :], in_=ident[:, :], compare_op=ALU.not_equal, fill=1.0,
                                        base=0, pattern=[[-1, P]], channel_multiplier=1).then_inc(prep_pe, 1)
                nc.gpsimd.affine_select(out=head_mask[:, :], in_=head_mask[:, :], compare_op=ALU.is_ge, fill=0.0,
                                        base=0, pattern=[[-HD, NH]], channel_multiplier=1).then_inc(prep_pe, 1)
                pool.wait_ge(prep_pe, 6)
                nc.gpsimd.affine_select(out=head_mask[:, :], in_=head_mask[:, :], compare_op=ALU.is_ge, fill=0.0,
                                        base=HD - 1, pattern=[[HD, NH]], channel_multiplier=-1).then_inc(prep_pe, 1)
                q2 = q_rows[HALF:P, :, :, :].rearrange("p u w q -> p (u w) q")
                nc.gpsimd.affine_select(out=q2, in_=q2, compare_op=ALU.not_equal, fill=1.0, base=-(N - 1),
                                        pattern=[[0, 2 * NW], [1, HALF]], channel_multiplier=1).then_inc(prep_pe, 1)

            @block.vector
            def _(dve):
                for t in (w_qkv, w_proj, w_up):
                    nc.vector.memset(t[:, :], 0.0).then_inc(zeroed, 1)
                nc.vector.memset(k_rows[:, :, :, :, :], 0.0).then_inc(prep_act, 1)
                if k:
                    nc.vector.memset(low_k_rows[:, :, :, :, :], 0.0).then_inc(prep_act, 1)
                    dve.wait_ge(prep_act, 2)
                nc.vector.memset(v_blk[0:HALF, :, :, :, :], 0.0).then_inc(prep, 1)
                nc.vector.memset(v_blk[HALF:P, :, :, :, :], 0.0).then_inc(prep, 1)
                nc.vector.memset(probs[:, :, :, :], 0.0)
                nc.vector.memset(xa[:, :, :, :], 0.0)
                for t in (xt, ot, xt2):
                    nc.vector.memset(t[C:P, :], 1.0)
                if k == 0:
                    nc.vector.memset(patches[:, :, :, :], 0.0).then_inc(prep, 1)
                    dve.wait_ge(prep, 3)
                    nc.vector.memset(patches[:, :, :, :], 1.0).then_inc(prep, 1)
                    dve.wait_ge(prep, 4)
                    nc.vector.memset(patches[0:PIX, :, :, :], 0.0)
                else:
                    nc.vector.memset(masks[0:HALF, :, :], 0.0).then_inc(prep, 1)
                    nc.vector.memset(rec[:, :], 0.0).then_inc(prep, 1)
                dve.wait_ge(prep, 4)
                nc.vector.memset(v_blk[0:HALF, :, :, :, HD:HD + 1], 1.0)
                nc.vector.memset(v_blk[HALF:P, :, :, :, HV + HD:HV + HD + 1], 1.0)
                dve.wait_ge(loaded, 16 * (16 if k == 0 else 12))
                dve.wait_ge(pe_fold, 1)
                nc.vector.tensor_tensor(folded[:, 0:3 * C], ps_a[0:1, 0:3 * C], bias_in[:, 0:3 * C], ALU.add).then_inc(prep, 1)
                nc.vector.tensor_tensor(folded[:, 3 * C:], ps_c[0:1, 0:F], bias_in[:, 3 * C:], ALU.add).then_inc(prep, 1)
                nc.vector.tensor_scalar(w_qkv[0:C, :], w_qkv[0:C, :], norm_g[:, 0:1], None, ALU.mult).then_inc(prep, 1)
                nc.vector.tensor_scalar(w_up[0:C, :], w_up[0:C, :], norm_g[:, 1:2], None, ALU.mult).then_inc(prep, 1)
                dve.wait_ge(prep, 8)
                dve.wait_ge(row_moved, 32)
                nc.vector.tensor_scalar(w_qkv[:, 0:C], w_qkv[:, 0:C], float(HD) ** -0.5, None, ALU.mult)
                dve.wait_ge(bias_set, 16 * (WS * NH + (k == 1)))
                fill_bias()

            @block.tensor
            def _(pe):
                pe.wait_ge(loaded, 16 * (16 if k == 0 else 12))
                nc.tensor.matmul(ps_a[0:1, 0:3 * C], norm_b[:, 0:1], w_qkv[0:C, :], start=True, stop=True)
                nc.tensor.matmul(ps_c[0:1, 0:F], norm_b[:, 1:2], w_up[0:C, :], start=True, stop=True).then_inc(pe_fold, 1)

        def norm_stats(eng, name, group, x):
            T = norms[name]
            c = T["chain"]
            c.start(group.g)
            c.did(nc.vector.tensor_reduce(T["s"][:, :], x, AX.X, ALU.add))
            c.wait(eng)
            c.did(nc.vector.tensor_scalar(T["m"][:, :], T["s"][:, :], 1.0 / C, None, ALU.mult))
            c.wait(eng)
            c.did(nc.vector.tensor_tensor(T["xc"][:, :, :], x, T["m"][:, :].unsqueeze(2).broadcast_to([P, PAIRS, C]), ALU.subtract))
            c.wait(eng)
            c.did(nc.vector.tensor_tensor(T["sq"][:, :, :], T["xc"][:, :, :], T["xc"][:, :, :], ALU.mult))
            c.wait(eng)
            c.did(nc.vector.tensor_reduce(T["ss"][:, :], T["sq"][:, :, :], AX.X, ALU.add))
            c.wait(eng)
            c.did(nc.vector.tensor_scalar(T["var"][:, :], T["ss"][:, :], 1.0 / C, EPS, ALU.mult, ALU.add))

        def norm_apply(eng, name, group, affine=False):
            T = norms[name]
            c = T["chain"]
            c.start(group.g, 6)
            eng.wait_ge(T["rstd_ready"], group.g + 1)
            out = T["xn"][:, :, :]
            c.did(nc.vector.tensor_tensor(out, T["xc"][:, :, :], T["rstd"][:, :].unsqueeze(2).broadcast_to([P, PAIRS, C]), ALU.mult))
            if affine:
                c.wait(eng)
                c.did(nc.vector.tensor_tensor(out, out, pe_gain[:, :].unsqueeze(1).broadcast_to([P, PAIRS, C]), ALU.mult))
                c.wait(eng)
                after(eng, xr_ready, group.g - 1)
                after(eng, norms["ln1"]["chain"].sem, (group.g - 2) * LN_N + 3)
                c.did(nc.vector.tensor_tensor(xa[:, group.odd, :, :], out, pe_shift[:, :].unsqueeze(1).broadcast_to([P, PAIRS, C]), ALU.add))
            c.end()

        def rsqrt(eng, name, g):
            T = norms[name]
            eng.wait_ge(T["chain"].sem, g * T["chain"].per + 6)
            nc.gpsimd.tensor_tensor(T["rstd"][:, :], T["var"][:, :], neghalf[:, :], ALU.pow).then_inc(T["rstd_ready"], 1)

        PE_N, LN_N = norms["pe"]["chain"].per, 7

        def x_present(eng, group):
            if k == 0:
                eng.wait_ge(norms["pe"]["chain"].sem, group.g * PE_N + PE_N)
            else:
                eng.wait_ge(x_in[group.odd], group.half * 32 + 32)

        def rows_of(group):
            return low_k_rows if k and group.low else k_rows

        def sync_load(sp, group):
            g, u = group.g, group.odd
            if k == 0:
                after(sp, xp_psum, g - 1)
                sp.dma_start(patches[0:PIX, u, :, 0:N],
                             src[:, bass.ds(g, 1), :, :].rearrange("x g w t -> x (g w) t")).then_inc(x_in[u], 16)
            else:
                after(sp, norms["ln1"]["chain"].sem, (g - 2) * LN_N + LN_N)
                settle(sp)
                after(sp, xr_ready, g - 1)
                for half in range(2):
                    sp.dma_start(xa[HALF * half:HALF * half + N, u, :, :],
                                 tokens(src[bass.ds(g, 1)].rearrange("g w t c -> (g w) t c"), half)).then_inc(x_in[u], 16)

        def sync_store(sp, group):
            g, u = group.g, group.odd
            sp.wait_ge(out_ready, g + 1)
            for half in range(2):
                sp.dma_start(tokens(dst[bass.ds(g, 1)].rearrange("g w t c -> (g w) t c"), half),
                             xo[HALF * half:HALF * half + N, u, :, :]).then_inc(stored[u], 16)

        def pe_patch(pe, group):
            g, u = group.g, group.odd
            pe.wait_ge(x_in[u], group.half * 16 + 16)
            after(pe, v_ready, g - 1)
            if isinstance(g, int) and g == 1:
                pe.wait_ge(norms["pe"]["chain"].sem, 3)
            for p in range(PAIRS):
                i = nc.tensor.matmul(ps_a[:, p * C:(p + 1) * C], patches[:, u, 2 * p:2 * p + 2, :], w_pe[:, :],
                                     start=True, stop=True)
            i.then_inc(xp_psum, 1)

        def pe_transpose(pe, out, x):
            settle(pe)
            for p in range(PAIRS):
                i = nc.tensor.transpose(out[0:C, p * P:(p + 1) * P], x[:, p, :], ident[:, :])
            return i

        def pe_xt(pe, group):
            g = group.g
            pe.wait_ge(norms["ln1"]["chain"].sem, g * LN_N + LN_N)
            after(pe, v_ready, g)
            if k == 0 and not (isinstance(g, int) and g + 1 >= GROUPS):
                pe.wait_ge(norms["pe"]["chain"].sem, (g + 1) * PE_N + 3)
            pe_transpose(pe, ps_a, norms["ln1"]["xn"]).then_inc(xt_psum, 1)

        def pe_qk(pe, group):
            pe.wait_ge(xt_ready, group.g + 1)
            nc.tensor.matmul(ps_a[:, :], w_qkv[:, 0:2 * C], xt[:, :], start=True, stop=True).then_inc(qk_psum, 1)

        def pe_v(pe, group):
            pe.wait_ge(qk_ready, group.g * 2 + 2)
            for p in range(PAIRS):
                i = nc.tensor.matmul(ps_a[:, p * C:(p + 1) * C], xt[:, p * P:(p + 1) * P], w_qkv[:, 2 * C:3 * C],
                                     start=True, stop=True)
            i.then_inc(v_psum, 1)

        def pe_scores(pe, group, p):
            g, u = group.g, group.odd
            if p == 0:
                pe.wait_ge(qk_ready, g * 2 + 2)
            if p % 2 == 0:
                pe.wait_ge(k_ready, g * 2 + (p // 2 + 1))
            after(pe, shifted, g * 4 + (p - 1))
            for half in range(2):
                w = 2 * p + half
                i = nc.tensor.matmul(ps_s[p % 2][HALF * half:HALF * half + HALF, 0:KEYS],
                                     q_rows[:, u, w, :],
                                     rows_of(group)[:, u, w, :, :].rearrange("p h n -> p (h n)"),
                                     start=True, stop=True)
            i.then_inc(s_psum, 1)

        def pe_probs_t(pe, group, p):
            g = group.g
            pe.wait_ge(exp_ready, g * 4 + (p + 1))
            after(pe, pt_ready, g * 4 + (p - 1))
            for hp in range(NH // 2):
                i = nc.tensor.transpose(ps_pt[p % 2][:, hp * P:(hp + 1) * P],
                                        probs[:, p % 2, 2 * hp:2 * hp + 2, :].rearrange("p a b -> p (a b)"), ident[:, :])
            i.then_inc(p_psum, 1)

        def pe_pv(pe, group, p):
            g, u = group.g, group.odd
            pe.wait_ge(pt_ready, g * 4 + (p + 1))
            if p == 0:
                pe.wait_ge(v_ready, g + 1)
                after(pe, oa_ready, g)
            for half in range(2):
                for hp in range(NH // 2):
                    at = (p * 4 + hp) * 2 * HV
                    i = nc.tensor.matmul(ps_o[HALF * half:HALF * half + HALF, at:at + 2 * HV],
                                         probs_t[:, p % 2, hp, HALF * half:HALF * half + HALF],
                                         v_blk[:, u, 2 * p + half, hp, :], start=True, stop=True)
            i.then_inc(pv_done, 1)

        def pe_ot(pe, group):
            g = group.g
            pe.wait_ge(oa_ready, g + 1)
            after(pe, h_ready, g * 2)
            pe_transpose(pe, ps_d, oa).then_inc(ot_psum, 1)

        def pe_proj(pe, group):
            g = group.g
            pe.wait_ge(ot_ready, g + 1)
            for p in range(PAIRS):
                i = nc.tensor.matmul(ps_d[:, p * C:(p + 1) * C], ot[:, p * P:(p + 1) * P], w_proj[:, :],
                                     start=True, stop=True)
            i.then_inc(proj_psum, 1)

        def pe_xt2(pe, group):
            pe.wait_ge(norms["ln2"]["chain"].sem, group.g * LN_N + LN_N)
            pe_transpose(pe, ps_d, norms["ln2"]["xn"]).then_inc(t2_psum, 1)

        def pe_up(pe, group):
            pe.wait_ge(xt2_ready, group.g + 1)
            after(pe, out_ready, group.g)
            for f, bank in enumerate((ps_c, ps_d)):
                nc.tensor.matmul(bank[:, :], w_up[:, f * P:(f + 1) * P], xt2[:, :], start=True, stop=True).then_inc(h_psum, 1)

        def pe_down(pe, group):
            pe.wait_ge(h_ready, group.g * 2 + 2)
            for p in range(PAIRS):
                out = ps_c[:, p * C:(p + 1) * C]
                for f in range(2):
                    i = nc.tensor.matmul(out, hid[:, f, p * P:(p + 1) * P], w_down[:, f, :], start=(f == 0),
                                         stop=(f == 1))
            i.then_inc(y_psum, 1)

        def act_xt(act, group):
            g = group.g
            act.wait_ge(xt_psum, g + 1)
            after(act, v_psum, g)
            nc.scalar.copy(xt[0:C, :], ps_a[0:C, :]).then_inc(xt_ready, 1)

        def act_qk(act, group):
            g, u = group.g, group.odd
            act.wait_ge(qk_psum, g + 1)
            after(act, s_psum, g * 4 - 4)
            nc.scalar.copy(q_rows[0:C, u, :, :].rearrange("p w q -> p (w q)"), ps_a[0:C, :]).then_inc(qk_ready, 1)
            after(act, k_ready, g * 2)
            nc.scalar.copy(kt[:, :], ps_a[C:2 * C, :]).then_inc(qk_ready, 1)

        def act_exp(act, group, p):
            act.wait_ge(shifted, group.g * 4 + (p + 1))
            nc.scalar.activation(probs[:, p % 2, :, 0:N], probs[:, p % 2, :, 0:N], ACT.Exp).then_inc(exp_ready, 1)

        def act_pt(act, group, p):
            g = group.g
            act.wait_ge(p_psum, g * 4 + (p + 1))
            after(act, pv_done, g * 4 + (p - 1))
            nc.scalar.copy(probs_t[:, p % 2, :, :].rearrange("p a b -> p (a b)"), ps_pt[p % 2][:, :]).then_inc(pt_ready, 1)

        def act_ot(act, group):
            g = group.g
            act.wait_ge(ot_psum, g + 1)
            after(act, proj_psum, g)
            nc.scalar.copy(ot[0:C, :], ps_d[0:C, :]).then_inc(ot_ready, 1)

        def act_xt2(act, group):
            g = group.g
            act.wait_ge(t2_psum, g + 1)
            after(act, h_psum, g * 2)
            nc.scalar.copy(xt2[0:C, :], ps_d[0:C, :]).then_inc(xt2_ready, 1)

        def act_gelu(act, group):
            g = group.g
            after(act, y_psum, g)
            for f, bank in enumerate((ps_c, ps_d)):
                act.wait_ge(h_psum, g * 2 + (f + 1))
                nc.scalar.activation(hid[:, f, :], bank[:, :], ACT.Gelu).then_inc(h_ready, 1)

        def dve_pe_stats(dve, group):
            dve.wait_ge(xp_psum, group.g + 1)
            norm_stats(dve, "pe", group, ps_a[:, 0:PAIRS * C].rearrange("p (a c) -> p a c", a=PAIRS))

        def dve_ln1_stats(dve, group):
            x_present(dve, group)
            norm_stats(dve, "ln1", group, xa[:, group.odd, :, :])

        def dve_ln1_apply(dve, group):
            after(dve, xt_psum, group.g)
            norm_apply(dve, "ln1", group)

        def dve_shift(dve, group, p):
            g = group.g
            dve.wait_ge(s_psum, g * 4 + (p + 1))
            s = ps_s[p % 2][:, 0:KEYS].rearrange("p (h n) -> p h n", h=NH)
            nc.vector.tensor_reduce(row_max[:, p % 2, :], s, AX.X, ALU.max).then_inc(max_ready, 1)
            after(dve, p_psum, g * 4 + (p - 1))
            dve.wait_ge(max_ready, g * 4 + (p + 1))
            nc.vector.tensor_tensor(probs[:, p % 2, :, 0:N], s, row_max[:, p % 2, :].unsqueeze(2).broadcast_to([P, NH, N]),
                                    ALU.subtract).then_inc(shifted, 1)

        def dve_v(dve, group):
            g, u = group.g, group.odd
            dve.wait_ge(v_psum, g + 1)
            after(dve, pv_done, g * 4 - 4)
            v = ps_a[:, 0:PAIRS * C].rearrange("p (a h d) -> p a h d", a=PAIRS, d=HD)
            blk = v_blk[:, u, :, :, :].rearrange("p (a w) h d -> p w a h d", w=2)
            for half in range(2):
                rows = v[HALF * half:HALF * half + HALF]
                nc.vector.tensor_copy(blk[0:HALF, half, :, :, 0:HD], rows[:, :, 0:NH:2, :])
                i = nc.vector.tensor_copy(blk[HALF:P, half, :, :, HV:HV + HD], rows[:, :, 1:NH:2, :])
            i.then_inc(v_ready, 1)

        def dve_oa(dve, group):
            g = group.g
            dve.wait_ge(pv_done, g * 4 + 4)
            o = ps_o[:, 0:PAIRS * NH * HV].rearrange("p (a v) -> p a v", v=HV)
            nc.vector.reciprocal(rec[:, :].unsqueeze(2), o[:, :, HD:HV]).then_inc(rec_ready, 1)
            dve.wait_ge(rec_ready, g + 1)
            after(dve, ot_psum, g)
            nc.vector.tensor_tensor(oa[:, :, :].rearrange("p a (h d) -> p (a h) d", d=HD), o[:, :, 0:HD],
                                    rec[:, :].unsqueeze(2).broadcast_to([P, PAIRS * NH, HD]), ALU.mult).then_inc(oa_ready, 1)

        def dve_x1(dve, group):
            g, u = group.g, group.odd
            dve.wait_ge(proj_psum, g + 1)
            dve.wait_ge(xr_ready, g + 1)
            after(dve, x1b_ready, g - 1)
            nc.vector.tensor_tensor(x1[:, u, :, :], xr[:, u, :, :], ps_d[:, 0:PAIRS * C].rearrange("p (a c) -> p a c", a=PAIRS),
                                    ALU.add).then_inc(x1_ready, 1)
            dve.wait_ge(x1_ready, g + 1)
            norm_stats(dve, "ln2", group, x1[:, u, :, :])

        def dve_ln2_apply(dve, group):
            after(dve, t2_psum, group.g)
            norm_apply(dve, "ln2", group)

        def dve_out(dve, group):
            g, u = group.g, group.odd
            dve.wait_ge(y_psum, g + 1)
            after(dve, stored[u], group.half * 32)
            dve.wait_ge(x1b_ready, g + 1)
            nc.vector.tensor_tensor(xo[:, u, :, :], x1b[:, u, :, :], ps_c[:, 0:PAIRS * C].rearrange("p (a c) -> p a c", a=PAIRS),
                                    ALU.add).then_inc(out_ready, 1)

        def pool_residual(pool, group):
            x_present(pool, group)
            after(pool, x1_ready, group.g - 1)
            settle(pool)
            nc.gpsimd.tensor_copy(xr[:, group.odd, :, :], xa[:, group.odd, :, :]).then_inc(xr_ready, 1)

        def pool_x1b(pool, group):
            g, u = group.g, group.odd
            pool.wait_ge(x1_ready, g + 1)
            after(pool, out_ready, g - 1)
            settle(pool)
            nc.gpsimd.tensor_tensor(x1b[:, u, :, :], x1[:, u, :, :],
                                    b_down[:, :].unsqueeze(1).broadcast_to([P, PAIRS, C]), ALU.add).then_inc(x1b_ready, 1)

        def pool_keys(pool, group, part):
            g, u = group.g, group.odd
            if part == 0:
                pool.wait_ge(qk_ready, g * 2 + 2)
                after(pool, s_psum, g * 4 - 4)
                settle(pool)
            windows = slice(part * NW // 2, (part + 1) * NW // 2)
            src_k = kt[:, :].rearrange("p (w q) -> p w q", w=NW)[:, windows, 0:N]
            for h in range(NH):
                i = nc.gpsimd.tensor_scalar(rows_of(group)[0:C, u, windows, h, :], src_k, head_mask[:, h:h + 1], 1.0, ALU.mult, ALU.mult)
            i.then_inc(k_ready, 1)

        BACK, AHEAD = 2, 3

        def steps(eng, step):
            def one(group, low):
                def do(piece, by, *rest):
                    other = group.on(by)
                    if isinstance(other.g, int):
                        if not 0 <= other.g < GROUPS:
                            return
                        other.low = other.g >= UNCUT
                    else:
                        other.low = low
                    piece(eng, other, *rest)
                step(do)

            def run(first, last, low=False):
                with eng.Fori(first // 2, last // 2) as i:
                    one(Group(i, 0), low)
                    one(Group(i, 1), low)

            def peel(first, last):
                for g in range(first, last):
                    one(Group(g // 2, g % 2), None)

            start = 2 * BACK
            if k == 0:
                stop = GROUPS - AHEAD - 1
                peel(-AHEAD, start)
                run(start, stop)
                peel(stop, GROUPS + BACK)
            else:
                stop, again, stop2 = UNCUT - AHEAD - 1, UNCUT, GROUPS - AHEAD - 1
                peel(-AHEAD, start)
                run(start, stop)
                peel(stop, again)
                run(again, stop2, low=True)
                peel(stop2, GROUPS + BACK)

        with nc.Block() as block:
            @block.sync
            def _(sp):
                def at(group):
                    for piece, by in ((sync_load, 3), (sync_store, -2)):
                        other = group.on(by)
                        if not isinstance(other.g, int) or 0 <= other.g < GROUPS:
                            piece(sp, other)

                def move(b, half, odd, part, parts):
                    if part == 0:
                        sp.wait_ge(stored[0], (half + odd) * 32)
                        settle(sp)
                        sp.wait_ge(stored[1], half * 32)
                        settle(sp)
                    for out, in_ in moves_of(b)[part::parts]:
                        sp.dma_start(out, in_).then_inc(moved, 16)

                span, size = (1, NW) if k == 0 else (2, 2 * (NW - 1))
                LATE, PARTS = 3, 4
                per = size // span
                passes = B // span

                def images(i):
                    for j in range(size):
                        at(Group(i * (size // 2) + j // 2, j % 2))
                        for m in range(span):
                            part = j - m * per - LATE
                            if 0 <= part < PARTS:
                                b, ends = i * span + (m - 1), m * per
                                if not isinstance(b, int) or b >= 0:
                                    move(b, i * (size // 2) + ends // 2, ends % 2, part, PARTS)

                for g in range(-AHEAD, 0):
                    at(Group(g // 2, g % 2))
                images(0)
                looped = passes - 1 if k == 0 else passes
                with sp.Fori(1, looped) as i:
                    images(i)
                if looped < passes:
                    images(looped)
                for g in range(passes * size, GROUPS + BACK):
                    at(Group(g // 2, g % 2))
                    if g == min(passes * size + LATE, GROUPS + BACK - 1):
                        move(B - 1, passes * size // 2, 0, 0, 1)
                for u in range(2):
                    sp.wait_ge(stored[u], GROUPS // 2 * 32)
                sp.wait_ge(moved, B * len(moves_of(0)) * 16)

            @block.tensor
            def _(pe):
                def step(do):
                    do(pe_scores, 0, 2)
                    do(pe_up, -2)
                    do(pe_qk, 1)
                    do(pe_probs_t, 0, 1)
                    do(pe_pv, 0, 0)

                    do(pe_scores, 0, 3)
                    do(pe_v, 1)
                    do(pe_probs_t, 0, 2)
                    do(pe_ot, -1)
                    do(pe_pv, 0, 1)

                    do(pe_scores, 1, 0)
                    do(pe_proj, -1)
                    do(pe_probs_t, 0, 3)
                    if k == 0:
                        do(pe_patch, 3)
                    do(pe_pv, 0, 2)

                    do(pe_scores, 1, 1)
                    do(pe_down, -2)
                    do(pe_probs_t, 1, 0)
                    do(pe_pv, 0, 3)
                    do(pe_xt2, -1)
                    do(pe_xt, 2)
                steps(pe, step)

            @block.scalar
            def _(act):
                def step(do):
                    do(act_gelu, -2)
                    do(act_qk, 1)
                    do(act_exp, 0, 2)
                    do(act_pt, 0, 1)

                    do(act_pt, 0, 2)
                    do(act_ot, -1)
                    do(act_exp, 0, 3)

                    do(act_pt, 0, 3)
                    do(act_exp, 1, 0)

                    do(act_pt, 1, 0)
                    do(act_xt2, -1)
                    do(act_exp, 1, 1)
                    do(act_xt, 2)
                steps(act, step)

            @block.vector
            def _(dve):
                def step(do):
                    do(dve_shift, 0, 2)
                    do(dve_oa, -1)
                    if k == 0:
                        do(lambda dve, group: norm_apply(dve, "pe", group, affine=True), 2)

                    do(dve_shift, 0, 3)
                    do(dve_v, 1)
                    do(dve_ln1_stats, 2)

                    do(dve_shift, 1, 0)
                    do(dve_x1, -1)
                    do(dve_ln1_apply, 2)

                    do(dve_shift, 1, 1)
                    do(dve_ln2_apply, -1)
                    if k == 0:
                        do(dve_pe_stats, 3)
                    do(dve_out, -2)
                steps(dve, step)

            @block.gpsimd
            def _(pool):
                def rstd(name):
                    return lambda pool, group: rsqrt(pool, name, group.g)

                def step(do):
                    do(pool_keys, 1, 0)
                    do(rstd("ln1"), 2)
                    do(pool_keys, 1, 1)
                    do(rstd("ln2"), -1)
                    do(pool_residual, 1)
                    if k == 0:
                        do(rstd("pe"), 3)
                    do(pool_x1b, -1)
                steps(pool, step)


def fast_weights(nc, V, x, scratch):
    with ExitStack() as ctx:
        def sb(name, shape, dt=F32):
            return ctx.enter_context(nc.sbuf_tensor("f_" + name, shape, dt))

        def sem(name):
            return ctx.enter_context(nc.semaphore("f_" + name))

        banks = [ctx.enter_context(nc.psum_tensor(f"f_bank{i}", [P, 512], F32)) for i in range(8)]
        ps_pred, ps_out, ps_t = banks[0], banks[1], banks[2:4]
        ps_flag = ps_t[0]
        ps_p = [bank[:, QKV3 * j:QKV3 * j + QKV3] for bank in banks[4:8] for j in range(2)]

        t_banks = -(-J * P // 512)

        w_f = sb("w_f", [C, QKV3])
        ident = sb("ident", [P, P])
        same_image = sb("same_image", [P, P])
        ones = sb("ones", [P, P])
        neghalf = sb("neghalf", [P, 2 * J])
        st = [sb(n, [P, FI, C]) for n in ("s0", "m0", "s1", "m1")]
        s0, m0, s1, m1 = st
        wp = sb("wp", [P, 2, FI, C])
        xs = sb("xs", [P, J, C])
        xc = sb("xc", [P, J, C])
        sq = sb("sq", [P, J, 2 * C])
        small = sb("small", [P, 8, 2 * J])
        xn = sb("xn", [P, J, C])
        xnt = sb("xnt", [C, J * P])
        sg = sb("sg", [P, J, QKV3])
        pr = sb("pr", [P, J, QKV3])
        rows = sb("rows", [P, CH, QKV3])
        res = sb("res", [P, CH, C])
        now = sb("now", [P, 2, QKV3])
        prod_a = sb("prod_a", [P, FI, C])
        prod_b = sb("prod_b", [P, FI, C])
        em1 = sb("em1", [P, FI, C])
        prod_e = sb("prod_e", [P, FI, C])
        prod_f = sb("prod_f", [P, FI, C])
        prod_g = sb("prod_g", [P, FI, C])
        h, sig, act_, om, ds, da, dhs, h2, sig2, a2 = [sb(n, [P, FI]) for n in
                                                    ("h", "sig", "act", "om", "ds", "da", "dhs", "h2", "sig2", "a2")]
        pred, dp, dps, o_row = [sb(n, [P, C]) for n in ("pred", "dp", "dps", "o_row")]
        nz = sb("nz", [P, 8])
        flag = sb("flag", [P, 1], I32)

        loaded, prep, flag_ready = sem("loaded"), sem("prep"), sem("flag_ready")
        rows_first = sem("rows_first")
        x_in, rows_in, kept, saved = sem("x_in"), sem("rows_in"), sem("kept"), sem("saved")
        pre = Steps(sem("pre"), 12 + 2 * J)
        xt_psum, xt_ready, p_psum = sem("xt_psum"), sem("xt_ready"), sem("p_psum")
        sg_ready, rs_ready, row_ready = sem("sg_ready"), sem("rs_ready"), sem("row_ready")
        learn = Steps(sem("learn"), 19)
        answer = Steps(sem("answer"), 2)
        added = Steps(sem("added"), 2)
        H_AT, ACT_AT, B_AT, DP_AT, DPS_AT, DHS_AT, S0_AT, H2_AT, A2_AT = 3, 4, 5, 10, 11, 15, 19, 1, 2
        lo, hi = slice(0, SHARE), slice(SHARE, FI)
        da_lo, da_hi = slice(0, DA_SHARE), slice(DA_SHARE, FI)
        parts = sem("parts")
        PARTS, H_PART, DA_PART, E_PART, OUTER_PART = 4, 1, 2, 3, 4
        s1_ready, em1_ready, m1_ready = sem("s1_ready"), sem("em1_ready"), sem("m1_ready")
        gate_ready, ds_ready, e_ready, pred_psum = sem("gate_ready"), sem("ds_ready"), sem("e_ready"), sem("pred_psum")
        f_ready, g_ready, gate2_ready, out_psum = sem("f_ready"), sem("g_ready"), sem("gate2_ready"), sem("out_psum")
        pool_ds = sem("pool_ds")
        flag_psum, now_ready = sem("flag_psum"), sem("now_ready")
        flag_step = Steps(sem("flag_step"), 6)

        with nc.Block() as block:
            @block.sync
            def _(sp):
                sp.dma_start(w_f[:, :], V["w_fused_t"]).then_inc(loaded, 16)
                for j, (a, b) in enumerate((("W0_t", "P0_t"), ("W1", "P1"))):
                    for t, n in ((st[2 * j], a), (wp[:, j], b)):
                        src = V[n].rearrange("(s f) c -> s (f c)", s=FS).unsqueeze(0).broadcast_to([B, FS, FI * C])
                        sp.dma_start(t[:, :, :].rearrange("p f c -> p (f c)") , src).then_inc(loaded, 16)

            @block.gpsimd
            def _(pool):
                nc.gpsimd.memset(ident[:, :], 0.0).then_inc(prep, 1)
                nc.gpsimd.memset(same_image[:, :], 1.0).then_inc(prep, 1)
                nc.gpsimd.memset(neghalf[:, :], -0.5).then_inc(prep, 1)
                nc.gpsimd.memset(ones[:, :], 1.0).then_inc(prep, 1)
                pool.wait_ge(prep, 4)
                nc.gpsimd.affine_select(out=ident[:, :], in_=ident[:, :], compare_op=ALU.not_equal, fill=1.0,
                                        base=0, pattern=[[-1, P]], channel_multiplier=1).then_inc(prep, 1)
                blocks = same_image[:, :].rearrange("p (b s) -> p b s", s=FS)
                nc.gpsimd.affine_select(out=blocks, in_=blocks, compare_op=ALU.is_ge, fill=0.0, base=0,
                                        pattern=[[-FS, B], [0, FS]], channel_multiplier=1).then_inc(prep, 1)
                pool.wait_ge(prep, 6)
                nc.gpsimd.affine_select(out=blocks, in_=blocks, compare_op=ALU.is_ge, fill=0.0, base=FS - 1,
                                        pattern=[[FS, B], [0, FS]], channel_multiplier=-1).then_inc(prep, 1)

            @block.vector
            def _(dve):
                nc.vector.memset(m0[:, :, :], 0.0)
                nc.vector.memset(m1[:, :, :], 0.0).then_inc(m1_ready, 1)
                nc.vector.memset(flag[:, :], 1).then_inc(flag_ready, 1)
                dve.wait_ge(loaded, 16 * 5)
                nc.vector.tensor_tensor(s0[:, :, :], s0[:, :, :], wp[:, 0], ALU.add)
                nc.vector.tensor_tensor(s1[:, :, :], s1[:, :, :], wp[:, 1], ALU.add)

        def chunks(eng, chunk, skipped=None):
            with eng.Fori(0, CHUNKS) as i:
                eng.wait_ge(flag_ready, i + 1)
                settle(eng)
                live = eng.value_load(flag[0:1, 0:1], min_val=0, max_val=P)
                with eng.If(live > 0):
                    chunk(eng, i)
                with eng.Else():
                    if skipped:
                        skipped(eng)
                    else:
                        eng.nop()

        def in_chunk(eng, i, step):
            def pair(t):
                for u in range(2):
                    step(i * CH + (t + u), t + u, u)
            pair(0)
            settle(eng)
            with eng.Fori(1, CH // 2 - 1) as half:
                pair(half * 2)
            pair(CH - 2)
            step(i * CH + CH, CH, None)

        def has_last(t, by=1):
            return not isinstance(t, int) or t >= by

        def wide(ap, axis):
            return ap.unsqueeze(axis).broadcast_to([P, FI, C])

        def part(ap, axis, units):
            return ap.unsqueeze(axis).broadcast_to([P, units.stop - units.start, C])

        def fours(ap):
            return [ap[:, 4 * j:4 * j + 4, :].rearrange("p f c -> p (f c)") for j in range(FI // 4)]

        with nc.Block() as block:
            @block.sync
            def _(sp):
                def chunk(sp, i):
                    at = i * CH
                    for j in range(J):
                        sp.dma_start(xs[:, j, :], x[:, bass.ds(at + 8 * j, 8), :]).then_inc(x_in, 16)
                    sp.wait_ge(row_ready, i + 1)
                    for j in range(J):
                        sp.dma_start(scratch[:, 8 * j:8 * j + 8, :], pr[:, j, :]).then_inc(kept, 16)
                    sp.wait_ge(kept, i * 16 * J + 16 * J)
                    for part, there in ((slice(0, FIRST), rows_first), (slice(FIRST, CH), rows_in)):
                        width = (part.stop - part.start) * QKV3
                        sp.dma_start(rows[:, part, :].rearrange("p t c -> p (t c)"),
                                     scratch[:, part, :].rearrange("b t c -> b (t c)").unsqueeze(1)
                                     .broadcast_to([B, FS, width])).then_inc(there, 16)
                    sp.dma_start(res[:, :, :].rearrange("p t c -> p (t c)"),
                                 x[:, bass.ds(at, CH), :].rearrange("b t c -> b (t c)").unsqueeze(1).broadcast_to([B, FS, CH * C])).then_inc(rows_in, 16)
                    sp.wait_ge(added.sem, (i * CH + CH) * added.per)
                    sp.dma_start(x[:, bass.ds(at, CH), :].rearrange("b t c -> b (t c)"),
                                 res[0:P:FS, :, :].rearrange("p t c -> p (t c)")).then_inc(saved, 16)
                    sp.wait_ge(saved, i * 16 + 16)
                    settle(sp)
                chunks(sp, chunk)

            @block.tensor
            def _(pe):
                def chunk(pe, i):
                    pe.wait_ge(pre.sem, i * pre.per + 7)
                    settle(pe)
                    for j in range(J):
                        nc.tensor.transpose(ps_t[j // 4][0:C, j % 4 * P:(j % 4 + 1) * P], xn[:, j, :], ident[:, :]).then_inc(xt_psum, 1)
                    pe.wait_ge(xt_ready, i * t_banks + t_banks)
                    settle(pe)
                    for j in range(J):
                        nc.tensor.matmul(ps_p[j], xnt[:, j * P:(j + 1) * P], w_f[:, :], start=True, stop=True).then_inc(p_psum, 1)
                    def step(n, t, u):
                        if u is not None:
                            for j, e in enumerate(fours(prod_b)):
                                if j % 2 == 0:
                                    pe.wait_ge(learn.sem, n * learn.per + (B_AT + j // 2))
                                last = nc.tensor.matmul(ps_pred[:, 0:4 * C], same_image[:, :], e, start=(j == 0), stop=(j == 7))
                            last.then_inc(pred_psum, 1)
                        if has_last(t):
                            pe.wait_ge(g_ready, n)
                            for j, e in enumerate(fours(prod_g)):
                                last = nc.tensor.matmul(ps_out[:, 0:4 * C], same_image[:, :], e, start=(j == 0), stop=(j == 7))
                            last.then_inc(out_psum, 1)
                    in_chunk(pe, i, step)
                    pe.wait_ge(flag_step.sem, i * 6 + 5)
                    nc.tensor.matmul(ps_flag[:, 0:1], ones[:, :], nz[:, 4:5], start=True, stop=True).then_inc(flag_psum, 1)
                chunks(pe, chunk)

            @block.scalar
            def _(act):
                def chunk(act, i):
                    act.wait_ge(xt_psum, i * J + J)
                    for bank, at in zip(ps_t, range(0, J * P, 512)):
                        some = min(J * P - at, 512)
                        nc.scalar.copy(xnt[:, at:at + some], bank[0:C, 0:some]).then_inc(xt_ready, 1)
                    act.wait_ge(p_psum, i * J + J)
                    for j in range(J):
                        nc.scalar.activation(sg[:, j, 0:3 * C], ps_p[j][:, 0:3 * C], ACT.Sigmoid).then_inc(sg_ready, 1)
                        nc.scalar.activation(pr[:, j, 3 * C:3 * C + 1], ps_p[j][:, 3 * C:3 * C + 1], ACT.Sigmoid, scale=-1.0).then_inc(sg_ready, 1)
                        nc.scalar.activation(pr[:, j, 3 * C + 1:QKV3], ps_p[j][:, 3 * C + 1:QKV3], ACT.Sigmoid).then_inc(sg_ready, 1)
                    def row(t, u):
                        nc.scalar.copy(now[:, u, :], rows[:, bass.ds(t, 1), :].rearrange("p t c -> p (t c)")).then_inc(now_ready, 1)

                    def step(n, t, u):
                        if u is not None:
                            act.wait_ge(learn.sem, n * learn.per + H_AT)
                            nc.scalar.activation(sig[:, :], h[:, :], ACT.Sigmoid).then_inc(gate_ready, 1)
                            act.wait_ge(m1_ready, n + 1)
                            nc.scalar.activation(em1[:, :, :], m1[:, :, :], ACT.Copy, scale=now[:, u, 3 * C + 2:3 * C + 3]).then_inc(em1_ready, 1)
                        if has_last(t):
                            act.wait_ge(answer.sem, (n - 1) * answer.per + H2_AT)
                            nc.scalar.activation(sig2[:, :], h2[:, :], ACT.Sigmoid).then_inc(gate2_ready, 1)
                        if isinstance(t, int) and t == 1:
                            act.wait_ge(rows_in, i * 32 + 32)
                            settle(act)
                        if u is not None and not (isinstance(t, int) and t + 1 >= CH):
                            row(t + 1, 1 - u)
                        if u is not None:
                            act.wait_ge(learn.sem, n * learn.per + DPS_AT)
                            for j in range(SHARE):
                                e = nc.scalar.activation(prod_e[:, j, :], dps[:, :], ACT.Copy, scale=act_[:, j:j + 1])
                            e.then_inc(e_ready, 1)
                    act.wait_ge(rows_first, i * 16 + 16)
                    settle(act)
                    row(0, 0)
                    in_chunk(act, i, step)
                chunks(act, chunk)

            @block.vector
            def _(dve):
                tt, ts, red = nc.vector.tensor_tensor, nc.vector.tensor_scalar, nc.vector.tensor_reduce

                def norms(c, i):
                    def pair(ap):
                        return ap.unsqueeze(2).broadcast_to([P, J, C])
                    c.start(i)
                    dve.wait_ge(x_in, i * 16 * J + 16 * J)
                    c.did(red(small[:, 0, 0:J], xs[:, :, :], AX.X, ALU.add))
                    c.wait(dve)
                    c.did(ts(small[:, 1, 0:J], small[:, 0, 0:J], 1.0 / C, None, ALU.mult))
                    c.wait(dve)
                    c.did(tt(xc[:, :, :], xs[:, :, :], pair(small[:, 1, 0:J]), ALU.subtract))
                    c.wait(dve)
                    c.did(tt(sq[:, :, 0:C], xc[:, :, :], xc[:, :, :], ALU.mult))
                    c.wait(dve)
                    c.did(red(small[:, 2, 0:J], sq[:, :, 0:C], AX.X, ALU.add))
                    c.wait(dve)
                    c.did(ts(small[:, 3, 0:J], small[:, 2, 0:J], 1.0 / C, EPS, ALU.mult, ALU.add))
                    dve.wait_ge(rs_ready, i * 2 + 1)
                    c.did(tt(xn[:, :, :], xc[:, :, :], pair(small[:, 4, 0:J]), ALU.mult))
                    dve.wait_ge(sg_ready, i * 3 * J + 3 * J)
                    for j in range(J):
                        c.did(tt(pr[:, j, 0:3 * C], ps_p[j][:, 0:3 * C], sg[:, j, 0:3 * C], ALU.mult))
                    c.wait(dve)
                    c.did(tt(sq[:, :, :], pr[:, :, 0:2 * C], pr[:, :, 0:2 * C], ALU.mult))
                    c.wait(dve)
                    c.did(red(small[:, 5, :], sq[:, :, :].rearrange("p j (a c) -> p (j a) c", a=2), AX.X, ALU.add))
                    c.did(ts(pr[:, :, 2 * C:3 * C], pr[:, :, 2 * C:3 * C], 2.0 / C, None, ALU.mult))
                    c.did(ts(pr[:, :, 3 * C + 1:3 * C + 2], pr[:, :, 3 * C + 1:3 * C + 2], -2.0 * LR, None, ALU.mult))
                    dve.wait_ge(rs_ready, i * 2 + 2)
                    c.did(ts(small[:, 7, :], small[:, 6, :], L2_LIMIT, None, ALU.min))
                    c.wait(dve)
                    for j in range(J):
                        v = pr[:, j, 0:2 * C].rearrange("p (a c) -> p a c", a=2)
                        c.did(tt(v, v, small[:, 7, 2 * j:2 * j + 2].unsqueeze(2).broadcast_to([P, 2, C]), ALU.mult))
                    c.end()
                    c.wait(dve)
                    nc.vector.tensor_copy(nz[:, 6:7], pr[:, 0, 0:1]).then_inc(row_ready, 1)

                stt = nc.vector.scalar_tensor_tensor

                def step(i, n, t, u):
                    c, a = learn, answer
                    if isinstance(t, int) and t == 1:
                        dve.wait_ge(rows_in, i * 32 + 32)
                        settle(dve)
                    if u is not None:
                        kk, v = (now[:, u, j * C:(j + 1) * C] for j in (1, 2))
                        keep, theta, eta = (now[:, u, 3 * C + j:3 * C + j + 1] for j in range(3))
                        c.start(n)
                        if has_last(t):
                            dve.wait_ge(learn.sem, n * learn.per)
                        dve.wait_ge(now_ready, n + 1)
                        c.did(tt(prod_a[:, lo, :], s0[:, lo, :], part(kk, 1, lo), ALU.mult))
                        c.wait(dve)
                        c.did(red(h[:, lo], prod_a[:, lo, :], AX.X, ALU.add))
                        dve.wait_ge(parts, n * PARTS + H_PART)
                        c.did(red(h[:, hi], prod_a[:, hi, :], AX.X, ALU.add))
                    if has_last(t):
                        dve.wait_ge(m1_ready, n + 1)
                        if has_last(t, 2):
                            dve.wait_ge(g_ready, n - 1)
                        last = now[:, 1 - (u or 0), 3 * C:3 * C + 1]
                        stt(out=s1[:, :, :], in0=s1[:, :, :], scalar=last, in1=m1[:, :, :], op0=ALU.mult, op1=ALU.add).then_inc(s1_ready, 1)
                    if u is not None:
                        dve.wait_ge(gate_ready, n + 1)
                        c.did(tt(act_[:, :], h[:, :], sig[:, :], ALU.mult))
                        c.wait(dve)
                        if has_last(t):
                            dve.wait_ge(s1_ready, n)
                        for j in range(4):
                            some = slice(8 * j, 8 * j + 8)
                            c.did(tt(prod_b[:, some, :], s1[:, some, :], part(act_[:, some], 2, some), ALU.mult))
                    if has_last(t):
                        a.start(n - 1)
                        dve.wait_ge(f_ready, n)
                        a.did(red(h2[:, :], prod_f[:, :, :], AX.X, ALU.add))
                    if has_last(t, 2):
                        add_answer(n - 2, t - 2)
                    if has_last(t):
                        dve.wait_ge(gate2_ready, n)
                        a.did(tt(a2[:, :], h2[:, :], sig2[:, :], ALU.mult))
                    if u is not None:
                        dve.wait_ge(pred_psum, n + 1)
                        c.did(red(pred[:, :], ps_pred[:, 0:4 * C].rearrange("p (f c) -> p c f", c=C), AX.X, ALU.add))
                        c.wait(dve)
                        c.did(stt(out=dp[:, :], in0=pred[:, :], scalar=2.0 / C, in1=v, op0=ALU.mult, op1=ALU.subtract))
                        c.wait(dve)
                        c.did(ts(dps[:, :], dp[:, :], theta, None, ALU.mult))
                        c.did(tt(prod_a[:, da_lo, :], s1[:, da_lo, :], part(dp[:, :], 1, da_lo), ALU.mult))
                    if u is not None:
                        c.wait(dve)
                        c.did(red(da[:, da_lo], prod_a[:, da_lo, :], AX.X, ALU.add))
                        dve.wait_ge(parts, n * PARTS + DA_PART)
                        c.did(red(da[:, da_hi], prod_a[:, da_hi, :], AX.X, ALU.add))
                        c.wait(dve)
                        dve.wait_ge(ds_ready, n + 1)
                        c.did(stt(out=dhs[:, :], in0=da[:, :], scalar=theta, in1=ds[:, :], op0=ALU.mult, op1=ALU.mult))
                        c.wait(dve)
                        halves = slice(0, FI // 2), slice(FI // 2, FI)
                        c.did(tt(prod_a[:, halves[0], :], part(dhs[:, halves[0]], 2, halves[0]), part(kk, 1, halves[0]), ALU.mult))
                        c.wait(dve)
                        for half in halves:
                            if half is halves[1]:
                                dve.wait_ge(parts, n * PARTS + OUTER_PART)
                            c.did(stt(out=m0[:, half, :], in0=m0[:, half, :], scalar=eta, in1=prod_a[:, half, :], op0=ALU.mult, op1=ALU.add))
                        c.wait(dve)
                        c.did(stt(out=s0[:, :, :], in0=s0[:, :, :], scalar=keep, in1=m0[:, :, :], op0=ALU.mult, op1=ALU.add))
                        c.end()
                    else:
                        state_flags(i)
                        add_answer(n - 1, t - 1)

                def state_flags(i):
                    c = flag_step
                    c.start(i)
                    dve.wait_ge(s1_ready, i * CH + CH)
                    for j, s in enumerate(st):
                        c.did(nc.vector.tensor_scalar(prod_a[:, :, :], s[:, :, :], 0.0, None, ALU.not_equal, ALU.max, accum_out=nz[:, j:j + 1]))
                        c.wait(dve)

                def add_answer(n, t):
                    a = added
                    a.start(n)
                    dve.wait_ge(out_psum, n + 1)
                    a.did(red(o_row[:, :], ps_out[:, 0:4 * C].rearrange("p (f c) -> p c f", c=C), AX.X, ALU.add))
                    a.wait(dve)
                    r = res[:, bass.ds(t, 1), :].rearrange("p t c -> p (t c)")
                    a.did(tt(r, r, o_row[:, :], ALU.add))
                    a.end()

                def chunk(dve, i):
                    norms(pre, i)
                    dve.wait_ge(rows_first, i * 16 + 16)
                    settle(dve)
                    in_chunk(dve, i, lambda n, t, u: step(i, n, t, u))
                    c = flag_step
                    c.did(red(nz[:, 4:5], nz[:, 0:4], AX.X, ALU.max))
                    dve.wait_ge(flag_psum, i + 1)
                    dve.wait_ge(saved, i * 16 + 16)
                    c.did(nc.vector.tensor_copy(nz[:, 5:6], ps_flag[:, 0:1]))
                    c.end()
                    c.wait(dve)
                    nc.vector.tensor_copy(flag[:, :], nz[:, 5:6]).then_inc(flag_ready, 1)
                chunks(dve, chunk, lambda dve: dve.sem_inc(flag_ready, 1))

            @block.gpsimd
            def _(pool):
                def chunk(pool, i):
                    pool.wait_ge(pre.sem, i * pre.per + 6)
                    nc.gpsimd.tensor_tensor(small[:, 4, 0:J], small[:, 3, 0:J], neghalf[:, 0:J], ALU.pow).then_inc(rs_ready, 1)
                    pool.wait_ge(pre.sem, i * pre.per + (9 + J))
                    nc.gpsimd.tensor_tensor(small[:, 6, :], small[:, 5, :], neghalf[:, :], ALU.pow).then_inc(rs_ready, 1)
                    def step(n, t, u):
                        at = n * learn.per
                        if u is not None:
                            pool.wait_ge(learn.sem, at + ACT_AT)
                            settle(pool)
                            nc.gpsimd.tensor_scalar(om[:, :], sig[:, :], -1.0, 1.0, ALU.mult, ALU.add).then_inc(pool_ds, 1)
                            pool.wait_ge(pool_ds, n * 2 + 1)
                            nc.gpsimd.tensor_tensor(ds[:, :], om[:, :], act_[:, :], ALU.mult).then_inc(pool_ds, 1)
                            pool.wait_ge(pool_ds, n * 2 + 2)
                            nc.gpsimd.tensor_tensor(ds[:, :], ds[:, :], sig[:, :], ALU.add).then_inc(ds_ready, 1)
                        if has_last(t):
                            pool.wait_ge(s1_ready, n)
                            settle(pool)
                        if has_last(t):
                            pool.wait_ge(answer.sem, (n - 1) * answer.per + A2_AT)
                            nc.gpsimd.tensor_tensor(prod_g[:, :, :], s1[:, :, :], wide(a2[:, :], 2), ALU.mult).then_inc(g_ready, 1)
                        if u is not None:
                            pool.wait_ge(learn.sem, at + DP_AT)
                            nc.gpsimd.tensor_tensor(prod_a[:, da_hi, :], s1[:, da_hi, :], part(dp[:, :], 1, da_hi), ALU.mult).then_inc(parts, 1)
                            pool.wait_ge(learn.sem, at + DPS_AT)
                            nc.gpsimd.tensor_tensor(prod_e[:, hi, :], part(act_[:, hi], 2, hi), part(dps[:, :], 1, hi), ALU.mult).then_inc(parts, 1)
                            pool.wait_ge(learn.sem, at + DHS_AT)
                            kk = now[:, u, C:2 * C]
                            half = slice(FI // 2, FI)
                            nc.gpsimd.tensor_tensor(prod_a[:, half, :], part(dhs[:, half], 2, half), part(kk, 1, half), ALU.mult).then_inc(parts, 1)
                            pool.wait_ge(parts, n * PARTS + E_PART)
                            settle(pool)
                            pool.wait_ge(e_ready, n + 1)
                            settle(pool)
                            pool.wait_ge(em1_ready, n + 1)
                            nc.gpsimd.tensor_tensor(m1[:, :, :], em1[:, :, :], prod_e[:, :, :], ALU.add).then_inc(m1_ready, 1)
                            pool.wait_ge(learn.sem, at + S0_AT)
                            if not isinstance(t, int) or t + 1 < CH:
                                times_k(n + 1, 1 - u)
                            q = now[:, u, 0:C]
                            nc.gpsimd.tensor_tensor(prod_f[:, :, :], s0[:, :, :], wide(q, 1), ALU.mult).then_inc(f_ready, 1)

                    def times_k(n, u):
                        settle(pool)
                        pool.wait_ge(now_ready, n + 1)
                        nc.gpsimd.tensor_tensor(prod_a[:, hi, :], s0[:, hi, :], part(now[:, u, C:2 * C], 1, hi), ALU.mult).then_inc(parts, 1)
                    times_k(i * CH, 0)
                    in_chunk(pool, i, step)
                chunks(pool, chunk)


def experts(nc, V, x, out):
    with ExitStack() as ctx:
        def sb(name, shape, dt=F32):
            return ctx.enter_context(nc.sbuf_tensor("e_" + name, shape, dt))

        def sem(name):
            return ctx.enter_context(nc.semaphore("e_" + name))

        banks = [ctx.enter_context(nc.psum_tensor(f"e_bank{i}", [P, 512], F32)) for i in range(8)]
        ps_t, ps_small, ps_h0, ps_h1, ps_h2, ps_h3, ps_yt, ps_y = banks
        ps_h = [ps_h0, ps_h1, ps_h2, ps_h3]
        ps_logit, ps_cum, ps_tot = (ps_small[:, j * TILES * E:(j + 1) * TILES * E].rearrange("p (t e) -> p t e", e=E)
                                    for j in range(3))

        w1 = sb("w1", [P, E, F])
        w2 = sb("w2", [P, E, 2, C])
        b2 = sb("b2", [P, C])
        w_gate = sb("w_gate", [C, E])
        b_gate = sb("b_gate", [1, E])
        ones1 = sb("ones1", [1, P])
        ident = sb("ident", [P, P])
        upto = sb("upto", [P, P])
        ones = sb("ones", [P, P])
        fold = sb("fold", [P, C])
        rank = sb("rank", [P, TILES, E])
        neghalf = sb("neghalf", [P, TILES])
        xg = sb("xg", [P, 2, TILES, C])
        xr = sb("xr", [P, 2, TILES, C])
        xc, sq, xn = sb("xc", [P, TILES, C]), sb("sq", [P, TILES, C]), sb("xn", [P, TILES, C])
        s, m, ss, var, rstd = [sb(n, [P, TILES]) for n in ("s", "m", "ss", "var", "rstd")]
        xt = sb("xt", [P, 2, SIZE])
        top, low, first, total, share, pos, kept = [sb(n, [P, TILES]) for n in
                                                    ("top", "low", "first", "total", "share", "pos", "kept")]
        z, ez, eq, choice, place = [sb(n, [P, TILES, E]) for n in ("z", "ez", "eq", "choice", "place")]
        before = sb("before", [P, TILES + 1, E])
        weight = sb("weight", [P, 2, TILES])
        hid = sb("hid", [P, 4, 512])
        yt = sb("yt", [P, 512])
        y, over, under = [sb(n, [P, TILES, C]) for n in ("y", "over", "under")]
        finite = sb("finite", [P, TILES, C], I32)
        res = sb("res", [P, 2, TILES, C])

        loaded, prep, zeroed = sem("loaded"), sem("prep"), sem("zeroed")
        x_in, stored = [sem("x_in0"), sem("x_in1")], [sem("stored0"), sem("stored1")]
        ln = Steps(sem("ln"), 7)
        pick = Steps(sem("pick"), 17)
        end = Steps(sem("end"), 7)
        rstd_ready, xt_psum, xt_ready, logit_psum, ez_ready = [sem(n) for n in (
            "rstd_ready", "xt_psum", "xt_ready", "logit_psum", "ez_ready")]
        choice_psum, count_psum, choice_ready = sem("choice_psum"), sem("count_psum"), sem("choice_ready")
        xr_ready = sem("xr_ready")
        yt_ready = sem("yt_ready")
        h_psum, y_psum = sem("h_psum"), sem("y_psum")
        hid_act, hid_dve, hid_used = sem("hid_act"), sem("hid_dve"), sem("hid_used")
        UNITS = E * 2

        with nc.Block() as block:
            @block.sync
            def _(sp):
                def load(o, i):
                    sp.dma_start(o, i).then_inc(loaded, 16)
                sp.wait_ge(zeroed, 3)
                load(w1[0:C, :, :], V["moe_w1"].rearrange("e d f -> d e f"))
                load(w2[:, :, :, :], V["moe_w2"].rearrange("e (h p) d -> p e h d", p=P))
                load(w_gate[:, :], V["gate_w"])
                load(b_gate[:, :], V["gate_b"].rearrange("(a e) -> a e", a=1))
                load(w1[K1 - 1:K1, :, :], V["moe_b1"].unsqueeze(0))
                load(b2[C:C + E, :], V["moe_b2"])
                sp.wait_ge(loaded, 16 * 6)

            @block.gpsimd
            def _(pool):
                nc.gpsimd.memset(ident[:, :], 0.0).then_inc(prep, 1)
                nc.gpsimd.memset(upto[:, :], 1.0).then_inc(prep, 1)
                nc.gpsimd.memset(ones[:, :], 1.0).then_inc(prep, 1)
                nc.gpsimd.memset(neghalf[:, :], -0.5).then_inc(prep, 1)
                nc.gpsimd.memset(before[:, :, :], 0.0).then_inc(prep, 1)
                nc.gpsimd.memset(ones1[:, :], 1.0).then_inc(prep, 1)
                nc.gpsimd.memset(fold[:, :], 0.0).then_inc(prep, 1)
                pool.wait_ge(prep, 7)
                nc.gpsimd.affine_select(out=fold[:, :], in_=fold[:, :], compare_op=ALU.not_equal, fill=1.0,
                                        base=0, pattern=[[-1, C]], channel_multiplier=1).then_inc(prep, 1)
                pool.wait_ge(prep, 8)
                nc.gpsimd.affine_select(out=fold[:, :], in_=fold[:, :], compare_op=ALU.not_equal, fill=1.0,
                                        base=-C, pattern=[[-1, C]], channel_multiplier=1).then_inc(prep, 1)
                nc.gpsimd.affine_select(out=ident[:, :], in_=ident[:, :], compare_op=ALU.not_equal, fill=1.0,
                                        base=0, pattern=[[-1, P]], channel_multiplier=1).then_inc(prep, 1)
                nc.gpsimd.affine_select(out=upto[:, :], in_=upto[:, :], compare_op=ALU.is_ge, fill=0.0,
                                        base=0, pattern=[[1, P]], channel_multiplier=-1).then_inc(prep, 1)
                pool.wait_ge(prep, 11)
                pool.wait_ge(zeroed, 3)
                own = w1[C:C + E, :, :]
                nc.gpsimd.affine_select(out=own, in_=own, compare_op=ALU.not_equal, fill=0.0,
                                        base=0, pattern=[[-1, E], [0, F]], channel_multiplier=1).then_inc(prep, 1)

            @block.vector
            def _(dve):
                nc.vector.memset(w1[C:P, :, :], 0.0).then_inc(zeroed, 1)
                dve.wait_ge(zeroed, 1)
                nc.vector.memset(w1[C:C + E, :, :], OFF).then_inc(zeroed, 1)
                nc.vector.memset(b2[:, :], 0.0).then_inc(zeroed, 1)
                nc.vector.memset(xt[C:P, :, :], 1.0)
                for e in range(E):
                    nc.vector.memset(rank[:, :, e:e + 1], float(E - e))

        def tiles(ap, g):
            return ap[bass.ds(g, 1)].rearrange("g t p c -> p (g t) c")

        x_t = x.rearrange("b t c -> (b t) c").rearrange("(g t p) c -> g t p c", t=TILES, p=P)
        out_t = out.rearrange("b t c -> (b t) c").rearrange("(g t p) c -> g t p c", t=TILES, p=P)

        def on_tiles(ap, n):
            return ap.unsqueeze(2).broadcast_to([P, TILES, n])

        def sync_load(sp, group):
            u = group.odd
            after(sp, ln.sem, (group.g - 2) * ln.per + ln.per)
            settle(sp)
            after(sp, xr_ready, group.g - 1)
            settle(sp)
            sp.dma_start(xg[:, u, :, :], tiles(x_t, group.g)).then_inc(x_in[u], 16)

        def sync_store(sp, group):
            u = group.odd
            sp.wait_ge(end.sem, group.g * end.per + end.per)
            settle(sp)
            sp.dma_start(tiles(out_t, group.g), res[:, u, :, :]).then_inc(stored[u], 16)

        def pe_xt(pe, group):
            pe.wait_ge(ln.sem, group.g * ln.per + ln.per)
            settle(pe)
            for t in range(TILES):
                i = nc.tensor.transpose(ps_t[0:C, t * P:(t + 1) * P], xn[:, t, :], ident[:, :])
            i.then_inc(xt_psum, 1)

        def pe_logits(pe, group):
            pe.wait_ge(xt_ready, group.g + 1)
            after(pe, pick.sem, (group.g - 1) * pick.per + pick.per)
            settle(pe)
            for t in range(TILES):
                nc.tensor.matmul(ps_logit[:, t, :], xt[0:C, group.odd, t * P:(t + 1) * P], w_gate[:, :], start=True, stop=False)
                i = nc.tensor.matmul(ps_logit[:, t, :], ones1[:, :], b_gate[:, :], start=False, stop=True)
            i.then_inc(logit_psum, 1)

        def pe_choice(pe, group):
            g = group.g
            pe.wait_ge(pick.sem, g * pick.per + 6)
            after(pe, choice_ready, g)
            settle(pe)
            for t in range(TILES):
                i = nc.tensor.transpose(ps_t[0:E, t * P:(t + 1) * P], choice[:, t, :], ident[:, :])
            i.then_inc(choice_psum, 1)
            flat = choice[:, :, :].rearrange("p t e -> p (t e)")
            nc.tensor.matmul(ps_cum.rearrange("p t e -> p (t e)"), upto[:, :], flat, start=True, stop=True)
            nc.tensor.matmul(ps_tot.rearrange("p t e -> p (t e)"), ones[:, :], flat, start=True, stop=True).then_inc(count_psum, 1)

        def pe_hidden(pe, group, n):
            g, u = group.g, group.odd
            e, half = n // 2, n % 2
            if n == 0:
                pe.wait_ge(choice_ready, g + 1)
                pe.wait_ge(xt_ready, g + 1)
            relu_of(pe, group, n - 4)
            nc.tensor.matmul(ps_h[n % 4][:, :], w1[:, e, half * P:(half + 1) * P], xt[:, u, :], start=True, stop=True).then_inc(h_psum, 1)

        def relu_of(eng, group, n):
            g = group.g
            if n < 0:
                if isinstance(g, int) and g == 0:
                    return
                n, g = n + UNITS, g - 1
            eng.wait_ge((hid_act, hid_dve)[n % 2], g * (UNITS // 2) + (n // 2 + 1))

        def pe_out(pe, group, n):
            g = group.g
            e, half = n // 2, n % 2
            if n == 0:
                after(pe, yt_ready, g)
            relu_of(pe, group, n)
            nc.tensor.matmul(ps_yt[C * half:C * half + C, :], w2[:, e, half, :], hid[:, n % 4, :],
                             start=(n < 2), stop=(n >= UNITS - 2)).then_inc(hid_used, 1)

        def pe_sum(pe, group):
            g, u = group.g, group.odd
            pe.wait_ge(yt_ready, g + 1)
            after(pe, end.sem, (g - 1) * end.per + 1)
            settle(pe)
            for t in range(TILES):
                tile = slice(t * P, (t + 1) * P)
                y_of = ps_y[:, t * C:(t + 1) * C]
                nc.tensor.matmul(y_of, yt[:, tile], fold[:, :], start=True, stop=False)
                i = nc.tensor.matmul(y_of, xt[:, u, tile], b2[:, :], start=False, stop=True)
            i.then_inc(y_psum, 1)

        def act_yt(act, group):
            g = group.g
            act.wait_ge(hid_used, g * UNITS + UNITS)
            after(act, y_psum, g)
            nc.scalar.copy(yt[:, :], ps_yt[:, :]).then_inc(yt_ready, 1)

        def relu(eng, group, n):
            g = group.g
            eng.wait_ge(h_psum, g * UNITS + (n + 1))
            after(eng, hid_used, g * UNITS + (n - 3))
            if n % 2 == 0:
                nc.scalar.activation(hid[:, n % 4, :], ps_h[n % 4][:, :], ACT.Relu).then_inc(hid_act, 1)
            else:
                nc.vector.tensor_scalar(hid[:, n % 4, :], ps_h[n % 4][:, :], 0.0, None, ALU.max).then_inc(hid_dve, 1)

        def act_xt(act, group):
            act.wait_ge(xt_psum, group.g + 1)
            after(act, y_psum, group.g - 1)
            nc.scalar.copy(xt[0:C, group.odd, :], ps_t[0:C, :]).then_inc(xt_ready, 1)

        def act_exp(act, group):
            act.wait_ge(pick.sem, group.g * pick.per + 2)
            nc.scalar.activation(ez[:, :, :], z[:, :, :], ACT.Exp).then_inc(ez_ready, 1)

        def act_choice(act, group):
            act.wait_ge(choice_psum, group.g + 1)
            nc.scalar.copy(xt[C:C + E, group.odd, :], ps_t[0:E, :]).then_inc(choice_ready, 1)

        tt, ts, red = nc.vector.tensor_tensor, nc.vector.tensor_scalar, nc.vector.tensor_reduce

        def dve_norm(dve, group):
            u, g, c = group.odd, group.g, ln
            c.start(g)
            dve.wait_ge(x_in[u], group.half * 16 + 16)
            c.did(red(s[:, :], xg[:, u, :, :], AX.X, ALU.add))
            c.wait(dve)
            c.did(ts(m[:, :], s[:, :], 1.0 / C, None, ALU.mult))
            c.wait(dve)
            c.did(tt(xc[:, :, :], xg[:, u, :, :], on_tiles(m[:, :], C), ALU.subtract))
            c.wait(dve)
            c.did(tt(sq[:, :, :], xc[:, :, :], xc[:, :, :], ALU.mult))
            c.wait(dve)
            c.did(red(ss[:, :], sq[:, :, :], AX.X, ALU.add))
            c.wait(dve)
            c.did(ts(var[:, :], ss[:, :], 1.0 / C, EPS, ALU.mult, ALU.add))
            dve.wait_ge(rstd_ready, g + 1)
            after(dve, xt_psum, g)
            c.did(tt(xn[:, :, :], xc[:, :, :], on_tiles(rstd[:, :], C), ALU.mult))
            c.end()

        def dve_choose(dve, group):
            g, c = group.g, pick
            c.start(g)
            dve.wait_ge(logit_psum, g + 1)
            c.did(red(top[:, :], ps_logit, AX.X, ALU.max))
            c.wait(dve)
            c.did(tt(z[:, :, :], ps_logit, on_tiles(top[:, :], E), ALU.subtract))
            c.wait(dve)
            c.did(ts(eq[:, :, :], z[:, :, :], 0.0, None, ALU.is_equal))
            c.wait(dve)
            c.did(tt(eq[:, :, :], eq[:, :, :], rank[:, :, :], ALU.mult))
            c.wait(dve)
            c.did(red(first[:, :], eq[:, :, :], AX.X, ALU.max))
            c.wait(dve)
            after(dve, count_psum, g)
            c.did(tt(choice[:, :, :], eq[:, :, :], on_tiles(first[:, :], E), ALU.is_equal))
            dve.wait_ge(ez_ready, g + 1)
            c.did(red(total[:, :], ez[:, :, :], AX.X, ALU.add))
            c.wait(dve)
            c.did(nc.vector.reciprocal(share[:, :], total[:, :]))

        def dve_count(dve, group):
            g, c = group.g, pick
            c.start(g)
            c.n = 8
            dve.wait_ge(count_psum, g + 1)
            for t in range(TILES):
                c.did(tt(before[:, t + 1, :], before[:, t, :], ps_tot[:, t, :], ALU.add))
                c.wait(dve)
            c.did(tt(place[:, :, :], before[:, 0:TILES, :], ps_cum, ALU.add))
            c.wait(dve)
            c.did(tt(place[:, :, :], place[:, :, :], choice[:, :, :], ALU.mult))
            c.wait(dve)
            c.did(red(pos[:, :], place[:, :, :], AX.X, ALU.add))
            c.wait(dve)
            c.did(nc.vector.scalar_tensor_tensor(out=weight[:, group.odd, :], in0=pos[:, :], scalar=float(CAPACITY),
                                                 in1=share[:, :], op0=ALU.is_le, op1=ALU.mult))
            c.did(nc.vector.tensor_copy(before[:, 0, :], before[:, TILES, :]))
            c.end()

        def dve_end(dve, group):
            g, u, c = group.g, group.odd, end
            c.start(g)
            dve.wait_ge(y_psum, g + 1)
            dve.wait_ge(pick.sem, g * pick.per + pick.per)
            c.did(tt(y[:, :, :], ps_y[:, 0:TILES * C].rearrange("p (t c) -> p t c", t=TILES),
                     on_tiles(weight[:, u, :], C), ALU.mult))
            c.wait(dve)
            c.did(ts(over[:, :, :], y[:, :, :], HUGE, CLIP, ALU.is_gt, ALU.mult))
            c.did(ts(under[:, :, :], y[:, :, :], -HUGE, -CLIP, ALU.is_lt, ALU.mult))
            c.did(ts(finite[:, :, :], y[:, :, :], 0.0, 0.0, ALU.mult, ALU.is_equal))
            c.wait(dve)
            c.did(tt(over[:, :, :], over[:, :, :], under[:, :, :], ALU.add))
            c.wait(dve)
            settle(dve)
            c.did(nc.vector.copy_predicated(over[:, :, :], finite[:, :, :], y[:, :, :]))
            c.wait(dve)
            after(dve, stored[u], group.half * 16)
            dve.wait_ge(xr_ready, g + 1)
            c.did(tt(res[:, u, :, :], over[:, :, :], xr[:, u, :, :], ALU.add))
            c.end()

        def pool_rstd(pool, group):
            u = group.odd
            pool.wait_ge(ln.sem, group.g * ln.per + 6)
            nc.gpsimd.tensor_tensor(rstd[:, :], var[:, :], neghalf[:, :], ALU.pow).then_inc(rstd_ready, 1)
            pool.wait_ge(x_in[u], group.half * 16 + 16)
            after(pool, end.sem, (group.g - 2) * end.per + end.per)
            settle(pool)
            nc.gpsimd.tensor_copy(xr[:, u, :, :], xg[:, u, :, :]).then_inc(xr_ready, 1)

        def steps(eng, step, a_only, c_only):
            f = Group(0, 0)
            a_only(eng, f)
            step(eng, f, True, False)
            for g in (1, 2):
                step(eng, Group(g // 2, g % 2), True, True)
            with eng.Fori(1, SETS // 2 - 1) as i:
                step(eng, Group(i, 1), True, True)
                step(eng, Group(i + 1, 0), True, True)
            last = Group(SETS // 2 - 1, 1)
            step(eng, last, False, True)
            c_only(eng, last)

        with nc.Block() as block:
            @block.sync
            def _(sp):
                def step(sp, group, a, c):
                    if a:
                        sync_load(sp, group.next())
                    if c:
                        sync_store(sp, group.prev())
                steps(sp, step, sync_load, sync_store)
                for u in range(2):
                    sp.wait_ge(stored[u], SETS // 2 * 16)

            @block.tensor
            def _(pe):
                def a_only(pe, group):
                    pe_xt(pe, group)
                    pe_logits(pe, group)
                    pe_choice(pe, group)

                def step(pe, group, a, c):
                    pe_hidden(pe, group, 0)
                    pe_hidden(pe, group, 1)
                    for n in range(0, UNITS, 2):
                        if n + 2 < UNITS:
                            pe_hidden(pe, group, n + 2)
                            pe_hidden(pe, group, n + 3)
                        if c and n == 0:
                            pe_sum(pe, group.prev())
                        pe_out(pe, group, n)
                        pe_out(pe, group, n + 1)
                        if a and n == 2:
                            pe_xt(pe, group.next())
                        if a and n == 6:
                            pe_logits(pe, group.next())
                        if a and n == 10:
                            pe_choice(pe, group.next())
                steps(pe, step, a_only, pe_sum)

            @block.scalar
            def _(act):
                def a_only(act, group):
                    act_xt(act, group)
                    act_exp(act, group)
                    act_choice(act, group)

                def step(act, group, a, c):
                    if c:
                        act_yt(act, group.prev())
                    for n in range(0, UNITS, 2):
                        relu(act, group, n)
                        if a and n == 4:
                            act_xt(act, group.next())
                        if a and n == 8:
                            act_exp(act, group.next())
                        if a and n == 12:
                            act_choice(act, group.next())
                steps(act, step, a_only, act_yt)

            @block.vector
            def _(dve):
                def a_only(dve, group):
                    dve_norm(dve, group)
                    dve_choose(dve, group)
                    dve_count(dve, group)

                def step(dve, group, a, c):
                    for n in range(1, UNITS, 2):
                        relu(dve, group, n)
                        if a and n == 1:
                            dve_norm(dve, group.next())
                        if c and n == 5:
                            dve_end(dve, group.prev())
                        if a and n == 7:
                            dve_choose(dve, group.next())
                        if a and n == 13:
                            dve_count(dve, group.next())
                steps(dve, step, a_only, dve_end)

            @block.gpsimd
            def _(pool):
                steps(pool, lambda pool, group, a, c: pool_rstd(pool, group.next()) if a else None,
                      pool_rstd, lambda pool, group: None)


def shift_moves(src, dst):
    old = src.rearrange("(b h) w (r c) d -> b h w r (c d)", b=B, r=WS)
    upper = dst[0:UNCUT].rearrange("(b h) w (r c) d -> b h w r (c d)", b=B, r=WS)
    lower = dst[UNCUT:GROUPS].rearrange("b w (r c) d -> b w r (c d)", r=WS)
    left, right = slice(0, KEEP * C), slice(KEEP * C, WS * C)
    old_left, old_right = slice(SHIFT * C, WS * C), slice(0, SHIFT * C)
    last = NW - 1

    def image(b):
        o, up, lo = (a[bass.ds(b, 1)].rearrange(f"z {s} -> (z {t}) {u}") for a, s, t, u in (
            (old, "h w r x", "h", "w r x"), (upper, "h w r x", "h", "w r x"), (lower, "w r x", "w", "r x")))
        moves = []
        for rows, old_rows, down in ((slice(0, KEEP), slice(SHIFT, WS), 0), (slice(KEEP, WS), slice(0, SHIFT), 1)):
            h, h_last = slice(down, last + down), last if not down else 0
            moves += [(up[:, :, rows, left].rearrange("h w r x -> (h w) r x"),
                       o[h, :, old_rows, old_left].rearrange("h w r x -> (h w) r x")),
                      (up[:, last, rows, right], o[h, 0, old_rows, old_right]),
                      (lo[:, rows, left], o[h_last, :, old_rows, old_left]),
                      (lo[0:last, rows, right], o[h_last, 1:NW, old_rows, old_right]),
                      (lo[last, rows, right], o[h_last, 0, old_rows, old_right])]
            moves += [(up[:, 0:last, rows.start + r, right], o[h, 1:NW, old_rows.start + r, old_right])
                      for r in range(rows.stop - rows.start)]
        return moves

    return image


def unshift_moves(src, dst):
    img = dst.rearrange("b (i j) c -> b i (j c)", i=SIDE)
    upper = src[0:UNCUT].rearrange("(b h) w (r c) d -> b h w r (c d)", b=B, r=WS)
    lower = src[UNCUT:GROUPS].rearrange("b w (r c) d -> b w r (c d)", r=WS)
    left, right = slice(0, KEEP * C), slice(KEEP * C, WS * C)
    last = NW - 1
    inner = slice(SHIFT, SIDE - KEEP)
    edge = slice((SIDE - KEEP) * C, SIDE * C)
    wrapped = slice(0, SHIFT * C)

    def image(b):
        im, up = (a[bass.ds(b, 1)].rearrange(f"z {s} -> (z {t}) {u}") for a, s, t, u in (
            (img, "i x", "i", "x"), (upper, "h w r x", "h", "w r x")))
        mid = im[inner].rearrange("(h r) x -> h r x", r=WS)
        moves = [(mid[:, :, edge], up[:, last, :, left]), (mid[:, :, wrapped], up[:, last, :, right])]
        moves += [(mid[:, r, SHIFT * C:(SIDE - KEEP) * C].rearrange("h (w x) -> h w x", w=last), up[:, 0:last, r, :])
                  for r in range(WS)]
        return moves

    def last_rows(b):
        im, lo = (a[bass.ds(b, 1)].rearrange(f"z {s} -> (z {t}) {u}") for a, s, t, u in (
            (img, "i x", "i", "x"), (lower, "w r x", "w", "r x")))
        moves = []
        for rows, at in ((slice(0, KEEP), slice(SIDE - KEEP, SIDE)), (slice(KEEP, WS), slice(0, SHIFT))):
            moves += [(im[at, SHIFT * C:(SIDE - KEEP) * C].rearrange("r (w x) -> r w x", w=last),
                       lo[0:last, rows, :].rearrange("w r x -> r w x")),
                      (im[at, edge], lo[last, rows, left]), (im[at, wrapped], lo[last, rows, right])]
        return moves

    return image, last_rows


def move_images(nc, name, image):
    with nc.semaphore(name + "_0") as s0, nc.semaphore(name + "_1") as s1, nc.Block() as block:
        def half(eng, sem, first):
            with eng.Fori(first, first + B // 2) as b:
                moves = image(b)
                for out, in_ in moves:
                    eng.dma_start(out, in_).then_inc(sem, 16)
            eng.wait_ge(sem, B // 2 * len(moves) * 16)

        @block.sync
        def _(sp):
            half(sp, s0, 0)

        @block.scalar
        def _(act):
            half(act, s1, B // 2)


def vit_tower(nc, V, out):
    def dram(name, shape):
        return nc.dram_tensor(name, shape, F32, kind="Internal").ap()

    windows = [GROUPS, NW, N, C]
    first, shifted, second = dram("first", windows), dram("shifted_in", windows), dram("second", windows)
    x = dram("x_tokens", [B, T, C])
    swin_block(nc, 0, V, V["patches"], first, shift_moves(first, shifted))
    upper_rows, last_rows = unshift_moves(second, x)
    swin_block(nc, 1, V, shifted, second, upper_rows)
    move_images(nc, "unshift", last_rows)
    fast_weights(nc, V, x, dram("rows_kept", [B, CH, QKV3]))
    experts(nc, V, x, out)


def kernel(**inputs):
    import numpy as np
    import concourse.bacc as bacc
    from concourse.bass_utils import run_bass_kernel_spmd

    a = {n: np.asarray(v) for n, v in inputs.items()}
    tok = {n[7:]: v for n, v in a.items() if n.startswith("L0_tok_")}
    att = {n[8:]: v for n, v in a.items() if n.startswith("L0_attn_")}
    ffn = {n[7:]: v for n, v in a.items() if n.startswith("L0_ffn_")}
    px = a["x"].reshape(B, NW, WS, 4, NW, WS, 4).transpose(3, 6, 0, 1, 4, 2, 5).reshape(PIX, GROUPS, NW, N)
    part = np.zeros((SIDE, SIDE), np.int32)
    cuts = (slice(0, -WS), slice(-WS, -SHIFT), slice(-SHIFT, None))
    for i, rows in enumerate(cuts):
        for j, cols in enumerate(cuts):
            part[rows, cols] = 3 * i + j
    part = part.reshape(NW, WS, NW, WS).transpose(0, 2, 1, 3).reshape(NW, NW, N)
    masks = np.stack([np.where(part[w][:, None] != part[w][None, :], np.float32(-100), np.float32(0))[::-1]
                      for w in ((0, NW - 1), (NW - 1, 0), (NW - 1, NW - 1))])
    arrays = {
        "patches": px, "masks": masks, "pe_t": tok["pe_w"].reshape(C, PIX).T,
        "qkv_t": tok["qkv_w"].transpose(0, 2, 1), "proj_t": tok["proj_w"].transpose(0, 2, 1),
        "w1_t": tok["w1"].transpose(0, 2, 1), "w2_t": tok["w2"].transpose(0, 2, 1),
        "rpb_t": tok["rpb"].transpose(0, 2, 1)[:, :, ::-1],
        "w_fused_t": att["W_fused"].T, "W0_t": att["W0"].T, "P0_t": att["P0"].T, "W1": att["W1"], "P1": att["P1"],
        "gate_w": ffn["gate_w"], "gate_b": ffn["gate_b"], "moe_w1": ffn["w1"], "moe_b1": ffn["b1"],
        "moe_w2": ffn["w2"], "moe_b2": ffn["b2"],
    }
    for n in ("pe_b", "pe_ng", "pe_nb", "n1g", "n1b", "qkv_b", "proj_b", "n2g", "n2b", "b1", "b2"):
        arrays[n] = tok[n]
    arrays = {n: np.ascontiguousarray(v) for n, v in arrays.items()}
    nc = bacc.Bacc("TRN2", target_bir_lowering=False, num_devices=1)
    V = {n: nc.dram_tensor("in_" + n, v.shape, mybir.dt.from_np(v.dtype), kind="ExternalInput").ap()
         for n, v in arrays.items()}
    out = nc.dram_tensor("out", (B, T, C), F32, kind="ExternalOutput").ap()
    vit_tower(nc, V, out)
    r = run_bass_kernel_spmd(nc, [{"in_" + n: v for n, v in arrays.items()}], core_ids=[0])
    return r.results[0]["out"]
```
